# Optimizing a Trainium2 kernel written in Bass

```python
import numpy as np
import jax
import jax.numpy as jnp

def _softmax(x, axis=-1):
    return jax.nn.softmax(x, axis=axis)

def _gelu(x):
    return jax.nn.gelu(x, approximate=True)

def _silu(x):
    return jax.nn.silu(x)

def _sigmoid(x):
    return jax.nn.sigmoid(x)

def _layernorm(x, axis=-1, eps=1e-05):
    m = jnp.mean(x, axis=axis, keepdims=True)
    v = jnp.var(x, axis=axis, keepdims=True)
    return (x - m) / jnp.sqrt(v + eps)

def _scatter_add(tgt, idx, src, axis=0):
    return tgt.at[idx].add(src)

def _segment_sum(src, seg, n):
    return jax.ops.segment_sum(src, seg, n)
kernel_name = 'mk_xattn_ffn_d1_seqx_r4_c909bc'

def setup_inputs(seed: int=0):
    np.random.seed(seed)
    _w = jnp.asarray

    def _rec_inputs():
        import jax
        import jax.numpy as jnp
        _rk = jax.random.key(seed)
        x = 7.22e-05 + 1 * jax.random.normal(jax.random.fold_in(_rk, 1), (8, 256, 512), jnp.float32)
        _lenS = 256 - jax.random.randint(jax.random.fold_in(_rk, 7), (8,), 0, max(1, 256 // 4) + 1, jnp.int32)
        _lenS2 = 256 - jax.random.randint(jax.random.fold_in(_rk, 8), (8,), 0, max(1, 256 // 4) + 1, jnp.int32)
        _ctx_2048P = jax.random.normal(jax.random.fold_in(_rk, 11), (8, 16, 512), jnp.float32)
        _ctx_2048c = jax.random.dirichlet(jax.random.fold_in(_rk, 511), 0.3 * jnp.ones((16,), jnp.float32), (8, 256))
        _ctx_2048t = jnp.einsum('bsk,bkd->bsd', _ctx_2048c, _ctx_2048P)
        _ctx_2048t = _ctx_2048t * jax.lax.rsqrt(jnp.mean(jnp.square(_ctx_2048t)) + 1e-12) * 0.953939
        ctx_2048 = 4.13588e-05 + 0.999923 * (_ctx_2048t + 0.3 * jax.random.normal(jax.random.fold_in(_rk, 611), (8, 256, 512), jnp.float32))
        return (x, ctx_2048)
    x, ctx_2048 = _rec_inputs()

    def _L0_xattn_setup():
        import jax, jax.numpy as jnp
        import numpy as np
        N_HEADS = 16
        K_CH = 256 // N_HEADS
        SCALE = 1.0 / np.sqrt(K_CH)
        key = jax.random.key(seed)
        ks = jax.random.split(key, 10)
        B, C, T = (4, 256, 512)
        Cout = 256
        xavier = lambda k, o, i: jax.random.uniform(k, (o, i), jnp.float32, -1.0, 1.0) * np.sqrt(6.0 / (o + i))
        return {'x': jax.random.normal(ks[0], (B, C, T), jnp.float32), 'c': jax.random.normal(ks[1], (B, C, T), jnp.float32), 'Wq': xavier(ks[2], C, C), 'bq': jnp.zeros((C,), jnp.float32), 'Wk': xavier(ks[3], C, C), 'bk': jnp.zeros((C,), jnp.float32), 'Wv': xavier(ks[4], C, C), 'bv': jnp.zeros((C,), jnp.float32), 'Wo': xavier(ks[5], Cout, C), 'bo': jnp.zeros((Cout,), jnp.float32)}
    _L0_xattn_all = _L0_xattn_setup()
    _L0_xattn_in = {k: v for k, v in _L0_xattn_all.items() if k in ('Wq', 'bq', 'Wk', 'bk', 'Wv', 'bv', 'Wo', 'bo')}
    del _L0_xattn_all

    def _L0_ffn_setup():
        import jax, jax.numpy as jnp
        import numpy as np
        B, S, D = (4, 512, 512)
        E, F, K = (8, 256, 2)
        SF = 256
        EPS = 1e-06

        def _rmsnorm(x, w, eps=EPS):
            var = jnp.mean(x * x, axis=-1, keepdims=True)
            return x * jax.lax.rsqrt(var + eps) * w
        key = jax.random.key(seed)
        ks = jax.random.split(key, 9)
        g = lambda k, shape, scale: jax.random.normal(k, shape, jnp.float32) * scale
        return {'x': g(ks[0], (B, S, D), 1.0), 'rms_weight': jnp.ones((D,), jnp.float32), 'router_w': g(ks[1], (D, E), 0.02), 'w_gate': g(ks[2], (E, D, F), 0.02), 'w_up': g(ks[3], (E, D, F), 0.02), 'w_down': g(ks[4], (E, F, D), 0.02), 'sw_gate': g(ks[5], (D, SF), 0.02), 'sw_up': g(ks[6], (D, SF), 0.02), 'sw_down': g(ks[7], (SF, D), 0.02)}
    _L0_ffn_all = _L0_ffn_setup()
    _L0_ffn_in = {k: v for k, v in _L0_ffn_all.items() if k in ('rms_weight', 'router_w', 'w_gate', 'w_up', 'w_down', 'sw_gate', 'sw_up', 'sw_down')}
    del _L0_ffn_all
    return {'x': x, 'ctx_2048': ctx_2048, 'L0_xattn_Wq': _L0_xattn_in['Wq'], 'L0_xattn_bq': _L0_xattn_in['bq'], 'L0_xattn_Wk': _L0_xattn_in['Wk'], 'L0_xattn_bk': _L0_xattn_in['bk'], 'L0_xattn_Wv': _L0_xattn_in['Wv'], 'L0_xattn_bv': _L0_xattn_in['bv'], 'L0_xattn_Wo': _L0_xattn_in['Wo'], 'L0_xattn_bo': _L0_xattn_in['bo'], 'L0_ffn_rms_weight': _L0_ffn_in['rms_weight'], 'L0_ffn_router_w': _L0_ffn_in['router_w'], 'L0_ffn_w_gate': _L0_ffn_in['w_gate'], 'L0_ffn_w_up': _L0_ffn_in['w_up'], 'L0_ffn_w_down': _L0_ffn_in['w_down'], 'L0_ffn_sw_gate': _L0_ffn_in['sw_gate'], 'L0_ffn_sw_up': _L0_ffn_in['sw_up'], 'L0_ffn_sw_down': _L0_ffn_in['sw_down']}

def reference(x, ctx_2048, L0_xattn_Wq, L0_xattn_bq, L0_xattn_Wk, L0_xattn_bk, L0_xattn_Wv, L0_xattn_bv, L0_xattn_Wo, L0_xattn_bo, L0_ffn_rms_weight, L0_ffn_router_w, L0_ffn_w_gate, L0_ffn_w_up, L0_ffn_w_down, L0_ffn_sw_gate, L0_ffn_sw_up, L0_ffn_sw_down):
    import jax
    import jax.numpy as jnp

    def _L0_xattn_ref(x, c, Wq, bq, Wk, bk, Wv, bv, Wo, bo):
        import jax, jax.numpy as jnp
        import numpy as np
        N_HEADS = 16
        K_CH = 256 // N_HEADS
        SCALE = 1.0 / np.sqrt(K_CH)
        B, C, T = x.shape
        H, K = (N_HEADS, K_CH)
        q = jnp.einsum('oc,bct->bot', Wq, x) + bq[None, :, None]
        k = jnp.einsum('oc,bct->bot', Wk, c) + bk[None, :, None]
        v = jnp.einsum('oc,bct->bot', Wv, c) + bv[None, :, None]
        q = q.reshape(B, H, K, T)
        k = k.reshape(B, H, K, -1)
        v = v.reshape(B, H, K, -1)
        scores = jnp.einsum('bhkt,bhks->bhts', q, k) * SCALE
        p = jax.nn.softmax(scores, axis=-1)
        out = jnp.einsum('bhts,bhks->bhkt', p, v)
        out = out.reshape(B, H * K, T)
        return jnp.einsum('oc,bct->bot', Wo, out) + bo[None, :, None]

    def _L0_ffn_ref(x, rms_weight, router_w, w_gate, w_up, w_down, sw_gate, sw_up, sw_down):
        import jax, jax.numpy as jnp
        import numpy as np
        B, S, D = (4, 512, 512)
        E, F, K = (8, 256, 2)
        SF = 256
        EPS = 1e-06

        def _rmsnorm(x, w, eps=EPS):
            var = jnp.mean(x * x, axis=-1, keepdims=True)
            return x * jax.lax.rsqrt(var + eps) * w
        b, s, d = x.shape
        e = router_w.shape[1]
        h = _rmsnorm(x, rms_weight)
        ht = h.reshape(-1, d)
        t = ht.shape[0]
        logits = ht @ router_w
        probs = jax.nn.softmax(logits, axis=-1)
        topv, topi = jax.lax.top_k(probs, K)
        topv = topv / jnp.sum(topv, axis=-1, keepdims=True)
        w_dense = jnp.zeros((t, e), ht.dtype).at[jnp.arange(t)[:, None], topi].set(topv)
        g = jnp.einsum('td,edf->tef', ht, w_gate)
        u = jnp.einsum('td,edf->tef', ht, w_up)
        eo = jnp.einsum('tef,efd->ted', jax.nn.silu(g) * u, w_down)
        moe = jnp.einsum('te,ted->td', w_dense, eo)
        sh = jax.nn.silu(ht @ sw_gate) * (ht @ sw_up) @ sw_down
        return (moe + sh).reshape(b, s, d)
    x = x + _L0_xattn_ref(_layernorm(x, axis=-1), ctx_2048, L0_xattn_Wq, L0_xattn_bq, L0_xattn_Wk, L0_xattn_bk, L0_xattn_Wv, L0_xattn_bv, L0_xattn_Wo, L0_xattn_bo)
    x = x + _L0_ffn_ref(_layernorm(x, axis=-1), L0_ffn_rms_weight, L0_ffn_router_w, L0_ffn_w_gate, L0_ffn_w_up, L0_ffn_w_down, L0_ffn_sw_gate, L0_ffn_sw_up, L0_ffn_sw_down)
    return x

_drawn_inputs = setup_inputs


def setup_inputs(seed=0):
    import zlib

    import numpy as np

    out = dict(_drawn_inputs(seed))
    spreads = {'L0_xattn_bq': (0.0, 0.1),
     'L0_xattn_bk': (0.0, 0.8),
     'L0_xattn_bv': (0.0, 0.1),
     'L0_xattn_bo': (0.0, 0.1),
     'L0_ffn_rms_weight': (1.0, 0.6)}
    factors = {}
    for name, (base, spread) in spreads.items():
        noise = np.random.default_rng([zlib.crc32(name.encode()), seed]).standard_normal(out[name].shape)
        drawn = base * np.exp(spread * noise) if base else spread * noise
        out[name] = jnp.asarray(drawn.astype(out[name].dtype))
    for name, factor in factors.items():
        out[name] = (out[name] * factor).astype(out[name].dtype)
    return out
```

```python
from contextlib import ExitStack

import concourse.bass as bass
from concourse import mybir

ALU = mybir.AluOpType
ACT = mybir.ActivationFunctionType
BF16 = mybir.dt.bfloat16
F32 = mybir.dt.float32
I32 = mybir.dt.int32
AX_X = mybir.AxisListType.X

P = 128
B, C, T = 8, 256, 512
HEADS, KCH = 16, 16
SCALE = float(KCH) ** -0.5
HALVES = 2 * B
HH = 8
CT = C // P
TT = T // P
UNITS = 16
LEAD = 4
PARTS = 3
Q_PART = (0, 0, 1, 0, 1, 2)
K_PART = (0, 1, 0, 2, 1, 0)
SROWS = KCH * len(Q_PART)
NBUF = 4
LN_EPS, RMS_EPS = 1e-5, 1e-6
E, F, D = 8, 256, T
FT, DT = F // P, D // P
NTILE = B * C // P
TOPK = 2
EXPERT_BLOCKS = NTILE * TOPK + E - 1
BLOCKS = NTILE + EXPERT_BLOCKS


def xattn_ffn_kernel(nc, x, ctxt, wq, bq, wk, bk, wv, bv, wo, bo, rms_w, router_w, w_gate, w_up, w_down,
                     sw_gate, sw_up, sw_down, out):
    x_t = x.rearrange("b (o p) t -> b p o t", p=P)
    c_t = ctxt.rearrange("b (o p) t -> b p o t", p=P)
    parts_dram = nc.dram_tensor("parts_dram", [NBUF, 2, PARTS, P, T], BF16, kind="Internal").ap()
    den_dram = nc.dram_tensor("den_dram", [4, 2, T], F32, kind="Internal").ap()
    rec_dram = nc.dram_tensor("rec_dram", [4, 2, T], F32, kind="Internal").ap()
    blocks_in = nc.dram_tensor("blocks_in", [BLOCKS, P, D], F32, kind="Internal").ap()
    blocks_out = nc.dram_tensor("blocks_out", [BLOCKS, P, D], F32, kind="Internal").ap()
    rows_in = blocks_in.rearrange("k p d -> (k p) d")
    rows_out = blocks_out.rearrange("k p d -> (k p) d")
    out_t = out.rearrange("b (o p) t -> (b o) p t", p=P)
    rows_dram = nc.dram_tensor("rows_dram", [NBUF, PARTS, HH * TT, P], BF16, kind="Internal").ap()

    with ExitStack() as outer:
        def sem(name):
            return outer.enter_context(nc.semaphore(name))

        def sb(name, shape, dt=F32, stack=outer):
            return stack.enter_context(nc.sbuf_tensor(name, shape, dt))

        x_sb = sb("x_sb", [P, B * CT, T])
        ident = sb("ident", [P, P])
        zeros = sb("zeros", [P, D])
        stats = sb("stats", [P, B * CT, 6])
        mv = sb("mv", [P, B * CT, 2])
        rstd = sb("rstd", [P, B * CT])
        rs_a = sb("rs_a", [P, B * CT])
        rs_b = sb("rs_b", [P, B * CT])

        attn_ctx = ExitStack()

        def asb(name, shape, dt=F32):
            return sb(name, shape, dt, attn_ctx)

        def aps(name, shape, dt=F32):
            return attn_ctx.enter_context(nc.psum_tensor(name, shape, dt))

        q_stack = [asb(f"q_stack{i}", [P, HH, T], BF16) for i in range(NBUF)]
        k_stack = [asb(f"k_stack{i}", [P, HH, T], BF16) for i in range(NBUF)]
        v_t = [asb(f"v_t{i}", [P, TT, HH, 32]) for i in range(NBUF)]
        probs = asb("probs", [P, 2, 4, T])
        attn = asb("attn", [P, 2, 4, T])
        c_sb = asb("c_sb", [P, 2, CT, T])
        xn = asb("xn", [P, CT, T])
        qk32 = asb("qk32", [P, 2, T])
        rest = asb("rest", [P, 2, T])
        parts = asb("parts", [P, 2, PARTS, T], BF16)
        recip = asb("recip", [P, 2, T])
        den = asb("den", [P, 4 * 2 * T // P])
        negmax = asb("negmax", [P, 2, HH * TT])
        nm32 = asb("nm32", [HH * TT, P])
        nm_rest = asb("nm_rest", [HH * TT, P])
        nm_parts = asb("nm_parts", [HH * TT, PARTS, P], BF16)
        w_raw = asb("w_raw", [P, 3, CT, C])
        wo_raw = asb("wo_raw", [P, CT, HEADS, 32])
        w_t = asb("w_t", [P, 3, CT, C])
        wo_t = asb("wo_t", [P, 4, C])
        bqk = asb("bqk", [P, 2, CT])
        bo_col = asb("bo_col", [P, CT])
        bo_all = asb("bo_all", [P, CT])
        bv_pad = asb("bv_pad", [P, 4])

        smax_ps = aps("smax_ps", [P, 2, T])
        st_ps = aps("st_ps", [P, 2, 2, T])
        pv_ps = aps("pv_ps", [P, T])
        proj_ps = aps("proj_ps", [P, T])

        ident_ready = sem("ident_ready")
        pads_zero = sem("pads_zero")
        ones_ready = sem("ones_ready")
        w_loaded = sem("w_loaded")
        wo_loaded = sem("wo_loaded")
        b_loaded = sem("b_loaded")
        c_loaded = [sem(f"c_loaded{i}") for i in range(2)]
        x0_loaded = sem("x0_loaded")
        xr_loaded = sem("xr_loaded")
        wt_ready = sem("wt_ready")
        wt_copied = sem("wt_copied")
        bo_ready = sem("bo_ready")
        bo_added = sem("bo_added")
        var_ready = sem("var_ready")
        std_ready = sem("std_ready")
        rstd_ready = sem("rstd_ready")
        dve_step = sem("dve_step")
        xn_ready = sem("xn_ready")
        qk_ready = sem("qk_ready")
        qk32_ready = sem("qk32_ready")
        high_ready = sem("high_ready")
        mid_rest_ready = sem("mid_rest_ready")
        mid_ready = sem("mid_ready")
        low_ready = sem("low_ready")
        parts_written = [sem(f"parts_written{i}") for i in range(2)]
        stack_loaded = [sem(f"stack_loaded{i}") for i in range(NBUF)]
        v_ready = sem("v_ready")
        vt_copied = sem("vt_copied")
        s_ready = sem("s_ready")
        max_done = sem("max_done")
        nm_turned = sem("nm_turned")
        nm_copied = sem("nm_copied")
        nm_step = sem("nm_step")
        nm_parts_ready = sem("nm_parts_ready")
        rows_written = sem("rows_written")
        rows_loaded = [sem(f"rows_loaded{i}") for i in range(NBUF)]
        st_ready = sem("st_ready")
        exp_done = sem("exp_done")
        pv_done = sem("pv_done")
        pv_copied = sem("pv_copied")
        recip_ones = sem("recip_ones")
        zeros_ready = sem("zeros_ready")
        zeroed = sem("zeroed")
        den_written = sem("den_written")
        den_loaded = sem("den_loaded")
        den_inverted = sem("den_inverted")
        rec_written = sem("rec_written")
        rec_loaded = sem("rec_loaded")
        attn_ready = sem("attn_ready")
        y_ready = sem("y_ready")
        x1_ready = sem("x1_ready")

        LOOP_SLOTS = 4
        LOOPS = 3

        def sync_wait(sp, sem, value):
            if not isinstance(value, int):
                sp.wait_ge(zeros_ready, 1)
            sp.wait_ge(sem, value)

        def slots(eng, slot, tail):
            slot(0, 0, False)
            with eng.Fori(0, LOOPS) as it:
                for s0 in range(1, 1 + LOOP_SLOTS):
                    slot(s0, it, True)
            for s in range(1 + LOOP_SLOTS * LOOPS, HALVES):
                slot(s, 0, False)
            tail(HALVES, 0, False)

        def at(per_slot, first, it):
            return first + per_slot * LOOP_SLOTS * it

        count = {"step": 0}

        with nc.Block() as block:

            @block.sync
            def _(sp):
                sp.dma_start(x_sb[:, 0:CT, :], x_t[0]).then_inc(x0_loaded, 16)
                for i, w in enumerate((wq, wk, wv)):
                    sp.dma_start(w_raw[:, i, :, :], w.rearrange("(o p) c -> p o c", p=P)).then_inc(w_loaded, 16)
                sp.dma_start(c_sb[:, 0, :, :], c_t[0]).then_inc(c_loaded[0], 16)
                sp.dma_start(bqk[:, 0, :], bq.rearrange("(o p) -> p o", p=P),
                             allow_slow_non_contiguous=True).then_inc(b_loaded, 16)
                sp.dma_start(bqk[:, 1, :], bk.rearrange("(o p) -> p o", p=P),
                             allow_slow_non_contiguous=True).then_inc(b_loaded, 16)
                sp.dma_start(bo_col[:, :], bo.rearrange("(o p) -> p o", p=P),
                             allow_slow_non_contiguous=True).then_inc(b_loaded, 16)
                sync_wait(sp, pads_zero, 2)
                for o in range(CT):
                    sp.dma_start(wo_raw[:, o, :, 0:KCH],
                                 wo[o * P:(o + 1) * P, :].rearrange("p (h k) -> p h k", k=KCH)).then_inc(wo_loaded, 16)
                for j in range(4):
                    sp.dma_start(bv_pad[32 * j:32 * j + KCH, :],
                                 bv.rearrange("(g j k) -> j k g", j=4, k=KCH)[j],
                                 allow_slow_non_contiguous=True).then_inc(b_loaded, 16)
                for b in range(1, B):
                    sp.dma_start(x_sb[:, CT * b:CT * b + CT, :], x_t[b]).then_inc(xr_loaded, 16)

                def stack(n0, it):
                    if not (isinstance(it, int) and n0 < NBUF):
                        sync_wait(sp, st_ready, at(UNITS, UNITS * (n0 - NBUF + 1), it))
                    for i in range(2):
                        sync_wait(sp, low_ready, at(2, 2 * n0 + i + 1, it))
                        sp.dma_start(parts_dram[n0 % NBUF, i].rearrange("s p t -> p s t"),
                                     parts[:, i, :, :]).then_inc(parts_written[i], 16)
                    for i, (dst, order) in enumerate(((q_stack, Q_PART), (k_stack, K_PART))):
                        sync_wait(sp, parts_written[i], at(16, 16 * (n0 + 1), it))
                        for g, part in enumerate(order):
                            sp.dma_start(dst[n0 % NBUF][KCH * g:KCH * (g + 1), :, :],
                                         parts_dram[n0 % NBUF, i, part].rearrange("(h i) t -> i h t", i=KCH)
                                         ).then_inc(stack_loaded[n0 % NBUF], 16)

                def rows(n0, it):
                    sync_wait(sp, nm_parts_ready, at(1, n0 + 1, it))
                    sp.dma_start(rows_dram[n0 % NBUF].rearrange("s r t -> r s t"),
                                 nm_parts[:, :, :]).then_inc(rows_written, 16)
                    sync_wait(sp, rows_written, at(16, 16 * (n0 + 1), it))
                    sp.dma_start(q_stack[n0 % NBUF][SROWS:SROWS + PARTS, :, :],
                                 rows_dram[n0 % NBUF].rearrange("s (h j) t -> s h (j t)", h=HH)
                                 ).then_inc(rows_loaded[n0 % NBUF], 16)

                def denominators(n0, it):
                    sync_wait(sp, pv_copied, at(2, 2 * n0 + 2, it))
                    sp.dma_start(den_dram[:, :, :],
                                 attn[KCH:P:32, n0 // 2 % 2, 2 * (n0 % 2):2 * (n0 % 2) + 2, :]).then_inc(den_written, 16)
                    sync_wait(sp, den_written, at(16, 16 * (n0 + 1), it))
                    sp.dma_start(den[:, :], den_dram.rearrange("j g (q r) -> (j g q) r", r=4 * 2 * T // P)
                                 ).then_inc(den_loaded, 16)
                    sync_wait(sp, den_inverted, at(1, n0 + 1, it))
                    if not (isinstance(it, int) and n0 == 0):
                        sync_wait(sp, attn_ready, at(1, n0, it))
                    sp.dma_start(rec_dram.rearrange("j g (q r) -> (j g q) r", r=4 * 2 * T // P), den[:, :]
                                 ).then_inc(rec_written, 16)
                    sync_wait(sp, rec_written, at(16, 16 * (n0 + 1), it))
                    if n0 == 0:
                        sync_wait(sp, recip_ones, 1)
                    for j in range(4):
                        sp.dma_start(recip[32 * j:32 * j + KCH, :, :],
                                     rec_dram[j:j + 1, :, :].broadcast_to([KCH, 2, T])).then_inc(rec_loaded, 16)

                def load_c(n0, it):
                    b0 = n0 // 2
                    src = c_t[b0 + 2 * it]
                    sync_wait(sp, v_ready, at(1, n0 - 2, it))
                    sp.dma_start(c_sb[:, b0 % 2, :, :], src).then_inc(c_loaded[b0 % 2], 16)

                sp.dma_start(c_sb[:, 1, :, :], c_t[1]).then_inc(c_loaded[1], 16)
                stack(0, 0)
                stack(1, 0)
                rows(0, 0)

                def clear_blocks(s0, it):
                    if s0 == 1:
                        sync_wait(sp, zeros_ready, 1)
                    for k in range(3):
                        sp.dma_start(blocks_in[NTILE + 3 * (s0 - 1) + k + 3 * LOOP_SLOTS * it], zeros[:, :]
                                     ).then_inc(zeroed, 16)

                def slot(s0, it, loop):
                    if loop or s0 > 0:
                        denominators(s0 - 1, it)
                    if loop or 0 < s0 <= EXPERT_BLOCKS // 3:
                        clear_blocks(s0, it)
                    if loop or s0 + 2 < HALVES:
                        stack(s0 + 2, it)
                    if s0 % 2 == 1 and (loop or s0 + 3 < HALVES):
                        load_c(s0 + 3, it)
                    if loop or s0 + 1 < HALVES:
                        rows(s0 + 1, it)

                slots(sp, slot, lambda s0, it, loop: denominators(s0 - 1, it))
                sync_wait(sp, zeroed, 16 * EXPERT_BLOCKS)

            @block.gpsimd
            def _(pool):
                nc.gpsimd.memset(ident[:, :], 0.0).then_inc(ident_ready, 1)
                pool.wait_ge(ident_ready, 1)
                nc.gpsimd.affine_select(out=ident[:, :], in_=ident[:, :], compare_op=ALU.not_equal, fill=1.0,
                                        base=0, pattern=[[-1, P]], channel_multiplier=1).then_inc(ident_ready, 1)
                nc.gpsimd.memset(wo_raw[:, :, :, :], 0.0).then_inc(pads_zero, 1)
                nc.gpsimd.memset(bv_pad[:, :], 0.0).then_inc(pads_zero, 1)
                pool.wait_ge(pads_zero, 2)
                for i in range(NBUF):
                    nc.gpsimd.memset(k_stack[i][SROWS:SROWS + PARTS, :, :], 1.0).then_inc(ones_ready, 1)
                    pool.wait_ge(ones_ready, 2 * i + 1)
                    nc.gpsimd.memset(v_t[i][:, :, :, KCH:32], 1.0).then_inc(ones_ready, 1)
                    pool.wait_ge(ones_ready, 2 * i + 2)

                def split(n0, it):
                    for i in range(2):
                        pool.wait_ge(high_ready, at(2, 2 * n0 + i + 1, it))
                        nc.gpsimd.tensor_tensor(rest[:, i, :], qk32[:, i, :], parts[:, i, 0, :],
                                                ALU.subtract).then_inc(mid_rest_ready, 1)
                        pool.wait_ge(mid_ready, at(2, 2 * n0 + i + 1, it))
                        nc.gpsimd.tensor_tensor(parts[:, i, 2, :], rest[:, i, :], parts[:, i, 1, :],
                                                ALU.subtract).then_inc(low_ready, 1)

                split(0, 0)
                split(1, 0)

                def slot(s0, it, loop):
                    if loop or s0 + 2 < HALVES:
                        split(s0 + 2, it)

                slots(pool, slot, lambda *a: None)

            @block.scalar
            def _(act):
                def std(lo, hi, i):
                    act.wait_ge(var_ready, i + 1)
                    nc.scalar.activation(rs_b[:, lo:hi], rs_a[:, lo:hi], ACT.Sqrt).then_inc(std_ready, 1)

                def qk_bias(n0, i, it):
                    act.wait_ge(qk_ready, at(2, 2 * n0 + i + 1, it))
                    if not (isinstance(it, int) and n0 == 0):
                        act.wait_ge(mid_rest_ready, at(2, 2 * n0 + i - 1, it))
                    nc.scalar.activation(qk32[:, i, :], proj_ps[:, :], ACT.Identity,
                                         bias=bqk[:, i, n0 % 2:n0 % 2 + 1]).then_inc(qk32_ready, 1)

                def v_copy(n0, it):
                    act.wait_ge(v_ready, at(1, n0 + 1, it))
                    if not (isinstance(it, int) and n0 < NBUF):
                        act.wait_ge(pv_done, at(8, 8 * (n0 - NBUF + 1), it))
                    nc.scalar.activation(v_t[n0 % NBUF][:, :, :, 0:KCH],
                                         proj_ps[:, :].rearrange("p (s h k) -> p s h k", s=TT, k=KCH),
                                         ACT.Copy).then_inc(vt_copied, 1)

                std(0, CT, 0)
                act.wait_ge(b_loaded, 16 * 7)
                for n in range(2):
                    qk_bias(n, 0, 0)
                    qk_bias(n, 1, 0)
                    v_copy(n, 0)
                    if n == 0:
                        std(CT, B * CT, 1)

                def pv_copy(g0, it):
                    act.wait_ge(pv_done, at(8, 4 * (g0 + 1), it))
                    if g0 % 4 == 0 and (not isinstance(it, int) or g0 >= 8):
                        act.wait_ge(nm_turned, at(1, g0 // 2, it))
                    nc.scalar.activation(attn[:, g0 // 4 % 2, g0 % 4, :], pv_ps[:, :], ACT.Copy).then_inc(pv_copied, 1)

                def slot(s0, it, loop):
                    proj = loop or s0 + 2 < HALVES
                    for u in range(UNITS):
                        act.wait_ge(st_ready, at(UNITS, UNITS * s0 + u + 1, it))
                        k0 = 8 * s0 + u // 2
                        if u % 2 == 0 and (loop or k0 >= 2):
                            act.wait_ge(pv_done, at(8, k0 - 1, it))
                        nc.scalar.activation(probs[:, k0 % 2, 2 * (u % 2):2 * (u % 2) + 2, :],
                                             st_ps[:, u % 2, :, :], ACT.Exp, scale=SCALE).then_inc(exp_done, 1)
                        if u == 1 and (loop or s0 > 0):
                            pv_copy(2 * s0 - 1, it)
                        if u == 9:
                            pv_copy(2 * s0, it)
                        if proj and u == 1:
                            qk_bias(s0 + 2, 0, it)
                        if proj and u == 3:
                            qk_bias(s0 + 2, 1, it)
                        if proj and u == 5:
                            v_copy(s0 + 2, it)

                slots(act, slot, lambda s0, it, loop: pv_copy(2 * s0 - 1, it))

            @block.tensor
            def _(pe):
                pe.wait_ge(ident_ready, 2)
                pe.wait_ge(w_loaded, 16 * 3)
                for i in range(3):
                    for o in range(CT):
                        for kt in range(CT):
                            mm = nc.tensor.transpose(st_ps[:, i // 2, i % 2, kt * C + o * P:kt * C + (o + 1) * P],
                                                     w_raw[:, i, o, kt * P:(kt + 1) * P], ident[:, :])
                    mm.then_inc(wt_ready, 1)
                pe.wait_ge(wo_loaded, 16 * CT)
                for g in range(4):
                    for o in range(CT):
                        mm = nc.tensor.transpose(smax_ps[:, g // 2, (g % 2) * C + o * P:(g % 2) * C + (o + 1) * P],
                                                 wo_raw[:, o, 4 * g:4 * g + 4, :], ident[:, :])
                mm.then_inc(wt_ready, 1)
                pe.wait_ge(wt_copied, 5)
                pe.wait_ge(b_loaded, 16 * 7)
                for o in range(CT):
                    for g in range(4):
                        mm = nc.tensor.matmul(pv_ps[:, o:o + 1], wo_t[:, g, o * P:(o + 1) * P], bv_pad[:, g:g + 1],
                                              start=(g == 0), stop=(g == 3))
                mm.then_inc(bo_ready, 1)

                def project_qk(n0, i, it):
                    if i == 0:
                        pe.wait_ge(xn_ready, n0 // 2 + 1 + 2 * it)
                        pe.wait_ge(c_loaded[(n0 // 2) % 2], 16 * (n0 // 4 + 1) + 16 * it)
                        if not (isinstance(it, int) and n0 < 2):
                            pe.wait_ge(nm_copied, at(1, n0 - 1, it))
                        elif n0 == 1:
                            pe.wait_ge(vt_copied, 1)
                    else:
                        pe.wait_ge(qk32_ready, at(2, 2 * n0 + 1, it))
                    src = xn if i == 0 else c_sb[:, (n0 // 2) % 2, :, :]
                    for kt in range(CT):
                        mm = nc.tensor.matmul(proj_ps[:, :], w_t[:, i, kt, (n0 % 2) * P:(n0 % 2) * P + P],
                                              src[:, kt, :], start=(kt == 0), stop=(kt == CT - 1))
                    mm.then_inc(qk_ready, 1)

                def project_v(n0, it):
                    pe.wait_ge(qk32_ready, at(2, 2 * n0 + 2, it))
                    for st in range(TT):
                        for kt in range(CT):
                            mm = nc.tensor.matmul(proj_ps[:, st * P:(st + 1) * P],
                                                  c_sb[:, (n0 // 2) % 2, kt, st * P:(st + 1) * P],
                                                  w_t[:, 2, kt, (n0 % 2) * P:(n0 % 2) * P + P],
                                                  start=(kt == 0), stop=(kt == CT - 1))
                    mm.then_inc(v_ready, 1)

                def max_pass(n0, u, it):
                    n0s = n0 % NBUF
                    if u == 0:
                        pe.wait_ge(stack_loaded[n0s], 16 * 12 * (n0 // NBUF + 1) + 16 * 12 * it)
                    for r in range(2):
                        i0 = 32 * n0 + 2 * u + r
                        if not isinstance(it, int) or i0 >= 2:
                            pe.wait_ge(max_done, at(32, i0 - 1, it))
                        tt = 2 * (u % 2) + r
                        nc.tensor.matmul(smax_ps[:, r, :], q_stack[n0s][0:SROWS, u // 2, tt * P:(tt + 1) * P],
                                         k_stack[n0s][0:SROWS, u // 2, :], start=True, stop=True).then_inc(s_ready, 1)

                def turn_max(n0, after, it):
                    if after == "y":
                        pe.wait_ge(x1_ready, at(1, n0 - 1, it))
                    else:
                        pe.wait_ge(vt_copied, at(1, min(n0 + 2, HALVES), it))
                    pe.wait_ge(max_done, at(32, 32 * (n0 + 1), it))
                    nc.tensor.transpose(proj_ps[0:HH * TT, 0:P], negmax[:, n0 % 2, :], ident[:, :]).then_inc(nm_turned, 1)

                def scores(s0, u, it):
                    g, st, pair = u // 8, u // 2 % 4, u % 2
                    n0s = s0 % NBUF
                    if u == 0:
                        pe.wait_ge(rows_loaded[n0s], 16 * (s0 // NBUF + 1) + 16 * it)
                        pe.wait_ge(ones_ready, 2 * NBUF)
                    i0 = UNITS * s0 + u
                    if not isinstance(it, int) or i0 >= 2:
                        pe.wait_ge(exp_done, at(UNITS, i0 - 1, it))
                    for h in range(2):
                        head = 4 * g + 2 * pair + h
                        mm = nc.tensor.matmul(st_ps[:, u % 2, h, :],
                                              k_stack[n0s][0:SROWS + PARTS, head, st * P:(st + 1) * P],
                                              q_stack[n0s][0:SROWS + PARTS, head, :], start=True, stop=True)
                    mm.then_inc(st_ready, 1)

                def pv(k0, it):
                    n0, g, st = k0 // 8, k0 // 4 % 2, k0 % 4
                    pe.wait_ge(exp_done, at(UNITS, 2 * k0 + 2, it))
                    if st == 0 and (not isinstance(it, int) or k0 >= 4):
                        pe.wait_ge(pv_copied, at(2, k0 // 4, it))
                    if st == 0 and g == 0:
                        pe.wait_ge(vt_copied, at(1, n0 + 1, it))
                    for j in range(4):
                        mm = nc.tensor.matmul(pv_ps[32 * j:32 * j + 32, :], v_t[n0 % NBUF][:, st, 4 * g + j, :],
                                              probs[:, k0 % 2, j, :], start=(st == 0), stop=(st == 3),
                                              tile_position=(0, 32 * j))
                    mm.then_inc(pv_done, 1)

                def project_out(s0, o, part, it):
                    b0 = s0 // 2 - 1
                    if part == 0:
                        if o == 0:
                            pe.wait_ge(attn_ready, at(1, 2 * (b0 + 1), it))
                            if s0 + 2 < HALVES:
                                pe.wait_ge(vt_copied, at(1, s0 + 3, it))
                            else:
                                pe.wait_ge(nm_copied, min(s0 + 1, HALVES))
                        else:
                            pe.wait_ge(x1_ready, 2 * b0 + 1 + 4 * it)
                    for g in (2 * part, 2 * part + 1):
                        mm = nc.tensor.matmul(proj_ps[:, :], wo_t[:, g, o * P:(o + 1) * P], attn[:, b0 % 2, g, :],
                                              start=(g == 0), stop=(g == 3))
                    if part == 1:
                        mm.then_inc(y_ready, 1)

                pe.wait_ge(bo_added, 1)
                for n in range(2):
                    project_qk(n, 0, 0)
                    project_qk(n, 1, 0)
                    project_v(n, 0)
                    if n == 0:
                        for u in range(UNITS):
                            max_pass(0, u, 0)
                turn_max(0, "v", 0)
                for u in range(LEAD):
                    max_pass(1, u, 0)

                def slot(s0, it, loop):
                    outs = s0 % 2 == 0 and s0 > 0
                    proj = loop or s0 + 2 < HALVES
                    for u in range(UNITS):
                        scores(s0, u, it)
                        if u % 2 == 1 and (loop or 8 * s0 + (u - 3) // 2 >= 0):
                            pv(8 * s0 + (u - 3) // 2, it)
                        n0 = s0 + 1 + (u + LEAD) // UNITS
                        if loop or n0 < HALVES:
                            max_pass(n0, (u + LEAD) % UNITS, it)
                        if proj and u == 0:
                            project_qk(s0 + 2, 0, it)
                        if proj and u == 2:
                            project_qk(s0 + 2, 1, it)
                        if proj and u == 4:
                            project_v(s0 + 2, it)
                        if outs and 8 <= u < 12:
                            project_out(s0, (u - 8) // 2, u % 2, it)
                        if u == 12 and (loop or s0 + 1 < HALVES):
                            turn_max(s0 + 1, "y" if outs else "v", it)

                def tail(s0, it, loop):
                    pv(8 * s0 - 1, it)
                    for o in range(CT):
                        project_out(s0, o, 0, it)
                        project_out(s0, o, 1, it)

                slots(pe, slot, tail)

            @block.vector
            def _(dve):
                def chained(ins):
                    count["step"] += 1
                    ins.then_inc(dve_step, 1)
                    dve.wait_ge(dve_step, count["step"])

                def row_stats(lo, hi, i):
                    for t in range(lo, hi):
                        last = nc.vector.bn_stats(stats[:, t, :], x_sb[:, t, :])
                    chained(last)
                    for t in range(lo, hi):
                        last = nc.vector.bn_aggr(mv[:, t, :], stats[:, t, :])
                    chained(last)
                    nc.vector.tensor_scalar(rs_a[:, lo:hi], mv[:, lo:hi, 1], LN_EPS, None, ALU.add).then_inc(var_ready, 1)

                def row_rstd(lo, hi, i):
                    dve.wait_ge(std_ready, i + 1)
                    chained(nc.vector.reciprocal(rs_b[:, lo:hi], rs_b[:, lo:hi]))
                    chained(nc.vector.tensor_tensor(rs_a[:, lo:hi], rs_a[:, lo:hi], rs_b[:, lo:hi], ALU.mult))
                    chained(nc.vector.tensor_tensor(rs_a[:, lo:hi], rs_a[:, lo:hi], rs_b[:, lo:hi], ALU.mult))
                    chained(nc.vector.tensor_scalar(rs_a[:, lo:hi], rs_a[:, lo:hi], -0.5, 1.5, ALU.mult, ALU.add))
                    chained(nc.vector.tensor_tensor(rstd[:, lo:hi], rs_a[:, lo:hi], rs_b[:, lo:hi], ALU.mult))

                def normalize(b0, it):
                    if not (isinstance(it, int) and b0 == 0):
                        dve.wait_ge(qk_ready, at(2, 2 * (2 * b0 - 1) + 1, it))
                    for ct in range(CT):
                        t = CT * b0 + ct + 2 * CT * it
                        last = nc.vector.tensor_scalar(xn[:, ct, :], x_sb[:, t, :], mv[:, t, 0:1], rstd[:, bass.ds(t, 1)],
                                                       ALU.subtract, ALU.mult)
                    last.then_inc(xn_ready, 1)

                def high(n0, i, it):
                    dve.wait_ge(qk32_ready, at(2, 2 * n0 + i + 1, it))
                    if not (isinstance(it, int) and n0 == 0):
                        dve.wait_ge(parts_written[i], at(16, 16 * n0, it))
                    nc.vector.tensor_copy(parts[:, i, 0, :], qk32[:, i, :]).then_inc(high_ready, 1)

                def mid(n0, i, it):
                    dve.wait_ge(mid_rest_ready, at(2, 2 * n0 + i + 1, it))
                    nc.vector.tensor_copy(parts[:, i, 1, :], rest[:, i, :]).then_inc(mid_ready, 1)

                def maxima(n0, u, it):
                    for r in range(2):
                        i0 = 32 * n0 + 2 * u + r
                        dve.wait_ge(s_ready, at(32, i0 + 1, it))
                        if u == 0 and r == 0 and (not isinstance(it, int) or n0 >= 2):
                            dve.wait_ge(nm_turned, at(1, n0 - 1, it))
                        nc.vector.tensor_reduce(negmax[:, n0 % 2, 2 * u + r:2 * u + r + 1], smax_ps[:, r, :],
                                                AX_X, ALU.max, negate=True).then_inc(max_done, 1)

                def max_parts(n0, it):
                    dve.wait_ge(nm_turned, at(1, n0 + 1, it))
                    nc.vector.tensor_copy(nm32[:, :], proj_ps[0:HH * TT, 0:P]).then_inc(nm_copied, 1)
                    dve.wait_ge(nm_copied, at(1, n0 + 1, it))
                    if not (isinstance(it, int) and n0 == 0):
                        dve.wait_ge(rows_written, at(16, 16 * n0, it))
                    nc.vector.tensor_copy(nm_parts[:, 0, :], nm32[:, :]).then_inc(nm_step, 1)
                    dve.wait_ge(nm_step, at(3, 3 * n0 + 1, it))
                    nc.vector.tensor_tensor(nm_rest[:, :], nm32[:, :], nm_parts[:, 0, :], ALU.subtract).then_inc(nm_step, 1)
                    dve.wait_ge(nm_step, at(3, 3 * n0 + 2, it))
                    nc.vector.tensor_copy(nm_parts[:, 1, :], nm_rest[:, :]).then_inc(nm_step, 1)
                    dve.wait_ge(nm_step, at(3, 3 * n0 + 3, it))
                    nc.vector.tensor_tensor(nm_parts[:, 2, :], nm_rest[:, :], nm_parts[:, 1, :],
                                            ALU.subtract).then_inc(nm_parts_ready, 1)

                def invert(n0, it):
                    dve.wait_ge(den_loaded, at(16, 16 * (n0 + 1), it))
                    nc.vector.reciprocal(den[:, :], den[:, :]).then_inc(den_inverted, 1)

                def divide(n0, it):
                    dve.wait_ge(rec_loaded, at(64, 64 * (n0 + 1), it))
                    half = attn[:, n0 // 2 % 2, 2 * (n0 % 2):2 * (n0 % 2) + 2, :]
                    nc.vector.tensor_tensor(half, half, recip[:, :, :], ALU.mult).then_inc(attn_ready, 1)

                def residual(s0, o, it):
                    b0 = s0 // 2 - 1
                    dve.wait_ge(y_ready, 2 * b0 + o + 1 + 4 * it)
                    t = CT * b0 + o + 2 * CT * it
                    nc.vector.scalar_tensor_tensor(out=x_sb[:, t, :], in0=proj_ps[:, :], scalar=bo_all[:, o:o + 1],
                                                   in1=x_sb[:, t, :], op0=ALU.add, op1=ALU.add).then_inc(x1_ready, 1)

                nc.vector.memset(recip[:, :, :], 1.0).then_inc(recip_ones, 1)
                nc.vector.memset(zeros[:, :], 0.0).then_inc(zeros_ready, 1)
                dve.wait_ge(x0_loaded, 16)
                row_stats(0, CT, 0)
                row_rstd(0, CT, 0)
                normalize(0, 0)
                for i in range(3):
                    dve.wait_ge(wt_ready, i + 1)
                    nc.vector.tensor_copy(w_t[:, i, :, :], st_ps[:, i // 2, i % 2, :].rearrange("p (k c) -> p k c", k=CT)
                                          ).then_inc(wt_copied, 1)
                dve.wait_ge(wt_ready, 4)
                for i in range(2):
                    nc.vector.tensor_copy(wo_t[:, 2 * i:2 * i + 2, :], smax_ps[:, i, :].rearrange("p (k c) -> p k c", k=2)
                                          ).then_inc(wt_copied, 1)
                dve.wait_ge(bo_ready, 1)
                nc.vector.tensor_tensor(bo_all[:, :], bo_col[:, :], pv_ps[:, 0:CT], ALU.add).then_inc(bo_added, 1)
                high(0, 0, 0)
                mid(0, 0, 0)
                high(0, 1, 0)
                mid(0, 1, 0)
                dve.wait_ge(xr_loaded, 16 * (B - 1))
                row_stats(CT, B * CT, 1)
                row_rstd(CT, B * CT, 1)
                for u in range(UNITS):
                    maxima(0, u, 0)
                high(1, 0, 0)
                mid(1, 0, 0)
                high(1, 1, 0)
                mid(1, 1, 0)
                normalize(1, 0)
                max_parts(0, 0)
                for u in range(LEAD):
                    maxima(1, u, 0)

                def slot(s0, it, loop):
                    outs = s0 % 2 == 0 and s0 > 0
                    proj = loop or s0 + 2 < HALVES
                    for u in range(UNITS):
                        n0 = s0 + 1 + (u + LEAD) // UNITS
                        if loop or n0 < HALVES:
                            maxima(n0, (u + LEAD) % UNITS, it)
                        if proj and u in (1, 3):
                            high(s0 + 2, u // 2, it)
                        if proj and u in (3, 5):
                            mid(s0 + 2, u // 4, it)
                        if u == 4 and (loop or s0 > 0):
                            invert(s0 - 1, it)
                        if u == 7 and (loop or s0 > 0):
                            divide(s0 - 1, it)
                        if outs and u == 9:
                            residual(s0, 0, it)
                        if outs and u == 11:
                            residual(s0, 1, it)
                        if u == 6 and s0 % 2 == 1 and (loop or s0 + 3 < HALVES):
                            normalize((s0 + 3) // 2, it)
                        if u == 12 and (loop or s0 + 1 < HALVES):
                            max_parts(s0 + 1, it)

                def tail(s0, it, loop):
                    invert(s0 - 1, it)
                    divide(s0 - 1, it)
                    for o in range(CT):
                        residual(s0, o, it)

                slots(dve, slot, tail)

        attn_ctx.close()

        token_ctx = ExitStack()

        def tsb(name, shape, dt=F32):
            return sb(name, shape, dt, token_ctx)

        def tps(name, shape, dt=F32):
            return token_ctx.enter_context(nc.psum_tensor(name, shape, dt))

        w_gu = tsb("w_gu", [P, E + 1, DT, 2 * F])
        w_dn = tsb("w_dn", [P, E + 1, FT, D])
        w_rt = tsb("w_rt", [P, DT, E])
        rms_bc = tsb("rms_bc", [P, D])
        h_ring = tsb("h_ring", [P, 2, D])
        h_all = tsb("h_all", [P, NTILE, D])
        h_t = tsb("h_t", [P, 2, DT, P])
        h_in = tsb("h_in", [P, 2, D])
        sig_g = tsb("sig_g", [P, F])
        act_gu = tsb("act_gu", [P, F])
        act_t = tsb("act_t", [P, FT, P])
        y_sb = tsb("y_sb", [P, 2, D])
        NR = 8
        rt = tsb("rt", [P, NR, NTILE, E])
        small = tsb("small", [P, 16, NTILE])
        blk = tsb("blk", [P, 48, E])
        blk_e = tsb("blk_e", [P, 64])
        blk_i = tsb("blk_i", [P, 64], I32)
        slot_i = tsb("slot_i", [P, 2, NTILE], I32)
        iota_i = tsb("iota_i", [P, 64], I32)
        iota = tsb("iota", [P, 64])
        rank = tsb("rank", [P, E])
        chosen = tsb("chosen", [P, NTILE, E], BF16)
        before = tsb("before", [P, P], BF16)
        ones_bf = tsb("ones_bf", [P, P], BF16)

        tr_ps = tps("tr_ps", [P, 2, D])
        lg_ps = tps("lg_ps", [P, NTILE, E])
        cnt_ps = tps("cnt_ps", [P, 2, NTILE, E])
        gu_ps = tps("gu_ps", [P, 2 * F])
        at_ps = tps("at_ps", [P, FT, P])
        y_ps = tps("y_ps", [P, 2, D])

        wgu_loaded = sem("wgu_loaded")
        wdn_loaded = sem("wdn_loaded")
        wrt_loaded = sem("wrt_loaded")
        rms_loaded = sem("rms_loaded")
        const_ready = sem("const_ready")
        var2_ready = sem("var2_ready")
        std2_ready = sem("std2_ready")
        h_part = sem("h_part")
        h_ready = sem("h_ready")
        h_kept = sem("h_kept")
        h_stored = [sem(f"h_stored{i}") for i in range(2)]
        h_turned = sem("h_turned")
        ht_ready = sem("ht_ready")
        lg_ready = sem("lg_ready")
        gap_ready = sem("gap_ready")
        egap_ready = sem("egap_ready")
        chosen_ready = sem("chosen_ready")
        cnt_ready = sem("cnt_ready")
        slots_ready = sem("slots_ready")
        blocks_ready = sem("blocks_ready")
        scattered = sem("scattered")
        in_loaded = [sem(f"in_loaded{i}") for i in range(2)]
        in_turned = sem("in_turned")
        inT_ready = sem("inT_ready")
        gu_ready = sem("gu_ready")
        silu_done = sem("silu_done")
        act_ready = sem("act_ready")
        act_turned = sem("act_turned")
        actT_ready = sem("actT_ready")
        dn_ready = sem("dn_ready")
        y_copied = sem("y_copied")
        y_stored = [sem(f"y_stored{i}") for i in range(2)]
        sh_loaded = [sem(f"sh_loaded{i}") for i in range(2)]
        got = [[sem(f"got{c}{i}") for i in range(4)] for c in range(TOPK)]
        mixed = sem("mixed")
        out_stored = sem("out_stored")

        def pairs(eng, step, n):
            rounds = (n - 4) // 2
            for t in range(3):
                step(t, 0)
            with eng.Fori(0, rounds) as it:
                step(3, it)
                step(4, it)
            for t in range(3 + 2 * rounds, n):
                step(t, 0)

        def inner(k0, lag, it):
            return k0 >= lag or not isinstance(it, int)

        with nc.Block() as block:

            @block.sync
            def _(sp):
                sp.dma_start(rms_bc[:, :], rms_w.rearrange("(o d) -> o d", o=1).broadcast_to([P, D])).then_inc(rms_loaded, 16)
                sp.dma_start(w_rt[:, :, :], router_w.rearrange("(a p) e -> p a e", p=P)).then_inc(wrt_loaded, 16)

                def keep_h(t0, it):
                    dst = blocks_in[t0 + 2 * it]
                    sync_wait(sp, h_ready, t0 + 1 + 2 * it)
                    sp.dma_start(dst, h_ring[:, t0 % 2, :]).then_inc(h_stored[t0 % 2], 16)

                pairs(sp, keep_h, NTILE)
                for i in range(2):
                    sync_wait(sp, h_stored[i], 16 * NTILE // 2)

                def load(k0, it):
                    src = blocks_in[k0 + 2 * it]
                    if inner(k0, 2, it):
                        sync_wait(sp, in_turned, k0 - 1 + 2 * it)
                    sp.dma_start(h_in[:, k0 % 2, :], src).then_inc(in_loaded[k0 % 2], 16)

                def store(k0, it):
                    dst = blocks_out[k0 + 2 * it]
                    sync_wait(sp, y_copied, k0 + 1 + 2 * it)
                    sp.dma_start(dst, y_sb[:, k0 % 2, :]).then_inc(y_stored[k0 % 2], 16)

                load(0, 0)
                load(1, 0)
                shared_rounds = (NTILE - 2) // 2
                with sp.Fori(0, shared_rounds) as it:
                    for k0 in range(2):
                        load(k0 + 2, it)
                        store(k0, it)
                sync_wait(sp, scattered, 16 * TOPK * NTILE)
                with sp.Fori(shared_rounds, (BLOCKS - 3) // 2) as it:
                    for k0 in range(2):
                        load(k0 + 2, it)
                        store(k0, it)
                load(BLOCKS - 1, 0)
                for k in range(BLOCKS - 3, BLOCKS):
                    store(k, 0)
                for i in range(2):
                    sync_wait(sp, y_stored[i], 16 * ((BLOCKS + 1 - i) // 2))
                for t in range(NTILE + 1):
                    if t < NTILE:
                        if t >= 2:
                            sync_wait(sp, mixed, t - 1)
                        sp.dma_start(h_in[:, t % 2, :], blocks_out[t]).then_inc(sh_loaded[t % 2], 16)
                    if t >= 1:
                        sync_wait(sp, mixed, t)
                        sp.dma_start(out_t[t - 1], x_sb[:, t - 1, :]).then_inc(out_stored, 16)
                sync_wait(sp, out_stored, 16 * NTILE)

            @block.gpsimd
            def _(pool):
                nc.gpsimd.iota(iota_i[:, :], [[1, 64]], base=0, channel_multiplier=0).then_inc(const_ready, 1)
                nc.gpsimd.memset(ones_bf[:, :], 1.0).then_inc(const_ready, 1)
                pool.wait_ge(const_ready, 2)
                nc.gpsimd.affine_select(out=before[:, :], in_=ones_bf[:, :], compare_op=ALU.is_ge, fill=0.0,
                                        base=-1, pattern=[[1, P]], channel_multiplier=-1).then_inc(const_ready, 1)

                def keep(t0, it):
                    pool.wait_ge(h_ready, t0 + 1 + 2 * it)
                    nc.gpsimd.tensor_copy(h_all[:, bass.ds(t0 + 2 * it, 1), :], h_ring[:, t0 % 2:t0 % 2 + 1, :]
                                          ).then_inc(h_kept, 1)

                pairs(pool, keep, NTILE)
                pool.wait_ge(slots_ready, 1)
                for i in range(2):
                    pool.wait_ge(h_stored[i], 16 * NTILE // 2)
                pool.wait_ge(h_kept, NTILE)
                for t in range(NTILE):
                    for c in range(2):
                        nc.gpsimd.indirect_dma_start(
                            rows_in, bass.IndirectOffsetOnAxis(ap=slot_i[:, c, t:t + 1], axis=0),
                            h_all[:, t, :], None).then_inc(scattered, 16)
                for i in range(2):
                    pool.wait_ge(y_stored[i], 16 * ((BLOCKS + 1 - i) // 2))
                pool.wait_ge(scattered, 16 * 2 * NTILE)
                for t in range(NTILE):
                    if t >= 4:
                        pool.wait_ge(mixed, t - 3)
                    for c in range(2):
                        nc.gpsimd.indirect_dma_start(
                            h_all[:, 2 * (t % 4) + c, :], None, rows_out,
                            bass.IndirectOffsetOnAxis(ap=slot_i[:, c, t:t + 1], axis=0)).then_inc(got[c][t % 4], 16)

            @block.scalar
            def _(act):
                for e in [E] + list(range(E)):
                    gate, up, down = (sw_gate, sw_up, sw_down) if e == E else (w_gate[e], w_up[e], w_down[e])
                    act.dma_start(w_gu[:, e, :, 0:F], gate.rearrange("(a p) f -> p a f", p=P)).then_inc(wgu_loaded, 16)
                    act.dma_start(w_gu[:, e, :, F:2 * F], up.rearrange("(a p) f -> p a f", p=P)).then_inc(wgu_loaded, 16)
                    act.dma_start(w_dn[:, e, :, :], down.rearrange("(a p) d -> p a d", p=P)).then_inc(wdn_loaded, 16)
                for i in range(2):
                    act.wait_ge(var2_ready, i + 1)
                    nc.scalar.activation(rs_b[:, :], rs_a[:, :], ACT.Sqrt).then_inc(std2_ready, 1)

                def turn_h(t0, it):
                    act.wait_ge(h_turned, t0 + 1 + 2 * it)
                    if inner(t0, 2, it):
                        act.wait_ge(lg_ready, t0 - 1 + 2 * it)
                    nc.scalar.activation(h_t[:, t0 % 2, :, :], tr_ps[:, t0 % 2, :].rearrange("p (a t) -> p a t", a=DT),
                                         ACT.Copy).then_inc(ht_ready, 1)

                pairs(act, turn_h, NTILE)
                act.wait_ge(gap_ready, 1)
                nc.scalar.activation(small[:, 3, :], small[:, 2, :], ACT.Exp).then_inc(egap_ready, 1)

                def turn_in(k0, it):
                    act.wait_ge(in_turned, k0 + 1 + 2 * it)
                    if inner(k0, 2, it):
                        act.wait_ge(gu_ready, k0 - 1 + 2 * it)
                    else:
                        act.wait_ge(lg_ready, NTILE)
                    nc.scalar.activation(h_t[:, k0 % 2, :, :], tr_ps[:, k0 % 2, :].rearrange("p (a t) -> p a t", a=DT),
                                         ACT.Copy).then_inc(inT_ready, 1)

                def y_copy(k0, it):
                    act.wait_ge(dn_ready, k0 + 1 + 2 * it)
                    if inner(k0, 2, it):
                        act.wait_ge(y_stored[k0 % 2], 16 * (k0 // 2) + 16 * it)
                    nc.scalar.activation(y_sb[:, k0 % 2, :], y_ps[:, k0 % 2, :], ACT.Copy).then_inc(y_copied, 1)

                turn_in(0, 0)

                def step(k0, it):
                    act.wait_ge(gu_ready, k0 + 1 + 2 * it)
                    if k0 >= 1:
                        act.wait_ge(act_ready, k0 + 2 * it)
                    nc.scalar.activation(sig_g[:, :], gu_ps[:, 0:F], ACT.Silu).then_inc(silu_done, 1)
                    if k0 + 1 < BLOCKS:
                        turn_in(k0 + 1, it)
                    if k0 >= 1:
                        y_copy(k0 - 1, it)

                pairs(act, step, BLOCKS)
                y_copy(BLOCKS - 1, 0)

            @block.tensor
            def _(pe):
                def logits(t0, it):
                    pe.wait_ge(ht_ready, t0 + 1 + 2 * it)
                    for a in range(DT):
                        mm = nc.tensor.matmul(lg_ps[:, bass.ds(t0 + 2 * it, 1), :], h_t[:, t0 % 2, a, :], w_rt[:, a, :],
                                              start=(a == 0), stop=(a == DT - 1))
                    mm.then_inc(lg_ready, 1)

                def turn_h(t0, it):
                    pe.wait_ge(h_ready, t0 + 1 + 2 * it)
                    if inner(t0, 2, it):
                        pe.wait_ge(ht_ready, t0 - 1 + 2 * it)
                    for a in range(DT):
                        mm = nc.tensor.transpose(tr_ps[:, t0 % 2, a * P:(a + 1) * P], h_ring[:, t0 % 2, a * P:(a + 1) * P],
                                                 ident[:, :])
                    mm.then_inc(h_turned, 1)
                    if t0 >= 1:
                        logits(t0 - 1, it)

                pe.wait_ge(wrt_loaded, 16)
                pairs(pe, turn_h, NTILE)
                logits(NTILE - 1, 0)
                pe.wait_ge(chosen_ready, 1)
                pe.wait_ge(const_ready, 3)
                nc.tensor.matmul(cnt_ps[:, 0, :, :], before[:, :], chosen[:, :, :], start=True, stop=True)
                nc.tensor.matmul(cnt_ps[:, 1, :, :], ones_bf[:, :], chosen[:, :, :], start=True, stop=True,
                                 ).then_inc(cnt_ready, 1)

                def turn_in(k0, it):
                    pe.wait_ge(in_loaded[k0 % 2], 16 * (k0 // 2 + 1) + 16 * it)
                    if inner(k0, 2, it):
                        pe.wait_ge(inT_ready, k0 - 1 + 2 * it)
                    for a in range(DT):
                        mm = nc.tensor.transpose(tr_ps[:, k0 % 2, a * P:(a + 1) * P], h_in[:, k0 % 2, a * P:(a + 1) * P],
                                                 ident[:, :])
                    mm.then_inc(in_turned, 1)

                def down(k0, expert, it):
                    pe.wait_ge(actT_ready, k0 + 1 + 2 * it)
                    if inner(k0, 2, it):
                        pe.wait_ge(y_copied, k0 - 1 + 2 * it)
                    for a in range(FT):
                        mm = nc.tensor.matmul(y_ps[:, k0 % 2, :], act_t[:, a, :], w_dn[:, bass.ds(expert, 1), a, :],
                                              start=(a == 0), stop=(a == FT - 1))
                    mm.then_inc(dn_ready, 1)

                def turn_act(k0, it):
                    pe.wait_ge(act_ready, k0 + 1 + 2 * it)
                    if k0 >= 1:
                        pe.wait_ge(actT_ready, k0 + 2 * it)
                    for a in range(FT):
                        mm = nc.tensor.transpose(at_ps[:, a, :], act_gu[:, a * P:(a + 1) * P], ident[:, :])
                    mm.then_inc(act_turned, 1)

                def expert_of(k0, it):
                    return pe.value_load(blk_i[0:1, bass.ds(k0 + 2 * it, 1)], min_val=0, max_val=E)

                pe.wait_ge(blocks_ready, 1)
                pe.wait_ge(wgu_loaded, 16 * 2 * (E + 1))
                pe.wait_ge(wdn_loaded, 16 * (E + 1))
                turn_in(0, 0)

                def step(k0, it):
                    expert = expert_of(k0, it)
                    if k0 >= 1:
                        turn_act(k0 - 1, it)
                    pe.wait_ge(inT_ready, k0 + 1 + 2 * it)
                    for a in range(DT):
                        mm = nc.tensor.matmul(gu_ps[:, :], h_t[:, k0 % 2, a, :], w_gu[:, bass.ds(expert, 1), a, :],
                                              start=(a == 0), stop=(a == DT - 1))
                    mm.then_inc(gu_ready, 1)
                    if k0 + 1 < BLOCKS:
                        turn_in(k0 + 1, it)
                    if k0 >= 1:
                        down(k0 - 1, expert_of(k0 - 1, it), it)

                pairs(pe, step, BLOCKS)
                turn_act(BLOCKS - 1, 0)
                down(BLOCKS - 1, expert_of(BLOCKS - 1, 0), 0)

            @block.vector
            def _(dve):
                def chained(ins):
                    count["step"] += 1
                    ins.then_inc(dve_step, 1)
                    dve.wait_ge(dve_step, count["step"])

                def rsqrt(dst, var, i):
                    dve.wait_ge(std2_ready, i + 1)
                    chained(nc.vector.reciprocal(rs_b[:, :], rs_b[:, :]))
                    chained(nc.vector.tensor_tensor(rs_a[:, :], rs_a[:, :], rs_b[:, :], ALU.mult))
                    chained(nc.vector.tensor_tensor(rs_a[:, :], rs_a[:, :], rs_b[:, :], ALU.mult))
                    chained(nc.vector.tensor_scalar(rs_a[:, :], rs_a[:, :], -0.5, 1.5, ALU.mult, ALU.add))
                    chained(nc.vector.tensor_tensor(dst, rs_a[:, :], rs_b[:, :], ALU.mult))

                V = nc.vector
                for t in range(NTILE):
                    last = V.bn_stats(stats[:, t, :], x_sb[:, t, :])
                chained(last)
                for t in range(NTILE):
                    last = V.bn_aggr(mv[:, t, :], stats[:, t, :])
                chained(last)
                V.tensor_scalar(rs_a[:, :], mv[:, :, 1], LN_EPS, None, ALU.add).then_inc(var2_ready, 1)
                rsqrt(rstd[:, :], None, 0)
                chained(V.tensor_tensor(rs_a[:, :], mv[:, :, 1], rstd[:, :], ALU.mult))
                chained(V.tensor_tensor(rs_a[:, :], rs_a[:, :], rstd[:, :], ALU.mult))
                V.tensor_scalar(rs_a[:, :], rs_a[:, :], RMS_EPS, None, ALU.add).then_inc(var2_ready, 1)
                rsqrt(small[:, 0, :], None, 1)
                chained(V.tensor_tensor(rstd[:, :], rstd[:, :], small[:, 0, :], ALU.mult))
                dve.wait_ge(rms_loaded, 16)

                def make_h(t0, it):
                    if inner(t0, 2, it):
                        dve.wait_ge(h_turned, t0 - 1 + 2 * it)
                        dve.wait_ge(h_kept, t0 - 1 + 2 * it)
                        dve.wait_ge(h_stored[t0 % 2], 16 * (t0 // 2) + 16 * it)
                    t = t0 + 2 * it
                    V.tensor_scalar(h_ring[:, t0 % 2, :], x_sb[:, t, :], mv[:, t, 0:1], rstd[:, bass.ds(t, 1)],
                                    ALU.subtract, ALU.mult).then_inc(h_part, 1)
                    dve.wait_ge(h_part, t0 + 1 + 2 * it)
                    V.tensor_tensor(h_ring[:, t0 % 2, :], h_ring[:, t0 % 2, :], rms_bc[:, :], ALU.mult).then_inc(h_ready, 1)

                pairs(dve, make_h, NTILE)

                dve.wait_ge(const_ready, 3)
                chained(V.tensor_copy(iota[:, :], iota_i[:, :]))
                chained(V.tensor_scalar(rank[:, :], iota[:, 0:E], -1.0, float(E), ALU.mult, ALU.add))

                def by_expert(ap):
                    return ap.rearrange("p (t o) -> p t o", o=1).broadcast_to([P, NTILE, E])

                def by_tile(ap):
                    return ap.rearrange("p (o e) -> p o e", o=1).broadcast_to([P, NTILE, E])

                def pick(dst, logit, top):
                    chained(V.tensor_reduce(top, logit, AX_X, ALU.max))
                    chained(V.tensor_tensor(dst, logit, by_expert(top), ALU.is_equal))
                    chained(V.tensor_tensor(dst, dst, by_tile(rank[:, :]), ALU.mult))
                    chained(V.tensor_reduce(small[:, 4, :], dst, AX_X, ALU.max))
                    chained(V.tensor_tensor(dst, dst, by_expert(small[:, 4, :]), ALU.is_equal))

                LG, M1, M2, LG2, TOT, PA, PB, POS = (rt[:, i, :, :] for i in range(8))
                dve.wait_ge(lg_ready, NTILE)
                chained(V.tensor_copy(LG, lg_ps[:, :, :]))
                pick(M1, LG, small[:, 0, :])
                chained(V.scalar_tensor_tensor(out=LG2, in0=M1, scalar=-3.0e38, in1=LG, op0=ALU.mult, op1=ALU.add))
                pick(M2, LG2, small[:, 1, :])
                chained(V.tensor_tensor(small[:, 2, :], small[:, 1, :], small[:, 0, :], ALU.subtract))
                V.tensor_tensor(chosen[:, :, :], M1, M2, ALU.add).then_inc(chosen_ready, 1)
                V.tensor_copy(small[:, 5, :], small[:, 2, :]).then_inc(gap_ready, 1)
                dve.wait_ge(egap_ready, 1)
                chained(V.tensor_scalar(small[:, 4, :], small[:, 3, :], 1.0, None, ALU.add))
                chained(V.reciprocal(small[:, 6, :], small[:, 4, :]))
                chained(V.tensor_tensor(small[:, 7, :], small[:, 3, :], small[:, 6, :], ALU.mult))
                dve.wait_ge(cnt_ready, 1)
                chained(V.tensor_copy(TOT, cnt_ps[:, 1, :, :]))
                src, dst = TOT, PA
                for s in (1, 2, 4, 8):
                    V.tensor_copy(dst[:, 0:s, :], src[:, 0:s, :])
                    chained(V.tensor_tensor(dst[:, s:NTILE, :], src[:, s:NTILE, :], src[:, 0:NTILE - s, :], ALU.add))
                    src, dst = dst, (PB if dst is PA else PA)
                run = src
                total = run[:, NTILE - 1, :]
                chained(V.tensor_scalar(blk_e[:, 0:NTILE], iota[:, 0:NTILE], float(P), None, ALU.mult))
                chained(V.tensor_tensor(blk[:, 0:NTILE, :],
                                        total.rearrange("p (o e) -> p o e", o=1).broadcast_to([P, NTILE, E]),
                                        blk_e[:, 0:NTILE].rearrange("p (t o) -> p t o", o=1).broadcast_to([P, NTILE, E]),
                                        ALU.is_gt))
                nb, na, spare = blk[:, 45, :], blk[:, 46, :], blk[:, 47, :]
                chained(V.tensor_reduce(nb, blk[:, 0:NTILE, :].rearrange("p t e -> p e t"), AX_X, ALU.add))
                src, dst = nb, na
                for s in (1, 2, 4):
                    V.tensor_copy(dst[:, 0:s], src[:, 0:s])
                    chained(V.tensor_tensor(dst[:, s:E], src[:, s:E], src[:, 0:E - s], ALU.add))
                    src, dst = dst, (spare if dst is na else na)
                ends, first = src, dst
                KB = EXPERT_BLOCKS
                chained(V.tensor_tensor(blk[:, 0:KB, 0:E - 1],
                                        iota[:, 0:KB].rearrange("p (t o) -> p t o", o=1).broadcast_to([P, KB, E - 1]),
                                        ends[:, 0:E - 1].rearrange("p (o e) -> p o e", o=1).broadcast_to([P, KB, E - 1]),
                                        ALU.is_ge))
                chained(V.memset(blk_e[:, 0:NTILE], float(E)))
                chained(V.tensor_reduce(blk_e[:, NTILE:BLOCKS], blk[:, 0:KB, 0:E - 1], AX_X, ALU.add))
                V.tensor_copy(blk_i[:, 0:BLOCKS], blk_e[:, 0:BLOCKS]).then_inc(blocks_ready, 1)
                chained(V.tensor_tensor(first, ends, nb, ALU.subtract))
                chained(V.tensor_scalar(first, first, float(NTILE), float(P), ALU.add, ALU.mult))
                chained(V.tensor_tensor(POS, run, TOT, ALU.subtract))
                chained(V.tensor_tensor(POS, POS, by_tile(first), ALU.add))
                chained(V.tensor_tensor(POS, POS, cnt_ps[:, 0, :, :], ALU.add))
                for c, m in enumerate((M1, M2)):
                    chained(V.tensor_tensor(LG, m, POS, ALU.mult))
                    chained(V.tensor_reduce(small[:, 8 + c, :], LG, AX_X, ALU.add))
                V.tensor_copy(slot_i[:, :, :], small[:, 8:10, :]).then_inc(slots_ready, 1)

                def turn_copy(k0, it):
                    dve.wait_ge(act_turned, k0 + 1 + 2 * it)
                    if k0 >= 1:
                        dve.wait_ge(dn_ready, k0 + 2 * it)
                    V.tensor_copy(act_t[:, :, :], at_ps[:, :, :]).then_inc(actT_ready, 1)

                def step(k0, it):
                    if k0 >= 1:
                        turn_copy(k0 - 1, it)
                    dve.wait_ge(silu_done, k0 + 1 + 2 * it)
                    if k0 >= 1:
                        dve.wait_ge(act_turned, k0 + 2 * it)
                    V.tensor_tensor(act_gu[:, :], sig_g[:, :], gu_ps[:, F:2 * F], ALU.mult).then_inc(act_ready, 1)

                pairs(dve, step, BLOCKS)
                turn_copy(BLOCKS - 1, 0)

                for t in range(NTILE):
                    dve.wait_ge(sh_loaded[t % 2], 16 * (t // 2 + 1))
                    chained(V.tensor_tensor(x_sb[:, t, :], x_sb[:, t, :], h_in[:, t % 2, :], ALU.add))
                    dve.wait_ge(got[0][t % 4], 16 * (t // 4 + 1))
                    chained(V.scalar_tensor_tensor(out=x_sb[:, t, :], in0=h_all[:, 2 * (t % 4), :], scalar=small[:, 6, t:t + 1],
                                                   in1=x_sb[:, t, :], op0=ALU.mult, op1=ALU.add))
                    dve.wait_ge(got[1][t % 4], 16 * (t // 4 + 1))
                    V.scalar_tensor_tensor(out=x_sb[:, t, :], in0=h_all[:, 2 * (t % 4) + 1, :], scalar=small[:, 7, t:t + 1],
                                           in1=x_sb[:, t, :], op0=ALU.mult, op1=ALU.add).then_inc(mixed, 1)

        token_ctx.close()


_INS = [n for n in (
    'x', 'ctx_2048', 'L0_xattn_Wq', 'L0_xattn_bq', 'L0_xattn_Wk', 'L0_xattn_bk', 'L0_xattn_Wv', 'L0_xattn_bv',
    'L0_xattn_Wo', 'L0_xattn_bo', 'L0_ffn_rms_weight', 'L0_ffn_router_w', 'L0_ffn_w_gate', 'L0_ffn_w_up',
    'L0_ffn_w_down', 'L0_ffn_sw_gate', 'L0_ffn_sw_up', 'L0_ffn_sw_down')]


def kernel(**inputs):
    import numpy as np
    import concourse.bacc as bacc
    from concourse.bass_utils import run_bass_kernel_spmd

    nc = bacc.Bacc("TRN2", target_bir_lowering=False, num_devices=1)
    arrays, args = {}, []
    for name in _INS:
        a = np.ascontiguousarray(inputs[name])
        arrays[f"in_{name}"] = a
        args.append(nc.dram_tensor(f"in_{name}", a.shape, mybir.dt.from_np(a.dtype), kind="ExternalInput").ap())
    args.append(nc.dram_tensor("out_0", (B, C, T), F32, kind="ExternalOutput").ap())
    xattn_ffn_kernel(nc, *args)
    r = run_bass_kernel_spmd(nc, [arrays], core_ids=[0])
    return r.results[0]["out_0"]
```

```python
from contextlib import ExitStack

import concourse.bass as bass
from concourse import mybir

ALU = mybir.AluOpType
ACT = mybir.ActivationFunctionType
BF16 = mybir.dt.bfloat16
F32 = mybir.dt.float32
I32 = mybir.dt.int32
AX_X = mybir.AxisListType.X

P = 128
B, C, T = 8, 256, 512
HEADS, KCH = 16, 16
SCALE = float(KCH) ** -0.5
HALVES = 2 * B
HH = 8
CT = C // P
TT = T // P
GH = 4
UNITS = HH * TT
STEPS = UNITS // GH
LEAD = 14
MAXBUF = 4
PARTS = 3
Q_PART = (0, 0, 0, 1, 1, 2)
K_PART = (0, 1, 2, 0, 1, 0)
SROWS = KCH * len(Q_PART)
NBUF = 4
LN_EPS, RMS_EPS = 1e-5, 1e-6
E, F, D = 8, 256, T
FT, DT = F // P, D // P
NTILE = B * C // P
TOPK = 2
EXPERT_BLOCKS = NTILE * TOPK + E - 1
BLOCKS = NTILE + EXPERT_BLOCKS


def xattn_ffn_kernel(nc, x, ctxt, wq, bq, wk, bk, wv, bv, wo, bo, rms_w, router_w, w_gate, w_up, w_down,
                     sw_gate, sw_up, sw_down, out):
    x_t = x.rearrange("b (o p) t -> b p o t", p=P)
    c_t = ctxt.rearrange("b (o p) t -> b p o t", p=P)
    parts_dram = nc.dram_tensor("parts_dram", [NBUF, 2, PARTS, P, T], BF16, kind="Internal").ap()
    den_dram = nc.dram_tensor("den_dram", [HH, T], F32, kind="Internal").ap()
    rec_dram = nc.dram_tensor("rec_dram", [HH, T], F32, kind="Internal").ap()
    num_dram = nc.dram_tensor("num_dram", [HH // GH, GH, KCH, T], F32, kind="Internal").ap()
    blocks_in = nc.dram_tensor("blocks_in", [BLOCKS, P, D], F32, kind="Internal").ap()
    blocks_out = nc.dram_tensor("blocks_out", [BLOCKS, P, D], F32, kind="Internal").ap()
    rows_in = blocks_in.rearrange("k p d -> (k p) d")
    rows_out = blocks_out.rearrange("k p d -> (k p) d")
    out_t = out.rearrange("b (o p) t -> (b o) p t", p=P)
    rows_dram = nc.dram_tensor("rows_dram", [NBUF, PARTS, HH * TT, P], BF16, kind="Internal").ap()

    with ExitStack() as outer:
        def sem(name):
            return outer.enter_context(nc.semaphore(name))

        def sb(name, shape, dt=F32, stack=outer):
            return stack.enter_context(nc.sbuf_tensor(name, shape, dt))

        x_sb = sb("x_sb", [P, B * CT, T])
        ident = sb("ident", [P, P])
        zeros = sb("zeros", [P, D])
        stats = sb("stats", [P, B * CT, 6])
        mv = sb("mv", [P, B * CT, 2])
        rstd = sb("rstd", [P, B * CT])
        rs_a = sb("rs_a", [P, B * CT])
        rs_b = sb("rs_b", [P, B * CT])

        attn_ctx = ExitStack()

        def asb(name, shape, dt=F32):
            return sb(name, shape, dt, attn_ctx)

        def aps(name, shape, dt=F32):
            return attn_ctx.enter_context(nc.psum_tensor(name, shape, dt))

        q_stack = [asb(f"q_stack{i}", [P, HH, T], BF16) for i in range(NBUF)]
        k_stack = [asb(f"k_stack{i}", [P, HH, T], BF16) for i in range(NBUF)]
        v_t = [asb(f"v_t{i}", [P, TT, HH, 32]) for i in range(NBUF)]
        probs = asb("probs", [P, 2, 4, T])
        pv_raw = asb("pv_raw", [P, 2, HH // GH, T])
        attn = asb("attn", [P, 2, CT, T])
        c_sb = asb("c_sb", [P, 2, CT, T])
        xn = asb("xn", [P, CT, T])
        qk32 = asb("qk32", [P, 2, T])
        rest = asb("rest", [P, 2, T])
        parts = asb("parts", [P, 2, PARTS, T], BF16)
        recip = asb("recip", [P, T])
        den = asb("den", [P, HH * T // P])
        negmax = asb("negmax", [P, 2, HH * TT])
        nm32 = asb("nm32", [HH * TT, P])
        nm_rest = asb("nm_rest", [HH * TT, P])
        nm_parts = asb("nm_parts", [HH * TT, PARTS, P], BF16)
        w_raw = asb("w_raw", [P, 4, CT, C])
        w_t = asb("w_t", [P, 4, CT, C])
        bqk = asb("bqk", [P, 2, CT])
        bo_col = asb("bo_col", [P, CT])
        bo_all = asb("bo_all", [P, CT])
        bv_col = asb("bv_col", [P, CT])

        smax_ps = aps("smax_ps", [P, MAXBUF, T])
        st_ps = aps("st_ps", [P, 2, T])
        pv_ps = aps("pv_ps", [P, T])
        proj_ps = aps("proj_ps", [P, T])

        ident_ready = sem("ident_ready")
        ones_ready = sem("ones_ready")
        w_loaded = sem("w_loaded")
        b_loaded = sem("b_loaded")
        c_loaded = [sem(f"c_loaded{i}") for i in range(2)]
        x0_loaded = sem("x0_loaded")
        xr_loaded = sem("xr_loaded")
        wt_ready = sem("wt_ready")
        wt_copied = sem("wt_copied")
        bo_ready = sem("bo_ready")
        var_ready = sem("var_ready")
        std_ready = sem("std_ready")
        rstd_ready = sem("rstd_ready")
        dve_step = sem("dve_step")
        xn_ready = sem("xn_ready")
        qk_ready = sem("qk_ready")
        qk32_ready = sem("qk32_ready")
        high_ready = sem("high_ready")
        mid_rest_ready = sem("mid_rest_ready")
        mid_ready = sem("mid_ready")
        low_ready = sem("low_ready")
        parts_written = [sem(f"parts_written{i}") for i in range(2)]
        stack_loaded = [sem(f"stack_loaded{i}") for i in range(NBUF)]
        v_ready = sem("v_ready")
        vt_copied = sem("vt_copied")
        s_ready = sem("s_ready")
        max_done = sem("max_done")
        nm_turned = sem("nm_turned")
        nm_copied = sem("nm_copied")
        nm_step = sem("nm_step")
        nm_parts_ready = sem("nm_parts_ready")
        rows_written = sem("rows_written")
        rows_loaded = [sem(f"rows_loaded{i}") for i in range(NBUF)]
        st_ready = sem("st_ready")
        exp_done = sem("exp_done")
        pv_done = sem("pv_done")
        pv_copied = sem("pv_copied")
        zeros_ready = sem("zeros_ready")
        zeroed = sem("zeroed")
        den_written = sem("den_written")
        den_loaded = sem("den_loaded")
        den_inverted = sem("den_inverted")
        rec_written = sem("rec_written")
        rec_loaded = sem("rec_loaded")
        num_written = sem("num_written")
        num_loaded = sem("num_loaded")
        attn_ready = sem("attn_ready")
        y_ready = sem("y_ready")
        x1_ready = sem("x1_ready")

        OUT_UNITS = (24, 25, 28, 30)
        LOOP_SLOTS = 4
        LOOPS = 3

        sp_wait_reg = [nc.sync.alloc_register(f"sp_wait{i}") for i in range(2)]

        def sync_wait(sp, *waits):
            for (_, value), reg in zip(waits, sp_wait_reg):
                if not isinstance(value, int):
                    sp.reg_mov(reg, value)
            for (sem, value), reg in zip(waits, sp_wait_reg):
                if isinstance(value, int):
                    sp.wait_ge(sem, value)
                else:
                    sp.wait_ge(zeros_ready, 1)
                    sp.wait_ge(sem, reg)

        def slots(eng, slot, tail, own=None):
            slot(0, 0, False)
            with eng.Fori(0, LOOPS) as it:
                for s0 in range(1, 1 + LOOP_SLOTS):
                    if own is None:
                        slot(s0, it, True)
                        continue
                    eng.reg_mov(own[s0 % 2], it)
                    slot(s0, eng.snap(own[s0 % 2], min_val=0, max_val=LOOPS - 1), True)
            for s in range(1 + LOOP_SLOTS * LOOPS, HALVES):
                slot(s, 0, False)
            tail(HALVES, 0, False)

        def at(per_slot, first, it):
            return first + per_slot * LOOP_SLOTS * it

        X1_START = 2
        count = {"step": 0}

        with nc.Block() as block:

            @block.sync
            def _(sp):
                sp.dma_start(x_sb[:, 0:CT, :], x_t[0]).then_inc(x0_loaded, 16)
                for i, w in enumerate((wk, wq, wv, wo)):
                    sp.dma_start(w_raw[:, i, :, :], w.rearrange("(o p) c -> p o c", p=P)).then_inc(w_loaded, 16)
                sp.dma_start(c_sb[:, 0, :, :], c_t[0]).then_inc(c_loaded[0], 16)
                for i, bias in enumerate((bk, bq)):
                    for o in range(CT):
                        sp.dma_start(bqk[:, i, o:o + 1],
                                     bias[P * o:P * (o + 1)].rearrange("(h k o) -> k h o", k=KCH, o=1),
                                     allow_slow_non_contiguous=True).then_inc(b_loaded, 16)
                sp.dma_start(bo_col[:, :], bo.rearrange("(o p) -> p o", p=P),
                             allow_slow_non_contiguous=True).then_inc(b_loaded, 16)
                sp.dma_start(bv_col[:, :], bv.rearrange("(o p) -> p o", p=P),
                             allow_slow_non_contiguous=True).then_inc(b_loaded, 16)
                for b in range(1, B):
                    sp.dma_start(x_sb[:, CT * b:CT * b + CT, :], x_t[b]).then_inc(xr_loaded, 16)

                def stack(n0, it):
                    for i in range(2):
                        waits = [(low_ready, at(2, 2 * n0 + i + 1, it))]
                        if i == 0 and not (isinstance(it, int) and n0 < NBUF):
                            waits.insert(0, (st_ready, at(UNITS, UNITS * (n0 - NBUF + 1), it)))
                        sync_wait(sp, *waits)
                        sp.dma_start(parts_dram[n0 % NBUF, i].rearrange("s p t -> p s t"),
                                     parts[:, i, :, :]).then_inc(parts_written[i], 16)
                    for i, dst in enumerate((k_stack, q_stack)):
                        sync_wait(sp, (parts_written[i], at(16, 16 * (n0 + 1), it)))
                        for part in range(PARTS):
                            g, count = (0, 3, 5)[part], PARTS - part
                            by_channel = parts_dram[n0 % NBUF, i].rearrange("s (i h) t -> s i (h t)", h=HH)
                            src = (by_channel[part:part + 1].broadcast_to([count, KCH, HH * T]) if i == 1
                                   else by_channel[0:count].rearrange("s i f -> (s i) f"))
                            sp.dma_start(dst[n0 % NBUF][KCH * g:KCH * (g + count), :, :].rearrange("p h t -> p (h t)"), src
                                         ).then_inc(stack_loaded[n0 % NBUF], 16)

                def rows(n0, it):
                    sync_wait(sp, (nm_parts_ready, at(1, n0 + 1, it)))
                    sp.dma_start(rows_dram[n0 % NBUF].rearrange("s r t -> r s t"),
                                 nm_parts[:, :, :]).then_inc(rows_written, 16)
                    sync_wait(sp, (rows_written, at(16, 16 * (n0 + 1), it)))
                    sp.dma_start(q_stack[n0 % NBUF][SROWS:SROWS + PARTS, :, :],
                                 rows_dram[n0 % NBUF].rearrange("s (h j) t -> s h (j t)", h=HH)
                                 ).then_inc(rows_loaded[n0 % NBUF], 16)

                def denominators(n0, it):
                    sync_wait(sp, (pv_copied, at(2, 2 * n0 + 2, it)))
                    sp.dma_start(den_dram.rearrange("(g j) t -> j g t", j=GH), pv_raw[KCH:P:32, n0 % 2, :, :]).then_inc(den_written, 16)
                    for j in range(GH):
                        sp.dma_start(num_dram[:, j].rearrange("g k t -> k g t"),
                                     pv_raw[32 * j:32 * j + KCH, n0 % 2, :, :]).then_inc(num_written, 16)
                    sync_wait(sp, (den_written, at(16, 16 * (n0 + 1), it)))
                    sp.dma_start(den[:, :], den_dram.rearrange("h (q r) -> (h q) r", r=HH * T // P)
                                 ).then_inc(den_loaded, 16)
                    waits = [(num_written, at(16 * GH, 16 * GH * (n0 + 1), it))]
                    if not (isinstance(it, int) and n0 < 4):
                        waits.append((nm_turned, at(1, n0 // 2 * 2, it)))
                    sync_wait(sp, *waits)
                    sp.dma_start(attn[:, n0 // 2 % 2, n0 % 2, :],
                                 num_dram.rearrange("g j k t -> (g j k) t")).then_inc(num_loaded, 16)
                    waits = [(den_inverted, at(1, n0 + 1, it))]
                    if not (isinstance(it, int) and n0 == 0):
                        waits.append((attn_ready, at(1, n0, it)))
                    sync_wait(sp, *waits)
                    sp.dma_start(rec_dram.rearrange("h (q r) -> (h q) r", r=HH * T // P), den[:, :]
                                 ).then_inc(rec_written, 16)
                    sync_wait(sp, (rec_written, at(16, 16 * (n0 + 1), it)))
                    sp.dma_start(recip[:, :], rec_dram.rearrange("h (o t) -> h o t", o=1).broadcast_to([HH, KCH, T])
                                 ).then_inc(rec_loaded, 16)

                def load_c(n0, it):
                    b0 = n0 // 2
                    src = c_t[b0 + 2 * it]
                    sync_wait(sp, (v_ready, at(1, n0 - 2, it)))
                    sp.dma_start(c_sb[:, b0 % 2, :, :], src).then_inc(c_loaded[b0 % 2], 16)

                sp.dma_start(c_sb[:, 1, :, :], c_t[1]).then_inc(c_loaded[1], 16)
                stack(0, 0)
                stack(1, 0)
                stack(2, 0)
                rows(0, 0)

                def clear_blocks(s0, it):
                    if s0 == 1:
                        sync_wait(sp, (zeros_ready, 1))
                    for k in range(3):
                        sp.dma_start(blocks_in[NTILE + 3 * (s0 - 1) + k + 3 * LOOP_SLOTS * it], zeros[:, :]
                                     ).then_inc(zeroed, 16)

                def slot(s0, it, loop):
                    if s0 % 2 == 1 and (loop or s0 + 3 < HALVES):
                        load_c(s0 + 3, it)
                    if loop or s0 > 0:
                        denominators(s0 - 1, it)
                    if loop or 0 < s0 <= EXPERT_BLOCKS // 3:
                        clear_blocks(s0, it)
                    if loop or s0 + 3 < HALVES:
                        stack(s0 + 3, it)
                    if loop or s0 + 1 < HALVES:
                        rows(s0 + 1, it)

                slots(sp, slot, lambda s0, it, loop: denominators(s0 - 1, it))
                sync_wait(sp, (zeroed, 16 * EXPERT_BLOCKS))

            @block.gpsimd
            def _(pool):
                nc.gpsimd.memset(ident[:, :], 0.0).then_inc(ident_ready, 1)
                pool.wait_ge(ident_ready, 1)
                nc.gpsimd.affine_select(out=ident[:, :], in_=ident[:, :], compare_op=ALU.not_equal, fill=1.0,
                                        base=0, pattern=[[-1, P]], channel_multiplier=1).then_inc(ident_ready, 1)
                pool.wait_ge(ident_ready, 2)
                for i in range(NBUF):
                    nc.gpsimd.memset(k_stack[i][SROWS:SROWS + PARTS, :, :], 1.0).then_inc(ones_ready, 1)
                    pool.wait_ge(ones_ready, 2 * i + 1)
                    nc.gpsimd.memset(v_t[i][:, :, :, KCH:32], 1.0).then_inc(ones_ready, 1)
                    pool.wait_ge(ones_ready, 2 * i + 2)

                def split(n0, it):
                    for i in range(2):
                        pool.wait_ge(high_ready, at(2, 2 * n0 + i + 1, it))
                        nc.gpsimd.tensor_tensor(rest[:, i, :], qk32[:, i, :], parts[:, i, 0, :],
                                                ALU.subtract).then_inc(mid_rest_ready, 1)
                        pool.wait_ge(mid_ready, at(2, 2 * n0 + i + 1, it))
                        nc.gpsimd.tensor_tensor(parts[:, i, 2, :], rest[:, i, :], parts[:, i, 1, :],
                                                ALU.subtract).then_inc(low_ready, 1)

                split(0, 0)
                split(1, 0)
                split(2, 0)

                def slot(s0, it, loop):
                    if loop or s0 + 3 < HALVES:
                        split(s0 + 3, it)

                slots(pool, slot, lambda *a: None)

            @block.scalar
            def _(act):
                def std(lo, hi, i):
                    act.wait_ge(var_ready, i + 1)
                    nc.scalar.activation(rs_b[:, lo:hi], rs_a[:, lo:hi], ACT.Sqrt).then_inc(std_ready, 1)

                def qk_bias(n0, i, it):
                    act.wait_ge(qk_ready, at(2, 2 * n0 + i + 1, it))
                    if not (isinstance(it, int) and n0 == 0):
                        act.wait_ge(mid_rest_ready, at(2, 2 * n0 + i - 1, it))
                    nc.scalar.activation(qk32[:, i, :], proj_ps[:, :], ACT.Identity,
                                         bias=bqk[:, i, n0 % 2:n0 % 2 + 1]).then_inc(qk32_ready, 1)

                def v_copy(n0, it):
                    act.wait_ge(v_ready, at(1, n0 + 1, it))
                    if not (isinstance(it, int) and n0 < NBUF):
                        act.wait_ge(pv_done, at(STEPS, STEPS * (n0 - NBUF + 1), it))
                    nc.scalar.activation(v_t[n0 % NBUF][:, :, :, 0:KCH],
                                         proj_ps[:, :].rearrange("p (s h k) -> p s h k", s=TT, k=KCH),
                                         ACT.Copy).then_inc(vt_copied, 1)

                std(0, CT, 0)
                act.wait_ge(b_loaded, 16 * 6)
                for n in range(3):
                    qk_bias(n, 0, 0)
                    qk_bias(n, 1, 0)
                    v_copy(n, 0)
                    if n == 0:
                        std(CT, B * CT, 1)

                def pv_copy(g0, it):
                    act.wait_ge(pv_done, at(STEPS, STEPS // 2 * (g0 + 1), it))
                    if g0 % 2 == 0 and (not isinstance(it, int) or g0 >= 4):
                        act.wait_ge(den_written, at(16, 16 * (g0 // 2 - 1), it))
                        act.wait_ge(num_written, at(16 * GH, 16 * GH * (g0 // 2 - 1), it))
                    nc.scalar.activation(pv_raw[:, g0 // 2 % 2, g0 % 2, :], pv_ps[:, :], ACT.Copy).then_inc(pv_copied, 1)

                def slot(s0, it, loop):
                    proj = loop or s0 + 3 < HALVES
                    for u in range(UNITS):
                        act.wait_ge(st_ready, at(UNITS, UNITS * s0 + u + 1, it))
                        k0 = STEPS * s0 + u // GH
                        if u % GH == 0 and (loop or k0 >= 2):
                            act.wait_ge(pv_done, at(STEPS, k0 - 1, it))
                        nc.scalar.activation(probs[:, k0 % 2, u % GH, :], st_ps[:, u % 2, :],
                                             ACT.Exp, scale=SCALE).then_inc(exp_done, 1)
                        if u == 2 and (loop or s0 > 0):
                            pv_copy(2 * s0 - 1, it)
                        if u == 18:
                            pv_copy(2 * s0, it)
                        if proj and u in (3, 9):
                            qk_bias(s0 + 3, u // 9, it)
                        if proj and u == 16:
                            v_copy(s0 + 3, it)

                slots(act, slot, lambda s0, it, loop: pv_copy(2 * s0 - 1, it))

            @block.tensor
            def _(pe):
                pe.wait_ge(ident_ready, 2)
                pe.wait_ge(w_loaded, 16 * 4)
                for i in range(4):
                    for o in range(CT):
                        for kt in range(CT):
                            mm = nc.tensor.transpose(smax_ps[:, i, kt * C + o * P:kt * C + (o + 1) * P],
                                                     w_raw[:, i, o, kt * P:(kt + 1) * P], ident[:, :])
                    mm.then_inc(wt_ready, 1)
                pe.wait_ge(wt_copied, 4)
                pe.wait_ge(b_loaded, 16 * 6)
                for o in range(CT):
                    for kt in range(CT):
                        mm = nc.tensor.matmul(pv_ps[:, o:o + 1], w_t[:, 3, kt, o * P:(o + 1) * P], bv_col[:, kt:kt + 1],
                                              start=(kt == 0), stop=(kt == CT - 1))
                mm.then_inc(bo_ready, 1)

                def project_qk(n0, i, kt, it):
                    if kt == 0 and i == 0:
                        pe.wait_ge(c_loaded[(n0 // 2) % 2], 16 * (n0 // 4 + 1) + 16 * it)
                        if n0 >= 4 and n0 % 2 == 0:
                            pe.wait_ge(x1_ready, at(1, X1_START + n0 - 4, it))
                        elif n0 >= 3:
                            pe.wait_ge(nm_copied, at(1, n0 - 2, it))
                        elif n0 >= 1:
                            pe.wait_ge(vt_copied, n0)
                    elif kt == 0:
                        pe.wait_ge(qk32_ready, at(2, 2 * n0 + 1, it))
                        pe.wait_ge(xn_ready, n0 // 2 + 1 + 2 * it)
                    src = c_sb[:, (n0 // 2) % 2, :, :] if i == 0 else xn
                    mm = nc.tensor.matmul(proj_ps[:, :], w_t[:, i, kt, (n0 % 2) * P:(n0 % 2) * P + P],
                                          src[:, kt, :], start=(kt == 0), stop=(kt == CT - 1))
                    if kt == CT - 1:
                        mm.then_inc(qk_ready, 1)

                def project_v(n0, st, it):
                    if st == 0:
                        pe.wait_ge(qk32_ready, at(2, 2 * n0 + 2, it))
                    for kt in range(CT):
                        mm = nc.tensor.matmul(proj_ps[:, st * P:(st + 1) * P],
                                              c_sb[:, (n0 // 2) % 2, kt, st * P:(st + 1) * P],
                                              w_t[:, 2, kt, (n0 % 2) * P:(n0 % 2) * P + P],
                                              start=(kt == 0), stop=(kt == CT - 1))
                    if st == TT - 1:
                        mm.then_inc(v_ready, 1)

                def max_pass(n0, u, it):
                    n0s = n0 % NBUF
                    if u == 0:
                        pe.wait_ge(stack_loaded[n0s], 16 * 2 * PARTS * (n0 // NBUF + 1) + 16 * 2 * PARTS * it)
                    i0 = UNITS * n0 + u
                    if not isinstance(it, int) or i0 >= MAXBUF:
                        pe.wait_ge(max_done, at(UNITS, i0 - MAXBUF + 1, it))
                    tt = u % TT
                    nc.tensor.matmul(smax_ps[:, u % MAXBUF, :], q_stack[n0s][0:SROWS, u // TT, tt * P:(tt + 1) * P],
                                     k_stack[n0s][0:SROWS, u // TT, :], start=True, stop=True).then_inc(s_ready, 1)

                def turn_max(n0, it):
                    pe.wait_ge(vt_copied, at(1, min(n0 + 3, HALVES), it))
                    if n0 >= HALVES - 2:
                        pe.wait_ge(x1_ready, X1_START + HALVES - 4)
                        pe.wait_ge(nm_copied, n0)
                    pe.wait_ge(max_done, at(UNITS, UNITS * (n0 + 1), it))
                    nc.tensor.transpose(proj_ps[0:UNITS, 0:P], negmax[:, n0 % 2, :], ident[:, :]).then_inc(nm_turned, 1)

                def scores(s0, u, it):
                    g, st, j = u // (GH * TT), u // GH % TT, u % GH
                    n0s = s0 % NBUF
                    if u == 0:
                        pe.wait_ge(rows_loaded[n0s], 16 * (s0 // NBUF + 1) + 16 * it)
                        pe.wait_ge(ones_ready, 2 * NBUF)
                    i0 = UNITS * s0 + u
                    if not isinstance(it, int) or i0 >= 2:
                        pe.wait_ge(exp_done, at(UNITS, i0 - 1, it))
                    nc.tensor.matmul(st_ps[:, u % 2, :],
                                     k_stack[n0s][0:SROWS + PARTS, GH * g + j, st * P:(st + 1) * P],
                                     q_stack[n0s][0:SROWS + PARTS, GH * g + j, :], start=True, stop=True).then_inc(st_ready, 1)

                def pv(k0, it):
                    n0, g, st = k0 // STEPS, k0 // TT % 2, k0 % TT
                    pe.wait_ge(exp_done, at(UNITS, GH * (k0 + 1), it))
                    if st == 0 and (not isinstance(it, int) or k0 >= TT):
                        pe.wait_ge(pv_copied, at(2, k0 // TT, it))
                    if st == 0 and g == 0:
                        pe.wait_ge(vt_copied, at(1, n0 + 1, it))
                    for j in range(GH):
                        mm = nc.tensor.matmul(pv_ps[32 * j:32 * j + 32, :], v_t[n0 % NBUF][:, st, GH * g + j, :],
                                              probs[:, k0 % 2, j, :], start=(st == 0), stop=(st == TT - 1),
                                              tile_position=(0, 32 * j))
                    mm.then_inc(pv_done, 1)

                def project_out(s0, o, kt, it):
                    b0 = s0 // 2 - 1
                    if kt == 0 and o == 0:
                        pe.wait_ge(attn_ready, at(1, 2 * (b0 + 1), it))
                        pe.wait_ge(nm_copied, at(1, min(s0 + 2, HALVES), it))
                    if kt == 0 and (not isinstance(it, int) or b0 > 0 or o > 0):
                        pe.wait_ge(x1_ready, at(1, X1_START + 2 * b0 + o, it))
                    mm = nc.tensor.matmul(proj_ps[:, :], w_t[:, 3, kt, o * P:(o + 1) * P], attn[:, b0 % 2, kt, :],
                                          start=(kt == 0), stop=(kt == CT - 1))
                    if kt == CT - 1:
                        mm.then_inc(y_ready, 1)

                pe.wait_ge(x1_ready, X1_START)
                def project(n0):
                    for i in range(2):
                        for kt in range(CT):
                            project_qk(n0, i, kt, 0)
                    for st in range(TT):
                        project_v(n0, st, 0)

                project(0)
                project(1)
                for u in range(UNITS):
                    max_pass(0, u, 0)
                project(2)
                turn_max(0, 0)
                for u in range(LEAD):
                    max_pass(1, u, 0)

                def slot(s0, it, loop):
                    outs = s0 % 2 == 0 and s0 > 0
                    proj = loop or s0 + 3 < HALVES
                    for u in range(UNITS):
                        scores(s0, u, it)
                        if u % GH == 1 and (loop or STEPS * s0 + (u - 5) // GH >= 0):
                            pv(STEPS * s0 + (u - 5) // GH, it)
                        n0 = s0 + 1 + (u + LEAD) // UNITS
                        if loop or n0 < HALVES:
                            max_pass(n0, (u + LEAD) % UNITS, it)
                        if proj and u in (0, 2, 6, 8):
                            project_qk(s0 + 3, u // 6, u % 6 // 2, it)
                        if proj and 12 <= u < 12 + TT:
                            project_v(s0 + 3, u - 12, it)
                        if u == 20 and (loop or s0 + 1 < HALVES):
                            turn_max(s0 + 1, it)
                        if outs and u in OUT_UNITS:
                            project_out(s0, OUT_UNITS.index(u) // CT, OUT_UNITS.index(u) % CT, it)

                def tail(s0, it, loop):
                    pv(STEPS * s0 - 1, it)
                    for o in range(CT):
                        for kt in range(CT):
                            project_out(s0, o, kt, it)

                slots(pe, slot, tail, [pe.alloc_register(f"round{i}") for i in range(2)])

            @block.vector
            def _(dve):
                def chained(ins):
                    count["step"] += 1
                    ins.then_inc(dve_step, 1)
                    dve.wait_ge(dve_step, count["step"])

                def row_stats(lo, hi, i):
                    for t in range(lo, hi):
                        last = nc.vector.bn_stats(stats[:, t, :], x_sb[:, t, :])
                    chained(last)
                    for t in range(lo, hi):
                        last = nc.vector.bn_aggr(mv[:, t, :], stats[:, t, :])
                    chained(last)
                    nc.vector.tensor_scalar(rs_a[:, lo:hi], mv[:, lo:hi, 1], LN_EPS, None, ALU.add).then_inc(var_ready, 1)

                def row_rstd(lo, hi, i):
                    dve.wait_ge(std_ready, i + 1)
                    chained(nc.vector.reciprocal(rs_b[:, lo:hi], rs_b[:, lo:hi]))
                    chained(nc.vector.tensor_tensor(rs_a[:, lo:hi], rs_a[:, lo:hi], rs_b[:, lo:hi], ALU.mult))
                    chained(nc.vector.tensor_tensor(rs_a[:, lo:hi], rs_a[:, lo:hi], rs_b[:, lo:hi], ALU.mult))
                    chained(nc.vector.tensor_scalar(rs_a[:, lo:hi], rs_a[:, lo:hi], -0.5, 1.5, ALU.mult, ALU.add))
                    chained(nc.vector.tensor_tensor(rstd[:, lo:hi], rs_a[:, lo:hi], rs_b[:, lo:hi], ALU.mult))

                def normalize(b0, it):
                    if not (isinstance(it, int) and b0 == 0):
                        dve.wait_ge(qk_ready, at(2, 2 * (2 * b0 - 1) + 2, it))
                    for ct in range(CT):
                        t = CT * b0 + ct + 2 * CT * it
                        last = nc.vector.tensor_scalar(xn[:, ct, :], x_sb[:, t, :], mv[:, t, 0:1], rstd[:, bass.ds(t, 1)],
                                                       ALU.subtract, ALU.mult)
                    last.then_inc(xn_ready, 1)

                def high(n0, i, it):
                    dve.wait_ge(qk32_ready, at(2, 2 * n0 + i + 1, it))
                    if not (isinstance(it, int) and n0 == 0):
                        dve.wait_ge(parts_written[i], at(16, 16 * n0, it))
                    nc.vector.tensor_copy(parts[:, i, 0, :], qk32[:, i, :]).then_inc(high_ready, 1)

                def mid(n0, i, it):
                    dve.wait_ge(mid_rest_ready, at(2, 2 * n0 + i + 1, it))
                    nc.vector.tensor_copy(parts[:, i, 1, :], rest[:, i, :]).then_inc(mid_ready, 1)

                def maxima(n0, u, it):
                    dve.wait_ge(s_ready, at(UNITS, UNITS * n0 + u + 1, it))
                    if u == 0 and (not isinstance(it, int) or n0 >= 2):
                        dve.wait_ge(nm_turned, at(1, n0 - 1, it))
                    nc.vector.tensor_reduce(negmax[:, n0 % 2, u:u + 1], smax_ps[:, u % MAXBUF, :],
                                            AX_X, ALU.max, negate=True).then_inc(max_done, 1)

                def max_parts(n0, it):
                    dve.wait_ge(nm_turned, at(1, n0 + 1, it))
                    nc.vector.tensor_copy(nm32[:, :], proj_ps[0:HH * TT, 0:P]).then_inc(nm_copied, 1)
                    dve.wait_ge(nm_copied, at(1, n0 + 1, it))
                    if not (isinstance(it, int) and n0 == 0):
                        dve.wait_ge(rows_written, at(16, 16 * n0, it))
                    nc.vector.tensor_copy(nm_parts[:, 0, :], nm32[:, :]).then_inc(nm_step, 1)
                    dve.wait_ge(nm_step, at(3, 3 * n0 + 1, it))
                    nc.vector.tensor_tensor(nm_rest[:, :], nm32[:, :], nm_parts[:, 0, :], ALU.subtract).then_inc(nm_step, 1)
                    dve.wait_ge(nm_step, at(3, 3 * n0 + 2, it))
                    nc.vector.tensor_copy(nm_parts[:, 1, :], nm_rest[:, :]).then_inc(nm_step, 1)
                    dve.wait_ge(nm_step, at(3, 3 * n0 + 3, it))
                    nc.vector.tensor_tensor(nm_parts[:, 2, :], nm_rest[:, :], nm_parts[:, 1, :],
                                            ALU.subtract).then_inc(nm_parts_ready, 1)

                def invert(n0, it):
                    dve.wait_ge(den_loaded, at(16, 16 * (n0 + 1), it))
                    nc.vector.reciprocal(den[:, :], den[:, :]).then_inc(den_inverted, 1)

                def divide(n0, it):
                    dve.wait_ge(rec_loaded, at(16, 16 * (n0 + 1), it))
                    dve.wait_ge(num_loaded, at(16, 16 * (n0 + 1), it))
                    half = attn[:, n0 // 2 % 2, n0 % 2, :]
                    nc.vector.tensor_tensor(half, half, recip[:, :], ALU.mult).then_inc(attn_ready, 1)

                def residual(s0, o, it):
                    b0 = s0 // 2 - 1
                    dve.wait_ge(y_ready, 2 * b0 + o + 1 + 4 * it)
                    t = CT * b0 + o + 2 * CT * it
                    nc.vector.scalar_tensor_tensor(out=x_sb[:, t, :], in0=proj_ps[:, :], scalar=bo_all[:, o:o + 1],
                                                   in1=x_sb[:, t, :], op0=ALU.add, op1=ALU.add).then_inc(x1_ready, 1)

                nc.vector.memset(zeros[:, :], 0.0).then_inc(zeros_ready, 1)
                dve.wait_ge(x0_loaded, 16)
                row_stats(0, CT, 0)
                row_rstd(0, CT, 0)
                normalize(0, 0)
                for i in range(4):
                    dve.wait_ge(wt_ready, i + 1)
                    src, dst = smax_ps[:, i, :], w_t[:, i, :, :].rearrange("p k c -> p (k c)")
                    if i < 2:
                        src = src.rearrange("p (m h k) -> p m k h", h=HH, k=KCH)
                        dst = dst.rearrange("p (m k h) -> p m k h", h=HH, k=KCH)
                    nc.vector.tensor_copy(dst, src).then_inc(wt_copied, 1)
                dve.wait_ge(bo_ready, 1)
                nc.vector.tensor_tensor(bo_all[:, :], bo_col[:, :], pv_ps[:, 0:CT], ALU.add).then_inc(x1_ready, X1_START)
                high(0, 0, 0)
                mid(0, 0, 0)
                high(0, 1, 0)
                mid(0, 1, 0)
                dve.wait_ge(xr_loaded, 16 * (B - 1))
                row_stats(CT, B * CT, 1)
                row_rstd(CT, B * CT, 1)
                high(1, 0, 0)
                mid(1, 0, 0)
                high(1, 1, 0)
                mid(1, 1, 0)
                normalize(1, 0)
                for u in range(UNITS):
                    maxima(0, u, 0)
                high(2, 0, 0)
                mid(2, 0, 0)
                high(2, 1, 0)
                mid(2, 1, 0)
                max_parts(0, 0)
                for u in range(LEAD):
                    maxima(1, u, 0)

                def slot(s0, it, loop):
                    outs = s0 % 2 == 0 and s0 > 0
                    proj = loop or s0 + 3 < HALVES
                    for u in range(UNITS):
                        n0 = s0 + 1 + (u + LEAD) // UNITS
                        if loop or n0 < HALVES:
                            maxima(n0, (u + LEAD) % UNITS, it)
                        if u == 1 and s0 % 2 == 1 and (loop or s0 + 3 < HALVES):
                            normalize((s0 + 3) // 2, it)
                        if proj and u in (4, 10):
                            high(s0 + 3, u // 10, it)
                        if proj and u in (7, 13):
                            mid(s0 + 3, u // 13, it)
                        if u == 11 and (loop or s0 > 0):
                            invert(s0 - 1, it)
                        if u == 18 and (loop or s0 > 0):
                            divide(s0 - 1, it)
                        if u == 21 and (loop or s0 + 1 < HALVES):
                            max_parts(s0 + 1, it)
                        if outs and u in (26, 31):
                            residual(s0, u // 31, it)

                def tail(s0, it, loop):
                    invert(s0 - 1, it)
                    divide(s0 - 1, it)
                    for o in range(CT):
                        residual(s0, o, it)

                slots(dve, slot, tail)

        attn_ctx.close()

        token_ctx = ExitStack()

        def tsb(name, shape, dt=F32):
            return sb(name, shape, dt, token_ctx)

        def tps(name, shape, dt=F32):
            return token_ctx.enter_context(nc.psum_tensor(name, shape, dt))

        w_gu = tsb("w_gu", [P, E + 1, DT, 2 * F])
        w_dn = tsb("w_dn", [P, E + 1, FT, D])
        w_rt = tsb("w_rt", [P, DT, E])
        rms_bc = tsb("rms_bc", [P, D])
        h_ring = tsb("h_ring", [P, 2, D])
        h_all = tsb("h_all", [P, NTILE, D])
        h_t = tsb("h_t", [P, 2, DT, P])
        h_in = tsb("h_in", [P, 2, D])
        sig_g = tsb("sig_g", [P, F])
        act_gu = tsb("act_gu", [P, F])
        act_t = tsb("act_t", [P, FT, P])
        y_sb = tsb("y_sb", [P, 2, D])
        NR = 8
        rt = tsb("rt", [P, NR, NTILE, E])
        small = tsb("small", [P, 16, NTILE])
        blk = tsb("blk", [P, 48, E])
        blk_e = tsb("blk_e", [P, 64])
        blk_i = tsb("blk_i", [P, 64], I32)
        slot_i = tsb("slot_i", [P, 2, NTILE], I32)
        iota_i = tsb("iota_i", [P, 64], I32)
        iota = tsb("iota", [P, 64])
        rank = tsb("rank", [P, E])
        chosen = tsb("chosen", [P, NTILE, E], BF16)
        before = tsb("before", [P, P], BF16)
        ones_bf = tsb("ones_bf", [P, P], BF16)

        tr_ps = tps("tr_ps", [P, 2, D])
        lg_ps = tps("lg_ps", [P, NTILE, E])
        cnt_ps = tps("cnt_ps", [P, 2, NTILE, E])
        gu_ps = tps("gu_ps", [P, 2 * F])
        at_ps = tps("at_ps", [P, FT, P])
        y_ps = tps("y_ps", [P, 2, D])

        wgu_loaded = sem("wgu_loaded")
        wdn_loaded = sem("wdn_loaded")
        wrt_loaded = sem("wrt_loaded")
        rms_loaded = sem("rms_loaded")
        const_ready = sem("const_ready")
        var2_ready = sem("var2_ready")
        std2_ready = sem("std2_ready")
        h_part = sem("h_part")
        h_ready = sem("h_ready")
        h_kept = sem("h_kept")
        h_stored = [sem(f"h_stored{i}") for i in range(2)]
        h_turned = sem("h_turned")
        ht_ready = sem("ht_ready")
        lg_ready = sem("lg_ready")
        gap_ready = sem("gap_ready")
        egap_ready = sem("egap_ready")
        chosen_ready = sem("chosen_ready")
        cnt_ready = sem("cnt_ready")
        slots_ready = sem("slots_ready")
        blocks_ready = sem("blocks_ready")
        scattered = sem("scattered")
        in_loaded = [sem(f"in_loaded{i}") for i in range(2)]
        in_turned = sem("in_turned")
        inT_ready = sem("inT_ready")
        gu_ready = sem("gu_ready")
        silu_done = sem("silu_done")
        act_ready = sem("act_ready")
        act_turned = sem("act_turned")
        actT_ready = sem("actT_ready")
        dn_ready = sem("dn_ready")
        y_copied = sem("y_copied")
        y_stored = [sem(f"y_stored{i}") for i in range(2)]
        sh_loaded = [sem(f"sh_loaded{i}") for i in range(2)]
        got = [[sem(f"got{c}{i}") for i in range(4)] for c in range(TOPK)]
        mixed = sem("mixed")
        out_stored = sem("out_stored")

        def pairs(eng, step, n):
            rounds = (n - 4) // 2
            for t in range(3):
                step(t, 0)
            with eng.Fori(0, rounds) as it:
                step(3, it)
                step(4, it)
            for t in range(3 + 2 * rounds, n):
                step(t, 0)

        def inner(k0, lag, it):
            return k0 >= lag or not isinstance(it, int)

        with nc.Block() as block:

            @block.sync
            def _(sp):
                sp.dma_start(rms_bc[:, :], rms_w.rearrange("(o d) -> o d", o=1).broadcast_to([P, D])).then_inc(rms_loaded, 16)
                sp.dma_start(w_rt[:, :, :], router_w.rearrange("(a p) e -> p a e", p=P)).then_inc(wrt_loaded, 16)

                def keep_h(t0, it):
                    dst = blocks_in[t0 + 2 * it]
                    sync_wait(sp, (h_ready, t0 + 1 + 2 * it))
                    sp.dma_start(dst, h_ring[:, t0 % 2, :]).then_inc(h_stored[t0 % 2], 16)

                pairs(sp, keep_h, NTILE)
                for i in range(2):
                    sync_wait(sp, (h_stored[i], 16 * NTILE // 2))

                def load(k0, it):
                    src = blocks_in[k0 + 2 * it]
                    if inner(k0, 2, it):
                        sync_wait(sp, (in_turned, k0 - 1 + 2 * it))
                    sp.dma_start(h_in[:, k0 % 2, :], src).then_inc(in_loaded[k0 % 2], 16)

                load(0, 0)
                load(1, 0)
                shared_rounds = (NTILE - 2) // 2
                with sp.Fori(0, shared_rounds) as it:
                    for k0 in range(2):
                        load(k0 + 2, it)
                sync_wait(sp, (scattered, 16 * TOPK * NTILE))
                with sp.Fori(shared_rounds, (BLOCKS - 3) // 2) as it:
                    for k0 in range(2):
                        load(k0 + 2, it)
                load(BLOCKS - 1, 0)
                for i in range(2):
                    sync_wait(sp, (y_stored[i], 16 * ((BLOCKS + 1 - i) // 2)))
                for t in range(NTILE + 1):
                    if t < NTILE:
                        if t >= 2:
                            sync_wait(sp, (mixed, t - 1))
                        sp.dma_start(h_in[:, t % 2, :], blocks_out[t]).then_inc(sh_loaded[t % 2], 16)
                    if t >= 1:
                        sync_wait(sp, (mixed, t))
                        sp.dma_start(out_t[t - 1], x_sb[:, t - 1, :]).then_inc(out_stored, 16)
                sync_wait(sp, (out_stored, 16 * NTILE))

            @block.gpsimd
            def _(pool):
                nc.gpsimd.iota(iota_i[:, :], [[1, 64]], base=0, channel_multiplier=0).then_inc(const_ready, 1)
                nc.gpsimd.memset(ones_bf[:, :], 1.0).then_inc(const_ready, 1)
                pool.wait_ge(const_ready, 2)
                nc.gpsimd.affine_select(out=before[:, :], in_=ones_bf[:, :], compare_op=ALU.is_ge, fill=0.0,
                                        base=-1, pattern=[[1, P]], channel_multiplier=-1).then_inc(const_ready, 1)

                def keep(t0, it):
                    pool.wait_ge(h_ready, t0 + 1 + 2 * it)
                    nc.gpsimd.tensor_copy(h_all[:, bass.ds(t0 + 2 * it, 1), :], h_ring[:, t0 % 2:t0 % 2 + 1, :]
                                          ).then_inc(h_kept, 1)

                pairs(pool, keep, NTILE)
                pool.wait_ge(slots_ready, 1)
                for i in range(2):
                    pool.wait_ge(h_stored[i], 16 * NTILE // 2)
                pool.wait_ge(h_kept, NTILE)
                for t in range(NTILE):
                    for c in range(2):
                        nc.gpsimd.indirect_dma_start(
                            rows_in, bass.IndirectOffsetOnAxis(ap=slot_i[:, c, t:t + 1], axis=0),
                            h_all[:, t, :], None).then_inc(scattered, 16)
                for i in range(2):
                    pool.wait_ge(y_stored[i], 16 * ((BLOCKS + 1 - i) // 2))
                pool.wait_ge(scattered, 16 * 2 * NTILE)
                for t in range(NTILE):
                    if t >= 4:
                        pool.wait_ge(mixed, t - 3)
                    for c in range(2):
                        nc.gpsimd.indirect_dma_start(
                            h_all[:, 2 * (t % 4) + c, :], None, rows_out,
                            bass.IndirectOffsetOnAxis(ap=slot_i[:, c, t:t + 1], axis=0)).then_inc(got[c][t % 4], 16)

            @block.scalar
            def _(act):
                for e in [E] + list(range(E)):
                    gate, up, down = (sw_gate, sw_up, sw_down) if e == E else (w_gate[e], w_up[e], w_down[e])
                    act.dma_start(w_gu[:, e, :, 0:F], gate.rearrange("(a p) f -> p a f", p=P)).then_inc(wgu_loaded, 16)
                    act.dma_start(w_gu[:, e, :, F:2 * F], up.rearrange("(a p) f -> p a f", p=P)).then_inc(wgu_loaded, 16)
                    act.dma_start(w_dn[:, e, :, :], down.rearrange("(a p) d -> p a d", p=P)).then_inc(wdn_loaded, 16)
                for i in range(2):
                    act.wait_ge(var2_ready, i + 1)
                    nc.scalar.activation(rs_b[:, :], rs_a[:, :], ACT.Sqrt).then_inc(std2_ready, 1)

                def turn_h(t0, it):
                    act.wait_ge(h_turned, t0 + 1 + 2 * it)
                    if inner(t0, 2, it):
                        act.wait_ge(lg_ready, t0 - 1 + 2 * it)
                    nc.scalar.activation(h_t[:, t0 % 2, :, :], tr_ps[:, t0 % 2, :].rearrange("p (a t) -> p a t", a=DT),
                                         ACT.Copy).then_inc(ht_ready, 1)

                pairs(act, turn_h, NTILE)
                act.wait_ge(gap_ready, 1)
                nc.scalar.activation(small[:, 3, :], small[:, 2, :], ACT.Exp).then_inc(egap_ready, 1)

                def turn_in(k0, it):
                    act.wait_ge(in_turned, k0 + 1 + 2 * it)
                    if inner(k0, 2, it):
                        act.wait_ge(gu_ready, k0 - 1 + 2 * it)
                    else:
                        act.wait_ge(lg_ready, NTILE)
                    nc.scalar.activation(h_t[:, k0 % 2, :, :], tr_ps[:, k0 % 2, :].rearrange("p (a t) -> p a t", a=DT),
                                         ACT.Copy).then_inc(inT_ready, 1)

                def y_copy(k0, it):
                    act.wait_ge(dn_ready, k0 + 1 + 2 * it)
                    if inner(k0, 2, it):
                        act.wait_ge(y_stored[k0 % 2], 16 * (k0 // 2) + 16 * it)
                    nc.scalar.activation(y_sb[:, k0 % 2, :], y_ps[:, k0 % 2, :], ACT.Copy).then_inc(y_copied, 1)
                    act.wait_ge(y_copied, k0 + 1 + 2 * it)
                    act.dma_start(blocks_out[k0 + 2 * it], y_sb[:, k0 % 2, :]).then_inc(y_stored[k0 % 2], 16)

                turn_in(0, 0)

                def step(k0, it):
                    act.wait_ge(gu_ready, k0 + 1 + 2 * it)
                    if k0 >= 1:
                        act.wait_ge(act_ready, k0 + 2 * it)
                    nc.scalar.activation(sig_g[:, :], gu_ps[:, 0:F], ACT.Silu).then_inc(silu_done, 1)
                    if k0 + 1 < BLOCKS:
                        turn_in(k0 + 1, it)
                    if k0 >= 1:
                        y_copy(k0 - 1, it)

                pairs(act, step, BLOCKS)
                y_copy(BLOCKS - 1, 0)

            @block.tensor
            def _(pe):
                def logits(t0, it):
                    pe.wait_ge(ht_ready, t0 + 1 + 2 * it)
                    for a in range(DT):
                        mm = nc.tensor.matmul(lg_ps[:, bass.ds(t0 + 2 * it, 1), :], h_t[:, t0 % 2, a, :], w_rt[:, a, :],
                                              start=(a == 0), stop=(a == DT - 1))
                    mm.then_inc(lg_ready, 1)

                def turn_h(t0, it):
                    pe.wait_ge(h_ready, t0 + 1 + 2 * it)
                    if inner(t0, 2, it):
                        pe.wait_ge(ht_ready, t0 - 1 + 2 * it)
                    for a in range(DT):
                        mm = nc.tensor.transpose(tr_ps[:, t0 % 2, a * P:(a + 1) * P], h_ring[:, t0 % 2, a * P:(a + 1) * P],
                                                 ident[:, :])
                    mm.then_inc(h_turned, 1)
                    if t0 >= 1:
                        logits(t0 - 1, it)

                pe.wait_ge(wrt_loaded, 16)
                pairs(pe, turn_h, NTILE)
                logits(NTILE - 1, 0)
                pe.wait_ge(chosen_ready, 1)
                pe.wait_ge(const_ready, 3)
                nc.tensor.matmul(cnt_ps[:, 0, :, :], before[:, :], chosen[:, :, :], start=True, stop=True)
                nc.tensor.matmul(cnt_ps[:, 1, :, :], ones_bf[:, :], chosen[:, :, :], start=True, stop=True,
                                 ).then_inc(cnt_ready, 1)

                def turn_in(k0, it):
                    pe.wait_ge(in_loaded[k0 % 2], 16 * (k0 // 2 + 1) + 16 * it)
                    if inner(k0, 2, it):
                        pe.wait_ge(inT_ready, k0 - 1 + 2 * it)
                    for a in range(DT):
                        mm = nc.tensor.transpose(tr_ps[:, k0 % 2, a * P:(a + 1) * P], h_in[:, k0 % 2, a * P:(a + 1) * P],
                                                 ident[:, :])
                    mm.then_inc(in_turned, 1)

                def down(k0, expert, it):
                    pe.wait_ge(actT_ready, k0 + 1 + 2 * it)
                    if inner(k0, 2, it):
                        pe.wait_ge(y_copied, k0 - 1 + 2 * it)
                    for a in range(FT):
                        mm = nc.tensor.matmul(y_ps[:, k0 % 2, :], act_t[:, a, :], w_dn[:, bass.ds(expert, 1), a, :],
                                              start=(a == 0), stop=(a == FT - 1))
                    mm.then_inc(dn_ready, 1)

                def turn_act(k0, it):
                    pe.wait_ge(act_ready, k0 + 1 + 2 * it)
                    if k0 >= 1:
                        pe.wait_ge(actT_ready, k0 + 2 * it)
                    for a in range(FT):
                        mm = nc.tensor.transpose(at_ps[:, a, :], act_gu[:, a * P:(a + 1) * P], ident[:, :])
                    mm.then_inc(act_turned, 1)

                expert_reg = [pe.alloc_register(f"expert_reg{i}") for i in range(2)]

                def load_expert(k0, it):
                    pe.reg_load(expert_reg[k0 % 2], blk_i[0:1, bass.ds(k0 + 2 * it, 1)])

                def expert_of(k0):
                    return pe.snap(expert_reg[k0 % 2], min_val=0, max_val=E)

                pe.wait_ge(blocks_ready, 1)
                pe.wait_ge(wgu_loaded, 16 * 2 * (E + 1))
                pe.wait_ge(wdn_loaded, 16 * (E + 1))
                turn_in(0, 0)
                load_expert(0, 0)

                def step(k0, it):
                    expert = expert_of(k0)
                    if k0 >= 1:
                        turn_act(k0 - 1, it)
                    pe.wait_ge(inT_ready, k0 + 1 + 2 * it)
                    for a in range(DT):
                        mm = nc.tensor.matmul(gu_ps[:, :], h_t[:, k0 % 2, a, :], w_gu[:, bass.ds(expert, 1), a, :],
                                              start=(a == 0), stop=(a == DT - 1))
                    mm.then_inc(gu_ready, 1)
                    if k0 + 1 < BLOCKS:
                        turn_in(k0 + 1, it)
                    if k0 >= 1:
                        down(k0 - 1, expert_of(k0 - 1), it)
                    if k0 + 1 < BLOCKS:
                        load_expert(k0 + 1, it)

                pairs(pe, step, BLOCKS)
                turn_act(BLOCKS - 1, 0)
                down(BLOCKS - 1, expert_of(BLOCKS - 1), 0)

            @block.vector
            def _(dve):
                def chained(ins):
                    count["step"] += 1
                    ins.then_inc(dve_step, 1)
                    dve.wait_ge(dve_step, count["step"])

                def rsqrt(dst, var, i):
                    dve.wait_ge(std2_ready, i + 1)
                    chained(nc.vector.reciprocal(rs_b[:, :], rs_b[:, :]))
                    chained(nc.vector.tensor_tensor(rs_a[:, :], rs_a[:, :], rs_b[:, :], ALU.mult))
                    chained(nc.vector.tensor_tensor(rs_a[:, :], rs_a[:, :], rs_b[:, :], ALU.mult))
                    chained(nc.vector.tensor_scalar(rs_a[:, :], rs_a[:, :], -0.5, 1.5, ALU.mult, ALU.add))
                    chained(nc.vector.tensor_tensor(dst, rs_a[:, :], rs_b[:, :], ALU.mult))

                V = nc.vector
                for t in range(NTILE):
                    last = V.bn_stats(stats[:, t, :], x_sb[:, t, :])
                chained(last)
                for t in range(NTILE):
                    last = V.bn_aggr(mv[:, t, :], stats[:, t, :])
                chained(last)
                V.tensor_scalar(rs_a[:, :], mv[:, :, 1], LN_EPS, None, ALU.add).then_inc(var2_ready, 1)
                rsqrt(rstd[:, :], None, 0)
                chained(V.tensor_tensor(rs_a[:, :], mv[:, :, 1], rstd[:, :], ALU.mult))
                chained(V.tensor_tensor(rs_a[:, :], rs_a[:, :], rstd[:, :], ALU.mult))
                V.tensor_scalar(rs_a[:, :], rs_a[:, :], RMS_EPS, None, ALU.add).then_inc(var2_ready, 1)
                rsqrt(small[:, 0, :], None, 1)
                chained(V.tensor_tensor(rstd[:, :], rstd[:, :], small[:, 0, :], ALU.mult))
                dve.wait_ge(rms_loaded, 16)

                def make_h(t0, it):
                    if inner(t0, 2, it):
                        dve.wait_ge(h_turned, t0 - 1 + 2 * it)
                        dve.wait_ge(h_kept, t0 - 1 + 2 * it)
                        dve.wait_ge(h_stored[t0 % 2], 16 * (t0 // 2) + 16 * it)
                    t = t0 + 2 * it
                    V.tensor_scalar(h_ring[:, t0 % 2, :], x_sb[:, t, :], mv[:, t, 0:1], rstd[:, bass.ds(t, 1)],
                                    ALU.subtract, ALU.mult).then_inc(h_part, 1)
                    dve.wait_ge(h_part, t0 + 1 + 2 * it)
                    V.tensor_tensor(h_ring[:, t0 % 2, :], h_ring[:, t0 % 2, :], rms_bc[:, :], ALU.mult).then_inc(h_ready, 1)

                pairs(dve, make_h, NTILE)

                dve.wait_ge(const_ready, 3)
                chained(V.tensor_copy(iota[:, :], iota_i[:, :]))
                chained(V.tensor_scalar(rank[:, :], iota[:, 0:E], -1.0, float(E), ALU.mult, ALU.add))

                def by_expert(ap):
                    return ap.rearrange("p (t o) -> p t o", o=1).broadcast_to([P, NTILE, E])

                def by_tile(ap):
                    return ap.rearrange("p (o e) -> p o e", o=1).broadcast_to([P, NTILE, E])

                def pick(dst, logit, top):
                    chained(V.tensor_reduce(top, logit, AX_X, ALU.max))
                    chained(V.tensor_tensor(dst, logit, by_expert(top), ALU.is_equal))
                    chained(V.tensor_tensor(dst, dst, by_tile(rank[:, :]), ALU.mult))
                    chained(V.tensor_reduce(small[:, 4, :], dst, AX_X, ALU.max))
                    chained(V.tensor_tensor(dst, dst, by_expert(small[:, 4, :]), ALU.is_equal))

                LG, M1, M2, LG2, TOT, PA, PB, POS = (rt[:, i, :, :] for i in range(8))
                dve.wait_ge(lg_ready, NTILE)
                chained(V.tensor_copy(LG, lg_ps[:, :, :]))
                pick(M1, LG, small[:, 0, :])
                chained(V.scalar_tensor_tensor(out=LG2, in0=M1, scalar=-3.0e38, in1=LG, op0=ALU.mult, op1=ALU.add))
                pick(M2, LG2, small[:, 1, :])
                chained(V.tensor_tensor(small[:, 2, :], small[:, 1, :], small[:, 0, :], ALU.subtract))
                V.tensor_tensor(chosen[:, :, :], M1, M2, ALU.add).then_inc(chosen_ready, 1)
                V.tensor_copy(small[:, 5, :], small[:, 2, :]).then_inc(gap_ready, 1)
                dve.wait_ge(egap_ready, 1)
                chained(V.tensor_scalar(small[:, 4, :], small[:, 3, :], 1.0, None, ALU.add))
                chained(V.reciprocal(small[:, 6, :], small[:, 4, :]))
                chained(V.tensor_tensor(small[:, 7, :], small[:, 3, :], small[:, 6, :], ALU.mult))
                dve.wait_ge(cnt_ready, 1)
                chained(V.tensor_copy(TOT, cnt_ps[:, 1, :, :]))
                src, dst = TOT, PA
                for s in (1, 2, 4, 8):
                    V.tensor_copy(dst[:, 0:s, :], src[:, 0:s, :])
                    chained(V.tensor_tensor(dst[:, s:NTILE, :], src[:, s:NTILE, :], src[:, 0:NTILE - s, :], ALU.add))
                    src, dst = dst, (PB if dst is PA else PA)
                run = src
                total = run[:, NTILE - 1, :]
                chained(V.tensor_scalar(blk_e[:, 0:NTILE], iota[:, 0:NTILE], float(P), None, ALU.mult))
                chained(V.tensor_tensor(blk[:, 0:NTILE, :],
                                        total.rearrange("p (o e) -> p o e", o=1).broadcast_to([P, NTILE, E]),
                                        blk_e[:, 0:NTILE].rearrange("p (t o) -> p t o", o=1).broadcast_to([P, NTILE, E]),
                                        ALU.is_gt))
                nb, na, spare = blk[:, 45, :], blk[:, 46, :], blk[:, 47, :]
                chained(V.tensor_reduce(nb, blk[:, 0:NTILE, :].rearrange("p t e -> p e t"), AX_X, ALU.add))
                src, dst = nb, na
                for s in (1, 2, 4):
                    V.tensor_copy(dst[:, 0:s], src[:, 0:s])
                    chained(V.tensor_tensor(dst[:, s:E], src[:, s:E], src[:, 0:E - s], ALU.add))
                    src, dst = dst, (spare if dst is na else na)
                ends, first = src, dst
                KB = EXPERT_BLOCKS
                chained(V.tensor_tensor(blk[:, 0:KB, 0:E - 1],
                                        iota[:, 0:KB].rearrange("p (t o) -> p t o", o=1).broadcast_to([P, KB, E - 1]),
                                        ends[:, 0:E - 1].rearrange("p (o e) -> p o e", o=1).broadcast_to([P, KB, E - 1]),
                                        ALU.is_ge))
                chained(V.memset(blk_e[:, 0:NTILE], float(E)))
                chained(V.tensor_reduce(blk_e[:, NTILE:BLOCKS], blk[:, 0:KB, 0:E - 1], AX_X, ALU.add))
                V.tensor_copy(blk_i[:, 0:BLOCKS], blk_e[:, 0:BLOCKS]).then_inc(blocks_ready, 1)
                chained(V.tensor_tensor(first, ends, nb, ALU.subtract))
                chained(V.tensor_scalar(first, first, float(NTILE), float(P), ALU.add, ALU.mult))
                chained(V.tensor_tensor(POS, run, TOT, ALU.subtract))
                chained(V.tensor_tensor(POS, POS, by_tile(first), ALU.add))
                chained(V.tensor_tensor(POS, POS, cnt_ps[:, 0, :, :], ALU.add))
                for c, m in enumerate((M1, M2)):
                    chained(V.tensor_tensor(LG, m, POS, ALU.mult))
                    chained(V.tensor_reduce(small[:, 8 + c, :], LG, AX_X, ALU.add))
                V.tensor_copy(slot_i[:, :, :], small[:, 8:10, :]).then_inc(slots_ready, 1)

                def turn_copy(k0, it):
                    dve.wait_ge(act_turned, k0 + 1 + 2 * it)
                    if k0 >= 1:
                        dve.wait_ge(dn_ready, k0 + 2 * it)
                    V.tensor_copy(act_t[:, :, :], at_ps[:, :, :]).then_inc(actT_ready, 1)

                def step(k0, it):
                    if k0 >= 1:
                        turn_copy(k0 - 1, it)
                    dve.wait_ge(silu_done, k0 + 1 + 2 * it)
                    if k0 >= 1:
                        dve.wait_ge(act_turned, k0 + 2 * it)
                    V.tensor_tensor(act_gu[:, :], sig_g[:, :], gu_ps[:, F:2 * F], ALU.mult).then_inc(act_ready, 1)

                pairs(dve, step, BLOCKS)
                turn_copy(BLOCKS - 1, 0)

                for t in range(NTILE):
                    dve.wait_ge(sh_loaded[t % 2], 16 * (t // 2 + 1))
                    chained(V.tensor_tensor(x_sb[:, t, :], x_sb[:, t, :], h_in[:, t % 2, :], ALU.add))
                    dve.wait_ge(got[0][t % 4], 16 * (t // 4 + 1))
                    chained(V.scalar_tensor_tensor(out=x_sb[:, t, :], in0=h_all[:, 2 * (t % 4), :], scalar=small[:, 6, t:t + 1],
                                                   in1=x_sb[:, t, :], op0=ALU.mult, op1=ALU.add))
                    dve.wait_ge(got[1][t % 4], 16 * (t // 4 + 1))
                    V.scalar_tensor_tensor(out=x_sb[:, t, :], in0=h_all[:, 2 * (t % 4) + 1, :], scalar=small[:, 7, t:t + 1],
                                           in1=x_sb[:, t, :], op0=ALU.mult, op1=ALU.add).then_inc(mixed, 1)

        token_ctx.close()


_INS = [n for n in (
    'x', 'ctx_2048', 'L0_xattn_Wq', 'L0_xattn_bq', 'L0_xattn_Wk', 'L0_xattn_bk', 'L0_xattn_Wv', 'L0_xattn_bv',
    'L0_xattn_Wo', 'L0_xattn_bo', 'L0_ffn_rms_weight', 'L0_ffn_router_w', 'L0_ffn_w_gate', 'L0_ffn_w_up',
    'L0_ffn_w_down', 'L0_ffn_sw_gate', 'L0_ffn_sw_up', 'L0_ffn_sw_down')]


def kernel(**inputs):
    import numpy as np
    import concourse.bacc as bacc
    from concourse.bass_utils import run_bass_kernel_spmd

    nc = bacc.Bacc("TRN2", target_bir_lowering=False, num_devices=1)
    arrays, args = {}, []
    for name in _INS:
        a = np.ascontiguousarray(inputs[name])
        arrays[f"in_{name}"] = a
        args.append(nc.dram_tensor(f"in_{name}", a.shape, mybir.dt.from_np(a.dtype), kind="ExternalInput").ap())
    args.append(nc.dram_tensor("out_0", (B, C, T), F32, kind="ExternalOutput").ap())
    xattn_ffn_kernel(nc, *args)
    r = run_bass_kernel_spmd(nc, [arrays], core_ids=[0])
    return r.results[0]["out_0"]
```

```python
from contextlib import ExitStack

import concourse.bass as bass
from concourse import mybir

ALU = mybir.AluOpType
ACT = mybir.ActivationFunctionType
BF16 = mybir.dt.bfloat16
F32 = mybir.dt.float32
I32 = mybir.dt.int32
AX_X = mybir.AxisListType.X

P = 128
B, C, T = 8, 256, 512
KCH = 16
SCALE = float(KCH) ** -0.5
HALVES = 2 * B
HH = 8
CT = C // P
TT = T // P
GH = 4
UNITS = HH * TT
STEPS = UNITS // GH
LEAD = 16
MAXBUF = 4
PARTS = 3
PRODUCTS = PARTS * (PARTS + 1) // 2
SROWS = KCH * PRODUCTS
NBUF = 4
LN_EPS, RMS_EPS = 1e-5, 1e-6
E, F, D = 8, 256, T
FT, DT = F // P, D // P
NTILE = B * C // P
TOPK = 2
BLOCKS = NTILE * TOPK + E - 1
GT = 4


def xattn_ffn_kernel(nc, x, ctxt, wq, bq, wk, bk, wv, bv, wo, bo, rms_w, router_w, w_gate, w_up, w_down,
                     sw_gate, sw_up, sw_down, out):
    x_t = x.rearrange("b (o p) t -> b p o t", p=P)
    c_t = ctxt.rearrange("b (o p) t -> b p o t", p=P)
    parts_dram = nc.dram_tensor("parts_dram", [NBUF, 2, PARTS, P, T], BF16, kind="Internal").ap()
    den_dram = nc.dram_tensor("den_dram", [HH, T], F32, kind="Internal").ap()
    rec_dram = nc.dram_tensor("rec_dram", [HH, T], F32, kind="Internal").ap()
    num_dram = nc.dram_tensor("num_dram", [HH // GH, GH, KCH, T], F32, kind="Internal").ap()
    blocks_in = nc.dram_tensor("blocks_in", [BLOCKS, P, D], F32, kind="Internal").ap()
    blocks_out = nc.dram_tensor("blocks_out", [BLOCKS, P, D], F32, kind="Internal").ap()
    rows_in = blocks_in.rearrange("k p d -> (k p) d")
    rows_out = blocks_out.rearrange("k p d -> (k p) d")
    out_t = out.rearrange("b (o p) t -> (b o) p t", p=P)
    rows_dram = nc.dram_tensor("rows_dram", [NBUF, PARTS, HH * TT, P], BF16, kind="Internal").ap()

    with ExitStack() as outer:
        def sem(name):
            return outer.enter_context(nc.semaphore(name))

        def sb(name, shape, dt=F32, stack=outer):
            return stack.enter_context(nc.sbuf_tensor(name, shape, dt))

        x_sb = sb("x_sb", [P, B * CT, T])
        ident = sb("ident", [P, P])
        zeros = sb("zeros", [P, D])
        stats = sb("stats", [P, B * CT, 6])
        mv = sb("mv", [P, B * CT, 2])
        rstd = sb("rstd", [P, B * CT])
        rs_a = sb("rs_a", [P, B * CT])
        rs_b = sb("rs_b", [P, B * CT])
        rstd2 = sb("rstd2", [P, B * CT])
        pv_raw = sb("pv_raw", [P, 2, HH // GH, T])
        attn = sb("attn", [P, 2, CT, T])
        recip = sb("recip", [P, T])
        den = sb("den", [P, HH * T // P])
        bo_all = sb("bo_all", [P, CT])
        w_o = sb("w_o", [P, CT, C])
        sh_gu = sb("sh_gu", [P, DT, 2 * F])
        sh_dn = sb("sh_dn", [P, FT, D])
        w_rt = sb("w_rt", [P, DT, E])
        rms_bc = sb("rms_bc", [P, D])
        shared_loaded = sem("shared_loaded")

        attn_ctx = ExitStack()

        def asb(name, shape, dt=F32):
            return sb(name, shape, dt, attn_ctx)

        def aps(name, shape, dt=F32):
            return attn_ctx.enter_context(nc.psum_tensor(name, shape, dt))

        q_stack = [asb(f"q_stack{i}", [P, HH, T], BF16) for i in range(NBUF)]
        k_stack = [asb(f"k_stack{i}", [P, HH, T], BF16) for i in range(NBUF)]
        v_t = [asb(f"v_t{i}", [P, TT, HH, 32]) for i in range(NBUF)]
        probs = asb("probs", [P, 2, 4, T])
        c_sb = asb("c_sb", [P, 2, CT, T])
        xn = asb("xn", [P, CT, T])
        qk32 = asb("qk32", [P, 2, T])
        rest = asb("rest", [P, 2, T])
        parts = asb("parts", [P, 2, PARTS, T], BF16)
        negmax = asb("negmax", [P, 2, HH * TT])
        nm32 = asb("nm32", [HH * TT, P])
        nm_rest = asb("nm_rest", [HH * TT, P])
        nm_parts = asb("nm_parts", [HH * TT, PARTS, P], BF16)
        w_raw = asb("w_raw", [P, 4, CT, C])
        w_t = asb("w_t", [P, 3, CT, C])
        bqk = asb("bqk", [P, 2, CT])
        bo_col = asb("bo_col", [P, CT])
        bv_col = asb("bv_col", [P, CT])

        smax_ps = aps("smax_ps", [P, MAXBUF, T])
        st_ps = aps("st_ps", [P, 2, T])
        pv_ps = aps("pv_ps", [P, T])
        proj_ps = aps("proj_ps", [P, T])

        ident_ready = sem("ident_ready")
        ones_ready = sem("ones_ready")
        w_loaded = sem("w_loaded")
        b_loaded = sem("b_loaded")
        c_loaded = [sem(f"c_loaded{i}") for i in range(2)]
        x_loaded = [sem(f"x_loaded{b}") for b in range(B)]
        wt_ready = sem("wt_ready")
        wt_copied = sem("wt_copied")
        bo_ready = sem("bo_ready")
        var_ready = sem("var_ready")
        std_ready = sem("std_ready")
        dve_step = sem("dve_step")
        xn_ready = sem("xn_ready")
        qk_ready = sem("qk_ready")
        qk32_ready = sem("qk32_ready")
        high_ready = sem("high_ready")
        mid_rest_ready = sem("mid_rest_ready")
        mid_ready = sem("mid_ready")
        low_ready = sem("low_ready")
        parts_written = [sem(f"parts_written{i}") for i in range(2)]
        stack_loaded = [sem(f"stack_loaded{i}") for i in range(NBUF)]
        v_ready = sem("v_ready")
        vt_copied = sem("vt_copied")
        s_ready = sem("s_ready")
        max_done = sem("max_done")
        nm_turned = sem("nm_turned")
        nm_copied = sem("nm_copied")
        nm_step = sem("nm_step")
        nm_parts_ready = sem("nm_parts_ready")
        rows_written = sem("rows_written")
        rows_loaded = [sem(f"rows_loaded{i}") for i in range(NBUF)]
        st_ready = sem("st_ready")
        exp_done = sem("exp_done")
        pv_done = sem("pv_done")
        pv_copied = sem("pv_copied")
        zeros_ready = sem("zeros_ready")
        zeroed = sem("zeroed")
        den_written = sem("den_written")
        den_loaded = sem("den_loaded")
        den_inverted = sem("den_inverted")
        rec_written = sem("rec_written")
        rec_loaded = sem("rec_loaded")
        num_written = sem("num_written")
        num_loaded = sem("num_loaded")
        attn_ready = sem("attn_ready")
        y_ready = sem("y_ready")
        stats_ready = sem("stats_ready")
        x1_ready = sem("x1_ready")

        OUT_UNITS = (22, 23, 26, 28)
        LOOP_SLOTS = NBUF
        LOOPS = 3

        sp_wait_reg = [nc.sync.alloc_register(f"sp_wait{i}") for i in range(2)]

        def sync_wait(sp, *waits):
            for (_, value), reg in zip(waits, sp_wait_reg):
                if not isinstance(value, int):
                    sp.reg_mov(reg, value)
            for (sem, value), reg in zip(waits, sp_wait_reg):
                if isinstance(value, int):
                    sp.wait_ge(sem, value)
                else:
                    sp.wait_ge(zeros_ready, 1)
                    sp.wait_ge(sem, reg)

        def slots(eng, slot, tail=None, own=None):
            slot(0, 0, False)
            with eng.Fori(0, LOOPS) as it:
                for s0 in range(1, 1 + LOOP_SLOTS):
                    if own is None:
                        slot(s0, it, True)
                        continue
                    eng.reg_mov(own[s0 % 2], it)
                    slot(s0, eng.snap(own[s0 % 2], min_val=0, max_val=LOOPS - 1), True)
            for s in range(1 + LOOP_SLOTS * LOOPS, HALVES):
                slot(s, 0, False)
            if tail is not None:
                tail(HALVES, 0, False)

        def at(per_slot, first, it):
            return first + per_slot * LOOP_SLOTS * it

        X1_START = CT + 1
        ATTN_START = 1
        LAST = CT * (B - 1)
        EARLY = LAST - CT
        count = {"step": 0}

        def score_bank(s0, u):
            if s0 < HALVES - 1:
                return st_ps[:, u % 2, :], 2
            banks = MAXBUF + 2
            bank = st_ps[:, u % banks, :] if u % banks < 2 else smax_ps[:, u % banks - 2, :]
            return bank, 2 if u < 2 else banks if u >= banks else 0

        def denominators(sp, n0, it):
            sync_wait(sp, (pv_copied, at(2, 2 * n0 + 2, it)))
            sp.dma_start(den_dram.rearrange("(g j) t -> j g t", j=GH), pv_raw[KCH:P:32, n0 % 2, :, :]).then_inc(den_written, 16)
            for j in range(GH):
                sp.dma_start(num_dram[:, j].rearrange("g k t -> k g t"),
                             pv_raw[32 * j:32 * j + KCH, n0 % 2, :, :]).then_inc(num_written, 16)
            sync_wait(sp, (den_written, at(16, 16 * (n0 + 1), it)))
            sp.dma_start(den[:, :], den_dram.rearrange("h (q r) -> (h q) r", r=HH * T // P)
                         ).then_inc(den_loaded, 16)
            sync_wait(sp, (num_written, at(16 * GH, 16 * GH * (n0 + 1), it)),
                      (x1_ready, at(1, X1_START + CT * (n0 // 2 - 1), it)))
            sp.dma_start(attn[:, n0 // 2 % 2, n0 % 2, :],
                         num_dram.rearrange("g j k t -> (g j k) t")).then_inc(num_loaded, 16)
            sync_wait(sp, (den_inverted, at(1, n0 + 1, it)), (attn_ready, at(1, ATTN_START + n0, it)))
            sp.dma_start(rec_dram.rearrange("h (q r) -> (h q) r", r=HH * T // P), den[:, :]
                         ).then_inc(rec_written, 16)
            sync_wait(sp, (rec_written, at(16, 16 * (n0 + 1), it)))
            sp.dma_start(recip[:, :], rec_dram.rearrange("h (o t) -> h o t", o=1).broadcast_to([HH, KCH, T])
                         ).then_inc(rec_loaded, 16)

        def project_out(pe, s0, o, kt, bank, it):
            b0 = s0 // 2 - 1
            if kt == 0 and o == 0:
                pe.wait_ge(attn_ready, at(1, ATTN_START + 2 * (b0 + 1), it))
                pe.wait_ge(nm_copied, at(1, min(s0 + 2, HALVES), it))
            if kt == 0 and (not isinstance(it, int) or b0 > 0 or o > 0):
                pe.wait_ge(x1_ready, at(1, X1_START + 2 * b0 + o, it))
            mm = nc.tensor.matmul(bank, w_o[:, kt, o * P:(o + 1) * P], attn[:, b0 % 2, kt, :],
                                  start=(kt == 0), stop=(kt == CT - 1))
            if kt == CT - 1:
                mm.then_inc(y_ready, 1)

        def chained(dve, ins):
            count["step"] += 1
            ins.then_inc(dve_step, 1)
            dve.wait_ge(dve_step, count["step"])

        def row_stats(dve, lo, hi):
            for b in range(lo // CT, hi // CT):
                dve.wait_ge(x_loaded[b], 16)
                for t in range(CT * b, CT * (b + 1)):
                    last = nc.vector.bn_stats(stats[:, t, :], x_sb[:, t, :])
            chained(dve, last)

        def row_variance(dve, lo, hi):
            for t in range(lo, hi):
                last = nc.vector.bn_aggr(mv[:, t, :], stats[:, t, :])
            chained(dve, last)
            nc.vector.tensor_scalar(rs_a[:, lo:hi], mv[:, lo:hi, 1], LN_EPS, None, ALU.add).then_inc(var_ready, 1)

        def row_rstd(dve, lo, hi, i, dst):
            dve.wait_ge(std_ready, i + 1)
            chained(dve, nc.vector.reciprocal(rs_b[:, lo:hi], rs_b[:, lo:hi]))
            chained(dve, nc.vector.tensor_tensor(rs_a[:, lo:hi], rs_a[:, lo:hi], rs_b[:, lo:hi], ALU.mult))
            chained(dve, nc.vector.tensor_tensor(rs_a[:, lo:hi], rs_a[:, lo:hi], rs_b[:, lo:hi], ALU.mult))
            chained(dve, nc.vector.tensor_scalar(rs_a[:, lo:hi], rs_a[:, lo:hi], -0.5, 1.5, ALU.mult, ALU.add))
            chained(dve, nc.vector.tensor_tensor(dst[:, lo:hi], rs_a[:, lo:hi], rs_b[:, lo:hi], ALU.mult))

        def row_scale(dve, lo, hi, i, steps=(0, 1, 2)):
            if 0 in steps:
                row_variance(dve, lo, hi)
            if 1 in steps:
                row_rstd(dve, lo, hi, i, rstd)
                chained(dve, nc.vector.tensor_tensor(rs_a[:, lo:hi], mv[:, lo:hi, 1], rstd[:, lo:hi], ALU.mult))
                chained(dve, nc.vector.tensor_tensor(rs_a[:, lo:hi], rs_a[:, lo:hi], rstd[:, lo:hi], ALU.mult))
                nc.vector.tensor_scalar(rs_a[:, lo:hi], rs_a[:, lo:hi], RMS_EPS, None, ALU.add).then_inc(var_ready, 1)
            if 2 in steps:
                row_rstd(dve, lo, hi, i + 1, rstd2)
                chained(dve, nc.vector.tensor_tensor(rstd[:, lo:hi], rstd[:, lo:hi], rstd2[:, lo:hi], ALU.mult))

        def invert(dve, n0, it):
            dve.wait_ge(den_loaded, at(16, 16 * (n0 + 1), it))
            nc.vector.reciprocal(den[:, :], den[:, :]).then_inc(den_inverted, 1)

        def divide(dve, n0, it):
            dve.wait_ge(rec_loaded, at(16, 16 * (n0 + 1), it))
            dve.wait_ge(num_loaded, at(16, 16 * (n0 + 1), it))
            half = attn[:, n0 // 2 % 2, n0 % 2, :]
            nc.vector.tensor_tensor(half, half, recip[:, :], ALU.mult).then_inc(attn_ready, 1)

        def residual(dve, s0, o, bank, it):
            b0 = s0 // 2 - 1
            dve.wait_ge(y_ready, 2 * b0 + o + 1 + 4 * it)
            t = CT * b0 + o + 2 * CT * it
            nc.vector.scalar_tensor_tensor(out=x_sb[:, t, :], in0=bank, scalar=bo_all[:, o:o + 1],
                                           in1=x_sb[:, t, :], op0=ALU.add, op1=ALU.add).then_inc(x1_ready, 1)

        def std(act, lo, hi, i):
            act.wait_ge(var_ready, i + 1)
            nc.scalar.activation(rs_b[:, lo:hi], rs_a[:, lo:hi], ACT.Sqrt).then_inc(std_ready, 1)

        with nc.Block() as block:

            @block.sync
            def _(sp):
                sp.dma_start(x_sb[:, 0:CT, :], x_t[0]).then_inc(x_loaded[0], 16)
                for i, w in enumerate((wk, wq, wv, wo)):
                    sp.dma_start(w_raw[:, i, :, :], w.rearrange("(o p) c -> p o c", p=P)).then_inc(w_loaded, 16)
                for i, bias in enumerate((bk, bq)):
                    for o in range(CT):
                        sp.dma_start(bqk[:, i, o:o + 1],
                                     bias[P * o:P * (o + 1)].rearrange("(h k o) -> k h o", k=KCH, o=1),
                                     allow_slow_non_contiguous=True).then_inc(b_loaded, 16)
                sp.dma_start(bo_col[:, :], bo.rearrange("(o p) -> p o", p=P),
                             allow_slow_non_contiguous=True).then_inc(b_loaded, 16)
                sp.dma_start(bv_col[:, :], bv.rearrange("(o p) -> p o", p=P),
                             allow_slow_non_contiguous=True).then_inc(b_loaded, 16)
                for b in range(1, B):
                    sp.dma_start(x_sb[:, CT * b:CT * b + CT, :], x_t[b]).then_inc(x_loaded[b], 16)

                def write_parts(n0, it):
                    for i in range(2):
                        sync_wait(sp, (low_ready, at(2, 2 * n0 + i + 1, it)))
                        sp.dma_start(parts_dram[n0 % NBUF, i].rearrange("s p t -> p s t"),
                                     parts[:, i, :, :]).then_inc(parts_written[i], 16)

                def load_stacks(n0, it):
                    if not (isinstance(it, int) and n0 < NBUF):
                        sync_wait(sp, (st_ready, at(UNITS, UNITS * (n0 - NBUF + 1), it)))
                    for i, dst in enumerate((k_stack, q_stack)):
                        sync_wait(sp, (parts_written[i], at(16, 16 * (n0 + 1), it)))
                        for part in range(PARTS):
                            count = PARTS - part
                            g = PRODUCTS - count * (count + 1) // 2
                            by_channel = parts_dram[n0 % NBUF, i].rearrange("s (i h) t -> s i (h t)", h=HH)
                            src = (by_channel[part:part + 1].broadcast_to([count, KCH, HH * T]) if i == 1
                                   else by_channel[0:count].rearrange("s i f -> (s i) f"))
                            sp.dma_start(dst[n0 % NBUF][KCH * g:KCH * (g + count), :, :].rearrange("p h t -> p (h t)"), src
                                         ).then_inc(stack_loaded[n0 % NBUF], 16)

                def rows(n0, it):
                    sync_wait(sp, (nm_parts_ready, at(1, n0 + 1, it)))
                    sp.dma_start(rows_dram[n0 % NBUF].rearrange("s r t -> r s t"),
                                 nm_parts[:, :, :]).then_inc(rows_written, 16)
                    sync_wait(sp, (rows_written, at(16, 16 * (n0 + 1), it)))
                    sp.dma_start(q_stack[n0 % NBUF][SROWS:SROWS + PARTS, :, :],
                                 rows_dram[n0 % NBUF].rearrange("s (h j) t -> s h (j t)", h=HH)
                                 ).then_inc(rows_loaded[n0 % NBUF], 16)

                for n in range(2):
                    write_parts(n, 0)
                    load_stacks(n, 0)
                write_parts(2, 0)
                rows(0, 0)
                load_stacks(2, 0)
                sp.dma_start(rms_bc[:, :], rms_w.rearrange("(o d) -> o d", o=1).broadcast_to([P, D])).then_inc(shared_loaded, 16)
                sp.dma_start(w_rt[:, :, :], router_w.rearrange("(a p) e -> p a e", p=P)).then_inc(shared_loaded, 16)
                sp.dma_start(sh_gu[:, :, 0:F], sw_gate.rearrange("(a p) f -> p a f", p=P)).then_inc(shared_loaded, 16)
                sp.dma_start(sh_gu[:, :, F:2 * F], sw_up.rearrange("(a p) f -> p a f", p=P)).then_inc(shared_loaded, 16)
                sp.dma_start(sh_dn[:, :, :], sw_down.rearrange("(a p) d -> p a d", p=P)).then_inc(shared_loaded, 16)

                def slot(s0, it, loop):
                    if loop or s0 > 0:
                        denominators(sp, s0 - 1, it)
                    if loop or s0 + 3 < HALVES:
                        write_parts(s0 + 3, it)
                    if loop or s0 + 1 < HALVES:
                        rows(s0 + 1, it)
                    if loop or s0 + 3 < HALVES:
                        load_stacks(s0 + 3, it)

                slots(sp, slot)

            @block.gpsimd
            def _(pool):
                nc.gpsimd.memset(ident[:, :], 0.0).then_inc(ident_ready, 1)
                pool.wait_ge(ident_ready, 1)
                nc.gpsimd.affine_select(out=ident[:, :], in_=ident[:, :], compare_op=ALU.not_equal, fill=1.0,
                                        base=0, pattern=[[-1, P]], channel_multiplier=1).then_inc(ident_ready, 1)
                for b in range(2):
                    nc.gpsimd.dma_start(c_sb[:, b, :, :], c_t[b]).then_inc(c_loaded[b], 16)
                pool.wait_ge(ident_ready, 2)

                def ones(i):
                    nc.gpsimd.memset(k_stack[i][SROWS:SROWS + PARTS, :, :], 1.0).then_inc(ones_ready, 1)
                    pool.wait_ge(ones_ready, 2 * i + 1)
                    nc.gpsimd.memset(v_t[i][:, :, :, KCH:32], 1.0).then_inc(ones_ready, 1)
                    pool.wait_ge(ones_ready, 2 * i + 2)

                ones(0)
                ones(1)

                def split(n0, it):
                    for i in range(2):
                        pool.wait_ge(high_ready, at(2, 2 * n0 + i + 1, it))
                        nc.gpsimd.tensor_tensor(rest[:, i, :], qk32[:, i, :], parts[:, i, 0, :],
                                                ALU.subtract).then_inc(mid_rest_ready, 1)
                        pool.wait_ge(mid_ready, at(2, 2 * n0 + i + 1, it))
                        nc.gpsimd.tensor_tensor(parts[:, i, 2, :], rest[:, i, :], parts[:, i, 1, :],
                                                ALU.subtract).then_inc(low_ready, 1)

                split(0, 0)
                split(1, 0)
                split(2, 0)
                pool.wait_ge(low_ready, 6)
                ones(2)
                ones(3)

                def load_c(n0, it):
                    b0 = n0 // 2
                    pool.wait_ge(v_ready, at(1, n0 - 2, it))
                    nc.gpsimd.dma_start(c_sb[:, b0 % 2, :, :], c_t[b0 + 2 * it]).then_inc(c_loaded[b0 % 2], 16)

                def clear_blocks(s0, it):
                    if s0 == 1:
                        pool.wait_ge(zeros_ready, 1)
                    for k in range(3):
                        nc.gpsimd.dma_start(blocks_in[3 * (s0 - 1) + k + 3 * LOOP_SLOTS * it], zeros[:, :]
                                            ).then_inc(zeroed, 16)

                def slot(s0, it, loop):
                    if s0 % 2 == 1 and (loop or s0 + 3 < HALVES):
                        load_c(s0 + 3, it)
                    if loop or s0 + 3 < HALVES:
                        split(s0 + 3, it)
                    if loop or 0 < s0 <= BLOCKS // 3:
                        clear_blocks(s0, it)

                slots(pool, slot)
                pool.wait_ge(zeroed, 16 * BLOCKS)

            @block.scalar
            def _(act):
                def qk_bias(n0, i, it):
                    act.wait_ge(qk_ready, at(2, 2 * n0 + i + 1, it))
                    if not (isinstance(it, int) and n0 == 0):
                        act.wait_ge(mid_rest_ready, at(2, 2 * n0 + i - 1, it))
                    nc.scalar.activation(qk32[:, i, :], proj_ps[:, :], ACT.Identity,
                                         bias=bqk[:, i, n0 % 2:n0 % 2 + 1]).then_inc(qk32_ready, 1)

                def v_copy(n0, it):
                    act.wait_ge(v_ready, at(1, n0 + 1, it))
                    if not (isinstance(it, int) and n0 < NBUF):
                        act.wait_ge(pv_done, at(STEPS, STEPS * (n0 - NBUF + 1), it))
                    nc.scalar.activation(v_t[n0 % NBUF][:, :, :, 0:KCH],
                                         proj_ps[:, :].rearrange("p (s h k) -> p s h k", s=TT, k=KCH),
                                         ACT.Copy).then_inc(vt_copied, 1)

                std(act, 0, CT, 0)
                act.wait_ge(b_loaded, 16 * 6)
                for n in range(3):
                    qk_bias(n, 0, 0)
                    qk_bias(n, 1, 0)
                    v_copy(n, 0)
                    if n == 1:
                        std(act, CT, B * CT, 1)

                def pv_copy(g0, it):
                    act.wait_ge(pv_done, at(STEPS, STEPS // 2 * (g0 + 1), it))
                    if g0 % 2 == 0 and g0 >= 2:
                        act.wait_ge(den_written, at(16, 16 * (g0 // 2), it))
                        act.wait_ge(num_written, at(16 * GH, 16 * GH * (g0 // 2), it))
                    nc.scalar.activation(pv_raw[:, g0 // 2 % 2, g0 % 2, :], pv_ps[:, :], ACT.Copy).then_inc(pv_copied, 1)

                def slot(s0, it, loop):
                    proj = loop or s0 + 3 < HALVES
                    for u in range(UNITS):
                        act.wait_ge(st_ready, at(UNITS, UNITS * s0 + u + 1, it))
                        k0 = STEPS * s0 + u // GH
                        if u % GH == 0 and (loop or k0 >= 2):
                            act.wait_ge(pv_done, at(STEPS, k0 - 1, it))
                        nc.scalar.activation(probs[:, k0 % 2, u % GH, :], score_bank(s0, u)[0],
                                             ACT.Exp, scale=SCALE).then_inc(exp_done, 1)
                        if u == 2 and (loop or s0 > 0):
                            pv_copy(2 * s0 - 1, it)
                        if u == (20 if s0 == HALVES - 1 else 18):
                            pv_copy(2 * s0, it)
                        if s0 == HALVES - 2 and u in (3, 9):
                            std(act, 0, EARLY, 2 + u // 9)
                        if proj and u in (3, 9):
                            qk_bias(s0 + 3, u // 9, it)
                        if proj and u == 16:
                            v_copy(s0 + 3, it)

                slots(act, slot, lambda s0, it, loop: pv_copy(2 * s0 - 1, it))

            @block.tensor
            def _(pe):
                pe.wait_ge(zeros_ready, 1)
                for _ in range(4):
                    nc.tensor.matmul(pv_ps[:, :], zeros[:, 0:P], zeros[:, :], start=True, stop=True)
                pe.wait_ge(ident_ready, 2)
                pe.wait_ge(w_loaded, 16 * 4)
                for i in range(4):
                    for o in range(CT):
                        for kt in range(CT):
                            mm = nc.tensor.transpose(smax_ps[:, i, kt * C + o * P:kt * C + (o + 1) * P],
                                                     w_raw[:, i, o, kt * P:(kt + 1) * P], ident[:, :])
                    mm.then_inc(wt_ready, 1)
                pe.wait_ge(wt_copied, 4)
                pe.wait_ge(b_loaded, 16 * 6)
                for o in range(CT):
                    for kt in range(CT):
                        mm = nc.tensor.matmul(pv_ps[:, o:o + 1], w_o[:, kt, o * P:(o + 1) * P], bv_col[:, kt:kt + 1],
                                              start=(kt == 0), stop=(kt == CT - 1))
                mm.then_inc(bo_ready, 1)

                def project_qk(n0, i, kt, it):
                    if kt == 0 and i == 0:
                        pe.wait_ge(c_loaded[(n0 // 2) % 2], 16 * (n0 // 4 + 1) + 16 * it)
                        if n0 >= 4 and n0 % 2 == 0:
                            pe.wait_ge(x1_ready, at(1, X1_START + n0 - 4, it))
                        elif n0 >= 3:
                            pe.wait_ge(nm_copied, at(1, n0 - 2, it))
                        elif n0 >= 1:
                            pe.wait_ge(vt_copied, n0)
                    elif kt == 0:
                        pe.wait_ge(qk32_ready, at(2, 2 * n0 + 1, it))
                        pe.wait_ge(xn_ready, n0 // 2 + 1 + 2 * it)
                    src = c_sb[:, (n0 // 2) % 2, :, :] if i == 0 else xn
                    mm = nc.tensor.matmul(proj_ps[:, :], w_t[:, i, kt, (n0 % 2) * P:(n0 % 2) * P + P],
                                          src[:, kt, :], start=(kt == 0), stop=(kt == CT - 1))
                    if kt == CT - 1:
                        mm.then_inc(qk_ready, 1)

                def project_v(n0, st, it):
                    if st == 0:
                        pe.wait_ge(qk32_ready, at(2, 2 * n0 + 2, it))
                    for kt in range(CT):
                        mm = nc.tensor.matmul(proj_ps[:, st * P:(st + 1) * P],
                                              c_sb[:, (n0 // 2) % 2, kt, st * P:(st + 1) * P],
                                              w_t[:, 2, kt, (n0 % 2) * P:(n0 % 2) * P + P],
                                              start=(kt == 0), stop=(kt == CT - 1))
                    if st == TT - 1:
                        mm.then_inc(v_ready, 1)

                def max_pass(n0, u, it):
                    n0s = n0 % NBUF
                    if u == 0:
                        pe.wait_ge(stack_loaded[n0s], 16 * 2 * PARTS * (n0 // NBUF + 1) + 16 * 2 * PARTS * it)
                    i0 = UNITS * n0 + u
                    if not isinstance(it, int) or i0 >= MAXBUF:
                        pe.wait_ge(max_done, at(UNITS, i0 - MAXBUF + 1, it))
                    tt = u % TT
                    nc.tensor.matmul(smax_ps[:, u % MAXBUF, :], q_stack[n0s][0:SROWS, u // TT, tt * P:(tt + 1) * P],
                                     k_stack[n0s][0:SROWS, u // TT, :], start=True, stop=True).then_inc(s_ready, 1)

                def turn_max(n0, it):
                    pe.wait_ge(vt_copied, at(1, min(n0 + 3, HALVES), it))
                    if n0 >= HALVES - 2:
                        pe.wait_ge(x1_ready, X1_START + HALVES - 4)
                        pe.wait_ge(nm_copied, n0)
                    pe.wait_ge(max_done, at(UNITS, UNITS * (n0 + 1), it))
                    nc.tensor.transpose(proj_ps[0:UNITS, 0:P], negmax[:, n0 % 2, :], ident[:, :]).then_inc(nm_turned, 1)

                def scores(s0, u, it):
                    bank, wait_exp = score_bank(s0, u)
                    g, st, j = u // (GH * TT), u // GH % TT, u % GH
                    n0s = s0 % NBUF
                    if u == 0:
                        pe.wait_ge(rows_loaded[n0s], 16 * (s0 // NBUF + 1) + 16 * it)
                        pe.wait_ge(ones_ready, 2 * NBUF)
                    i0 = UNITS * s0 + u
                    if wait_exp and (not isinstance(it, int) or i0 >= 2):
                        pe.wait_ge(exp_done, at(UNITS, i0 + 1 - wait_exp, it))
                    elif not wait_exp:
                        pe.wait_ge(max_done, UNITS * HALVES)
                    nc.tensor.matmul(bank,
                                     k_stack[n0s][0:SROWS + PARTS, GH * g + j, st * P:(st + 1) * P],
                                     q_stack[n0s][0:SROWS + PARTS, GH * g + j, :], start=True, stop=True).then_inc(st_ready, 1)

                def pv(k0, it):
                    n0, g, st = k0 // STEPS, k0 // TT % 2, k0 % TT
                    pe.wait_ge(exp_done, at(UNITS, GH * (k0 + 1), it))
                    if st == 0 and (not isinstance(it, int) or k0 >= TT):
                        pe.wait_ge(pv_copied, at(2, k0 // TT, it))
                    if st == 0 and g == 0:
                        pe.wait_ge(vt_copied, at(1, n0 + 1, it))
                    for j in range(GH):
                        mm = nc.tensor.matmul(pv_ps[32 * j:32 * j + 32, :], v_t[n0 % NBUF][:, st, GH * g + j, :],
                                              probs[:, k0 % 2, j, :], start=(st == 0), stop=(st == TT - 1),
                                              tile_position=(0, 32 * j))
                    mm.then_inc(pv_done, 1)

                def project(n0):
                    for i in range(2):
                        for kt in range(CT):
                            project_qk(n0, i, kt, 0)
                    for st in range(TT):
                        project_v(n0, st, 0)

                pe.wait_ge(x1_ready, X1_START)
                project(0)
                project(1)
                for u in range(UNITS):
                    max_pass(0, u, 0)
                    if u in (0, 2, 8, 10):
                        project_qk(2, u // 8, u % 8 // 2, 0)
                    if 16 <= u < 16 + TT:
                        project_v(2, u - 16, 0)
                turn_max(0, 0)
                for u in range(LEAD):
                    max_pass(1, u, 0)

                def slot(s0, it, loop):
                    outs = s0 % 2 == 0 and s0 > 0
                    proj = loop or s0 + 3 < HALVES
                    for u in range(UNITS):
                        scores(s0, u, it)
                        if s0 == HALVES - 1 and u > 1:
                            if u % GH == 3 and u > GH:
                                pv(STEPS * s0 + (u - 7) // GH, it)
                        elif u % GH == 1 and (loop or STEPS * s0 + (u - 5) // GH >= 0):
                            pv(STEPS * s0 + (u - 5) // GH, it)
                        n0 = s0 + 1 + (u + LEAD) // UNITS
                        if loop or n0 < HALVES:
                            max_pass(n0, (u + LEAD) % UNITS, it)
                        if proj and u in (0, 2, 6, 8):
                            project_qk(s0 + 3, u // 6, u % 6 // 2, it)
                        if proj and 12 <= u < 12 + TT:
                            project_v(s0 + 3, u - 12, it)
                        if u == 18 and (loop or s0 + 1 < HALVES):
                            turn_max(s0 + 1, it)
                        if outs and u in OUT_UNITS:
                            project_out(pe, s0, OUT_UNITS.index(u) // CT, OUT_UNITS.index(u) % CT, proj_ps[:, :], it)

                def tail(s0, it, loop):
                    pv(STEPS * s0 - 1, it)

                slots(pe, slot, tail, [pe.alloc_register(f"round{i}") for i in range(2)])

            @block.vector
            def _(dve):
                def normalize(b0, it):
                    if not (isinstance(it, int) and b0 == 0):
                        dve.wait_ge(qk_ready, at(2, 2 * (2 * b0 - 1) + 2, it))
                    for ct in range(CT):
                        t = CT * b0 + ct + 2 * CT * it
                        last = nc.vector.tensor_scalar(xn[:, ct, :], x_sb[:, t, :], mv[:, t, 0:1], rstd[:, bass.ds(t, 1)],
                                                       ALU.subtract, ALU.mult)
                    last.then_inc(xn_ready, 1)

                def high(n0, i, it):
                    dve.wait_ge(qk32_ready, at(2, 2 * n0 + i + 1, it))
                    if not (isinstance(it, int) and n0 == 0):
                        dve.wait_ge(parts_written[i], at(16, 16 * n0, it))
                    nc.vector.tensor_copy(parts[:, i, 0, :], qk32[:, i, :]).then_inc(high_ready, 1)

                def mid(n0, i, it):
                    dve.wait_ge(mid_rest_ready, at(2, 2 * n0 + i + 1, it))
                    nc.vector.tensor_copy(parts[:, i, 1, :], rest[:, i, :]).then_inc(mid_ready, 1)

                def maxima(n0, u, it):
                    dve.wait_ge(s_ready, at(UNITS, UNITS * n0 + u + 1, it))
                    if u == 0 and (not isinstance(it, int) or n0 >= 2):
                        dve.wait_ge(nm_turned, at(1, n0 - 1, it))
                    nc.vector.tensor_reduce(negmax[:, n0 % 2, u:u + 1], smax_ps[:, u % MAXBUF, :],
                                            AX_X, ALU.max, negate=True).then_inc(max_done, 1)

                def max_parts(n0, it):
                    dve.wait_ge(nm_turned, at(1, n0 + 1, it))
                    nc.vector.tensor_copy(nm32[:, :], proj_ps[0:HH * TT, 0:P]).then_inc(nm_copied, 1)
                    dve.wait_ge(nm_copied, at(1, n0 + 1, it))
                    if not (isinstance(it, int) and n0 == 0):
                        dve.wait_ge(rows_written, at(16, 16 * n0, it))
                    nc.vector.tensor_copy(nm_parts[:, 0, :], nm32[:, :]).then_inc(nm_step, 1)
                    dve.wait_ge(nm_step, at(3, 3 * n0 + 1, it))
                    nc.vector.tensor_tensor(nm_rest[:, :], nm32[:, :], nm_parts[:, 0, :], ALU.subtract).then_inc(nm_step, 1)
                    dve.wait_ge(nm_step, at(3, 3 * n0 + 2, it))
                    nc.vector.tensor_copy(nm_parts[:, 1, :], nm_rest[:, :]).then_inc(nm_step, 1)
                    dve.wait_ge(nm_step, at(3, 3 * n0 + 3, it))
                    nc.vector.tensor_tensor(nm_parts[:, 2, :], nm_rest[:, :], nm_parts[:, 1, :],
                                            ALU.subtract).then_inc(nm_parts_ready, 1)

                nc.vector.memset(zeros[:, :], 0.0).then_inc(zeros_ready, 1)
                nc.vector.memset(recip[:, :], 0.0).then_inc(attn_ready, ATTN_START)
                row_stats(dve, 0, CT)
                row_variance(dve, 0, CT)
                row_rstd(dve, 0, CT, 0, rstd)
                normalize(0, 0)
                for i in range(4):
                    dve.wait_ge(wt_ready, i + 1)
                    src = smax_ps[:, i, :]
                    dst = (w_o if i == 3 else w_t[:, i, :, :]).rearrange("p k c -> p (k c)")
                    if i < 2:
                        src = src.rearrange("p (m h k) -> p m k h", h=HH, k=KCH)
                        dst = dst.rearrange("p (m k h) -> p m k h", h=HH, k=KCH)
                    nc.vector.tensor_copy(dst, src).then_inc(wt_copied, 1)
                dve.wait_ge(bo_ready, 1)
                nc.vector.tensor_tensor(bo_all[:, :], bo_col[:, :], pv_ps[:, 0:CT], ALU.add).then_inc(x1_ready, X1_START)
                row_stats(dve, CT, 3 * CT)
                high(0, 0, 0)
                mid(0, 0, 0)
                row_stats(dve, 3 * CT, 4 * CT)
                high(0, 1, 0)
                mid(0, 1, 0)
                row_stats(dve, 4 * CT, 6 * CT)
                high(1, 0, 0)
                mid(1, 0, 0)
                row_stats(dve, 6 * CT, B * CT)
                row_variance(dve, CT, B * CT)
                high(1, 1, 0)
                mid(1, 1, 0)
                row_rstd(dve, CT, B * CT, 1, rstd)
                normalize(1, 0)
                for u in range(UNITS):
                    maxima(0, u, 0)
                    if u in (5, 13):
                        high(2, u // 13, 0)
                    if u in (8, 16):
                        mid(2, u // 16, 0)
                max_parts(0, 0)
                for u in range(LEAD):
                    maxima(1, u, 0)

                def row_stats_of(s0, o, it):
                    t = CT * (s0 // 2 - 1) + o + 2 * CT * it
                    dve.wait_ge(x1_ready, X1_START + 2 * (s0 // 2 - 1) + o + 1 + 4 * it)
                    nc.vector.bn_stats(stats[:, bass.ds(t, 1), :], x_sb[:, bass.ds(t, 1), :]).then_inc(stats_ready, 1)

                def slot(s0, it, loop):
                    outs = s0 % 2 == 0 and s0 > 0
                    proj = loop or s0 + 3 < HALVES
                    for u in range(UNITS):
                        n0 = s0 + 1 + (u + LEAD) // UNITS
                        if loop or n0 < HALVES:
                            maxima(n0, (u + LEAD) % UNITS, it)
                        if u == 1 and s0 % 2 == 1 and (loop or s0 + 3 < HALVES):
                            normalize((s0 + 3) // 2, it)
                        if proj and u in (4, 10):
                            high(s0 + 3, u // 10, it)
                        if proj and u in (7, 13):
                            mid(s0 + 3, u // 13, it)
                        if u == 8 and (loop or s0 > 0):
                            invert(dve, s0 - 1, it)
                        if u == 17 and (loop or s0 > 0):
                            divide(dve, s0 - 1, it)
                        if u == 19 and (loop or s0 + 1 < HALVES):
                            max_parts(s0 + 1, it)
                        if outs and u in (24, 29):
                            residual(dve, s0, u // 29, proj_ps[:, :], it)
                        if outs and u in (26, 31):
                            row_stats_of(s0, u // 31, it)
                        if s0 == HALVES - 2 and u in (0, 6, 12):
                            dve.wait_ge(stats_ready, EARLY)
                            row_scale(dve, 0, EARLY, 2, (u // 6,))

                slots(dve, slot)

        attn_ctx.close()

        token_ctx = ExitStack()

        def tsb(name, shape, dt=F32):
            return sb(name, shape, dt, token_ctx)

        def tps(name, shape, dt=F32):
            return token_ctx.enter_context(nc.psum_tensor(name, shape, dt))

        w_gu = tsb("w_gu", [P, E, DT, 2 * F])
        GROUPS = NTILE // GT
        GLEN = DT * GT * P
        PER = E // GROUPS
        stretch = tsb("stretch", [P, 2 * GROUPS * GLEN])
        h_all = stretch[:, GROUPS * GLEN:].rearrange("p (t d) -> p t d", d=D)
        w_dn = stretch[:, GLEN:(GROUPS + 1) * GLEN].rearrange("p (e a d) -> p e a d", e=E, a=FT)

        def ht_of(g):
            g = (g + 1) % GROUPS
            return stretch[:, g * GLEN:(g + 1) * GLEN].rearrange("p (a s) -> p a s", a=DT)

        silu_g = attn[:, 0, :, :]
        h_in = attn[:, 1, :, :]
        sh_act = pv_raw
        act_gu = zeros[:, 0:F]
        act_t = zeros[:, F:2 * F].rearrange("p (a t) -> p a t", a=FT)
        y_sb = [rms_bc, recip]
        h_t = sh_act[:, 1, :, :].rearrange("p r (a t) -> p r a t", a=DT)
        NR = 8
        rt = tsb("rt", [P, NR, NTILE, E])
        small = tsb("small", [P, 16, NTILE])
        blk = tsb("blk", [P, 48, E])
        blk_e = tsb("blk_e", [P, 64])
        blk_i = tsb("blk_i", [P, 64], I32)
        slot_i = tsb("slot_i", [P, 2, NTILE], I32)
        iota_i = tsb("iota_i", [P, 64], I32)
        iota = tsb("iota", [P, 64])
        rank = tsb("rank", [P, E])
        chosen = tsb("chosen", [P, NTILE, E], BF16)
        before = tsb("before", [P, P], BF16)
        ones_bf = tsb("ones_bf", [P, P], BF16)

        tr_ps = tps("tr_ps", [P, 2, D])
        lg_ps = tps("lg_ps", [P, NTILE, E])
        cnt_ps = tps("cnt_ps", [P, 2, NTILE, E])
        big_ps = tps("big_ps", [P, 4, 2 * F])
        gu_ps = big_ps[:, 0, :]
        at_ps = big_ps[:, 1, 0:FT * P].rearrange("p (a t) -> p a t", a=FT)
        y_ps = big_ps[:, 2:4, :]

        wgu_loaded = sem("wgu_loaded")
        wdn_loaded = sem("wdn_loaded")
        const_ready = sem("const_ready")
        h_part = sem("h_part")
        h_ready = sem("h_ready")
        h_turned = sem("h_turned")
        ht_ready = sem("ht_ready")
        lg_ready = sem("lg_ready")
        gap_ready = sem("gap_ready")
        egap_ready = sem("egap_ready")
        chosen_ready = sem("chosen_ready")
        cnt_ready = sem("cnt_ready")
        slots_ready = sem("slots_ready")
        blocks_ready = sem("blocks_ready")
        scattered_first = sem("scattered_first")
        scattered = sem("scattered")
        shgu_ready = sem("shgu_ready")
        shsilu_done = sem("shsilu_done")
        shact_ready = sem("shact_ready")
        shdn_ready = sem("shdn_ready")
        shared_added = sem("shared_added")
        in_loaded = [sem(f"in_loaded{i}") for i in range(2)]
        in_turned = sem("in_turned")
        inT_ready = sem("inT_ready")
        gu_ready = sem("gu_ready")
        silu_done = sem("silu_done")
        act_ready = sem("act_ready")
        act_turned = sem("act_turned")
        actT_ready = sem("actT_ready")
        dn_ready = sem("dn_ready")
        y_copied = sem("y_copied")
        y_stored = [sem(f"y_stored{i}") for i in range(2)]
        GOT = (NTILE - GT) // TOPK
        got = [[sem(f"got{c}_{i}") for i in range(GOT)] for c in range(TOPK)]
        mixed = sem("mixed")
        out_stored = sem("out_stored")

        def pairs(eng, step, n):
            rounds = (n - 4) // 2
            for t in range(3):
                step(t, 0)
            with eng.Fori(0, rounds) as it:
                step(3, it)
                step(4, it)
            for t in range(3 + 2 * rounds, n):
                step(t, 0)

        OUT_AFTER = GT - 1

        def inner(k0, lag, it):
            return k0 >= lag or not isinstance(it, int)

        with nc.Block() as block:

            @block.sync
            def _(sp):
                denominators(sp, HALVES - 1, 0)
                for e in range(E):
                    for w, at_col in ((w_gate, 0), (w_up, F)):
                        sp.dma_start(w_gu[:, e, :, at_col:at_col + F], w[e].rearrange("(a p) f -> p a f", p=P)
                                     ).then_inc(wgu_loaded, 16)

                def load_down(g):
                    if g < GROUPS - 1:
                        sync_wait(sp, (shgu_ready, FT * (g + 1)))
                    else:
                        sync_wait(sp, (scattered_first, 16 * TOPK * GT))
                    for e in range(PER * g, PER * (g + 1)):
                        sp.dma_start(w_dn[:, e, :, :], w_down[e].rearrange("(a p) d -> p a d", p=P)).then_inc(wdn_loaded, 16)

                def load(k0, it):
                    src = blocks_in[k0 + 2 * it]
                    if inner(k0, 2, it):
                        sync_wait(sp, (in_turned, k0 - 1 + 2 * it))
                    sp.dma_start(h_in[:, k0 % 2, :], src).then_inc(in_loaded[k0 % 2], 16)

                for g in (0, 1, GROUPS - 1):
                    load_down(g)
                sync_wait(sp, (y_ready, CT * B))
                sync_wait(sp, (scattered, 16 * TOPK * (NTILE - GT)))
                load(0, 0)
                load(1, 0)
                with sp.Fori(0, (BLOCKS - 3) // 2) as it:
                    for k0 in range(2):
                        load(k0 + 2, it)
                load(BLOCKS - 1, 0)
                for t in range(NTILE):
                    sync_wait(sp, (mixed, t + 1))
                    sp.dma_start(out_t[t], x_sb[:, t, :]).then_inc(out_stored, 16)
                sync_wait(sp, (out_stored, 16 * NTILE))

            @block.gpsimd
            def _(pool):
                nc.gpsimd.iota(iota_i[:, :], [[1, 64]], base=0, channel_multiplier=0).then_inc(const_ready, 1)
                nc.gpsimd.memset(ones_bf[:, :], 1.0).then_inc(const_ready, 1)
                pool.wait_ge(const_ready, 2)
                nc.gpsimd.affine_select(out=before[:, :], in_=ones_bf[:, :], compare_op=ALU.is_ge, fill=0.0,
                                        base=-1, pattern=[[1, P]], channel_multiplier=-1).then_inc(const_ready, 1)
                pool.wait_ge(h_ready, NTILE)
                pool.wait_ge(slots_ready, 1)
                for t in range(NTILE):
                    for c in range(TOPK):
                        nc.gpsimd.indirect_dma_start(
                            rows_in, bass.IndirectOffsetOnAxis(ap=slot_i[:, c, t:t + 1], axis=0),
                            h_all[:, t, :], None).then_inc(scattered_first if t < GT else scattered, 16)
                for i in range(2):
                    pool.wait_ge(y_stored[i], 16 * ((BLOCKS + 1 - i) // 2))
                pool.wait_ge(scattered, 16 * TOPK * (NTILE - GT))
                for t in range(NTILE):
                    if t >= GOT:
                        pool.wait_ge(mixed, t - GOT + 1)
                    for c in range(TOPK):
                        nc.gpsimd.indirect_dma_start(
                            h_all[:, GT + TOPK * (t % GOT) + c, :], None, rows_out,
                            bass.IndirectOffsetOnAxis(ap=slot_i[:, c, t:t + 1], axis=0)).then_inc(got[c][t % GOT], 16)

            @block.scalar
            def _(act):
                def turn_h(t):
                    act.wait_ge(h_turned, t + 1)
                    dst = ht_of(t // GT)[:, :, t % GT * P:(t % GT + 1) * P]
                    nc.scalar.activation(dst, tr_ps[:, t % 2, :].rearrange("p (a t) -> p a t", a=DT),
                                         ACT.Copy).then_inc(ht_ready, 1)

                def silu(j):
                    act.wait_ge(shgu_ready, j + 1)
                    if j >= 2:
                        act.wait_ge(shact_ready, j - 1)
                    nc.scalar.activation(silu_g[:, j % 2, :], big_ps[:, 2 * (j % 2), :], ACT.Silu).then_inc(shsilu_done, 1)

                for t in range(NTILE):
                    turn_h(t)
                    if t == GT - 1:
                        silu(0)
                    if t in (GT, GT + 1):
                        std(act, EARLY, NTILE, 4 + t - GT)
                act.wait_ge(gap_ready, 1)
                nc.scalar.activation(small[:, 3, :], small[:, 2, :], ACT.Exp).then_inc(egap_ready, 1)
                for j in range(1, FT * (GROUPS - 1)):
                    silu(j)
                for e in range(PER * 2, PER * 3):
                    act.dma_start(w_dn[:, e, :, :], w_down[e].rearrange("(a p) d -> p a d", p=P)).then_inc(wdn_loaded, 16)

                def turn_in(k0, it):
                    act.wait_ge(in_turned, k0 + 1 + 2 * it)
                    if inner(k0, 2, it):
                        act.wait_ge(gu_ready, k0 - 1 + 2 * it)
                    nc.scalar.activation(h_t[:, k0 % 2, :, :], tr_ps[:, k0 % 2, :].rearrange("p (a t) -> p a t", a=DT),
                                         ACT.Copy).then_inc(inT_ready, 1)

                def y_copy(k0, it):
                    act.wait_ge(dn_ready, k0 + 1 + 2 * it)
                    if inner(k0, 2, it):
                        act.wait_ge(y_stored[k0 % 2], 16 * (k0 // 2) + 16 * it)
                    nc.scalar.activation(y_sb[k0 % 2][:, :], y_ps[:, k0 % 2, :], ACT.Copy).then_inc(y_copied, 1)
                    act.wait_ge(y_copied, k0 + 1 + 2 * it)
                    act.dma_start(blocks_out[k0 + 2 * it], y_sb[k0 % 2][:, :]).then_inc(y_stored[k0 % 2], 16)

                turn_in(0, 0)

                def step(k0, it):
                    act.wait_ge(gu_ready, k0 + 1 + 2 * it)
                    if k0 >= 1:
                        act.wait_ge(act_ready, k0 + 2 * it)
                    else:
                        act.wait_ge(shact_ready, FT * (GROUPS - 1))
                    nc.scalar.activation(silu_g[:, 0, 0:F], gu_ps[:, 0:F], ACT.Silu).then_inc(silu_done, 1)
                    if k0 + 1 < BLOCKS:
                        turn_in(k0 + 1, it)
                    if k0 >= 1:
                        y_copy(k0 - 1, it)

                pairs(act, step, BLOCKS)
                y_copy(BLOCKS - 1, 0)
                act.wait_ge(act_ready, BLOCKS)
                for j in range(FT * (GROUPS - 1), FT * GROUPS):
                    silu(j)

            @block.tensor
            def _(pe):
                def logits(t):
                    pe.wait_ge(ht_ready, t + 1)
                    for a in range(DT):
                        mm = nc.tensor.matmul(lg_ps[:, t, :], ht_of(t // GT)[:, a, t % GT * P:(t % GT + 1) * P], w_rt[:, a, :],
                                              start=(a == 0), stop=(a == DT - 1))
                    mm.then_inc(lg_ready, 1)

                def turn_h(t):
                    pe.wait_ge(h_ready, t + 1)
                    if t == OUT_AFTER + 1:
                        pe.wait_ge(x1_ready, X1_START + NTILE)
                    elif t >= 2:
                        pe.wait_ge(ht_ready, t - 1)
                    for a in range(DT):
                        mm = nc.tensor.transpose(tr_ps[:, t % 2, a * P:(a + 1) * P], h_all[:, t, a * P:(a + 1) * P],
                                                 ident[:, :])
                    mm.then_inc(h_turned, 1)

                def shared_gates(j, which=(0, 1)):
                    g, c = j // FT, j % FT
                    pe.wait_ge(ht_ready, GT * (g + 1))
                    if j >= 2:
                        pe.wait_ge(shact_ready, j - 1)
                    for i in which:
                        for a in range(DT):
                            mm = nc.tensor.matmul(big_ps[:, 2 * (j % 2) + i, :], sh_gu[:, a, i * F + c * P:i * F + (c + 1) * P],
                                                  ht_of(g)[:, a, :],
                                                  start=(a == 0), stop=(a == DT - 1))
                    if 1 in which:
                        mm.then_inc(shgu_ready, 1)

                def shared_down(t):
                    g = t // GT
                    pe.wait_ge(shact_ready, FT * (g + 1))
                    if t < 2:
                        pe.wait_ge(ht_ready, NTILE - 1 + t)
                    elif t == 2 * GT:
                        pe.wait_ge(inT_ready, BLOCKS)
                    else:
                        pe.wait_ge(shared_added, t - 1)
                    for c in range(FT):
                        mm = nc.tensor.matmul(tr_ps[:, t % 2, :], sh_act[:, g % 2, c, t % GT * P:(t % GT + 1) * P],
                                              sh_dn[:, c, :], start=(c == 0), stop=(c == FT - 1))
                    mm.then_inc(shdn_ready, 1)

                def out_last(o):
                    pe.wait_ge(ht_ready, OUT_AFTER + 1)
                    for kt in range(CT):
                        project_out(pe, HALVES, o, kt, tr_ps[:, o, :], 0)

                pe.wait_ge(shared_loaded, 16 * 5)
                for t in range(NTILE):
                    turn_h(t)
                    if t >= 1:
                        logits(t - 1)
                    if t == GT - 1:
                        shared_gates(0)
                    if t == OUT_AFTER:
                        for o in range(CT):
                            out_last(o)
                    if t == 2 * GT - 1:
                        shared_gates(1, (0,))
                logits(NTILE - 1)
                shared_gates(1, (1,))
                pe.wait_ge(chosen_ready, 1)
                pe.wait_ge(const_ready, 3)
                nc.tensor.matmul(cnt_ps[:, 0, :, :], before[:, :], chosen[:, :, :], start=True, stop=True)
                nc.tensor.matmul(cnt_ps[:, 1, :, :], ones_bf[:, :], chosen[:, :, :], start=True, stop=True,
                                 ).then_inc(cnt_ready, 1)
                shared_gates(2)
                shared_gates(3)
                for t in range(2 * GT):
                    shared_down(t)
                shared_gates(4)
                shared_gates(5)

                def turn_in(k0, it):
                    pe.wait_ge(in_loaded[k0 % 2], 16 * (k0 // 2 + 1) + 16 * it)
                    if inner(k0, 2, it):
                        pe.wait_ge(inT_ready, k0 - 1 + 2 * it)
                    else:
                        pe.wait_ge(shared_added, 2 * GT - 1 + k0)
                    for a in range(DT):
                        mm = nc.tensor.transpose(tr_ps[:, k0 % 2, a * P:(a + 1) * P], h_in[:, k0 % 2, a * P:(a + 1) * P],
                                                 ident[:, :])
                    mm.then_inc(in_turned, 1)

                def down(k0, expert, it):
                    pe.wait_ge(actT_ready, k0 + 1 + 2 * it)
                    if inner(k0, 2, it):
                        pe.wait_ge(y_copied, k0 - 1 + 2 * it)
                    for a in range(FT):
                        mm = nc.tensor.matmul(y_ps[:, k0 % 2, :], act_t[:, a, :], w_dn[:, bass.ds(expert, 1), a, :],
                                              start=(a == 0), stop=(a == FT - 1))
                    mm.then_inc(dn_ready, 1)

                def turn_act(k0, it):
                    pe.wait_ge(act_ready, k0 + 1 + 2 * it)
                    if k0 >= 1:
                        pe.wait_ge(actT_ready, k0 + 2 * it)
                    for a in range(FT):
                        mm = nc.tensor.transpose(at_ps[:, a, :], act_gu[:, a * P:(a + 1) * P], ident[:, :])
                    mm.then_inc(act_turned, 1)

                expert_reg = [pe.alloc_register(f"expert_reg{i}") for i in range(2)]

                def load_expert(k0, it):
                    pe.reg_load(expert_reg[k0 % 2], blk_i[0:1, bass.ds(k0 + 2 * it, 1)])

                def expert_of(k0):
                    return pe.snap(expert_reg[k0 % 2], min_val=0, max_val=E - 1)

                pe.wait_ge(blocks_ready, 1)
                pe.wait_ge(shact_ready, FT * (GROUPS - 1))
                load_expert(0, 0)
                turn_in(0, 0)
                pe.wait_ge(wgu_loaded, 16 * 2 * E)
                pe.wait_ge(wdn_loaded, 16 * E)

                def step(k0, it):
                    expert = expert_of(k0)
                    if k0 >= 1:
                        turn_act(k0 - 1, it)
                    pe.wait_ge(inT_ready, k0 + 1 + 2 * it)
                    for a in range(DT):
                        mm = nc.tensor.matmul(gu_ps[:, :], h_t[:, k0 % 2, a, :], w_gu[:, bass.ds(expert, 1), a, :],
                                              start=(a == 0), stop=(a == DT - 1))
                    mm.then_inc(gu_ready, 1)
                    if k0 + 1 < BLOCKS:
                        turn_in(k0 + 1, it)
                    if k0 >= 1:
                        down(k0 - 1, expert_of(k0 - 1), it)
                    if k0 + 1 < BLOCKS:
                        load_expert(k0 + 1, it)

                pairs(pe, step, BLOCKS)
                turn_act(BLOCKS - 1, 0)
                down(BLOCKS - 1, expert_of(BLOCKS - 1), 0)
                for t in range(2 * GT, 3 * GT):
                    shared_down(t)
                pe.wait_ge(act_ready, BLOCKS)
                pe.wait_ge(actT_ready, BLOCKS)
                shared_gates(6)
                pe.wait_ge(y_copied, BLOCKS)
                shared_gates(7)
                for t in range(3 * GT, NTILE):
                    shared_down(t)

            @block.vector
            def _(dve):
                V = nc.vector

                def make_h(t):
                    V.scalar_tensor_tensor(out=h_all[:, t, :], in0=x_sb[:, t, :], scalar=mv[:, t, 0:1], in1=rms_bc[:, :],
                                           op0=ALU.subtract, op1=ALU.mult).then_inc(h_part, 1)
                    dve.wait_ge(h_part, t + 1)
                    V.tensor_scalar(h_all[:, t, :], h_all[:, t, :], rstd[:, t:t + 1], None, ALU.mult).then_inc(h_ready, 1)

                def shared_act(j):
                    g, c = j // FT, j % FT
                    dve.wait_ge(shsilu_done, j + 1)
                    if g >= 2:
                        dve.wait_ge(shdn_ready, GT * (g - 1))
                    V.tensor_tensor(sh_act[:, g % 2, c, :], silu_g[:, j % 2, :], big_ps[:, 2 * (j % 2) + 1, :],
                                    ALU.mult).then_inc(shact_ready, 1)

                def shared_add(t):
                    dve.wait_ge(shdn_ready, t + 1)
                    V.tensor_tensor(x_sb[:, t, :], x_sb[:, t, :], tr_ps[:, t % 2, :], ALU.add).then_inc(shared_added, 1)

                dve.wait_ge(shared_loaded, 16 * 5)
                for t in range(8):
                    make_h(t)
                invert(dve, HALVES - 1, 0)
                for t in range(8, EARLY):
                    make_h(t)
                divide(dve, HALVES - 1, 0)
                dve.wait_ge(num_written, 16 * GH * HALVES)
                shared_act(0)
                dve.wait_ge(const_ready, 3)
                chained(dve, V.tensor_copy(iota[:, :], iota_i[:, :]))
                chained(dve, V.tensor_scalar(rank[:, :], iota[:, 0:E], -1.0, float(E), ALU.mult, ALU.add))
                for o in range(CT):
                    residual(dve, HALVES, o, tr_ps[:, o, :], 0)
                    dve.wait_ge(x1_ready, X1_START + LAST + o + 1)
                    chained(dve, V.bn_stats(stats[:, LAST + o, :], x_sb[:, LAST + o, :]))
                dve.wait_ge(stats_ready, LAST)
                row_scale(dve, EARLY, NTILE, 4)
                for t in range(EARLY, NTILE):
                    make_h(t)

                def by_expert(ap):
                    return ap.rearrange("p (t o) -> p t o", o=1).broadcast_to([P, NTILE, E])

                def by_tile(ap):
                    return ap.rearrange("p (o e) -> p o e", o=1).broadcast_to([P, NTILE, E])

                def pick(dst, logit, top):
                    chained(dve, V.tensor_reduce(top, logit, AX_X, ALU.max))
                    chained(dve, V.tensor_tensor(dst, logit, by_expert(top), ALU.is_equal))
                    chained(dve, V.tensor_tensor(dst, dst, by_tile(rank[:, :]), ALU.mult))
                    chained(dve, V.tensor_reduce(small[:, 4, :], dst, AX_X, ALU.max))
                    chained(dve, V.tensor_tensor(dst, dst, by_expert(small[:, 4, :]), ALU.is_equal))

                LG, M1, M2, LG2, TOT, PA, PB, POS = (rt[:, i, :, :] for i in range(8))
                dve.wait_ge(lg_ready, NTILE)
                chained(dve, V.tensor_copy(LG, lg_ps[:, :, :]))
                pick(M1, LG, small[:, 0, :])
                chained(dve, V.scalar_tensor_tensor(out=LG2, in0=M1, scalar=-3.0e38, in1=LG, op0=ALU.mult, op1=ALU.add))
                pick(M2, LG2, small[:, 1, :])
                V.tensor_tensor(chosen[:, :, :], M1, M2, ALU.add).then_inc(chosen_ready, 1)
                V.tensor_tensor(small[:, 2, :], small[:, 1, :], small[:, 0, :], ALU.subtract).then_inc(gap_ready, 1)
                dve.wait_ge(cnt_ready, 1)
                chained(dve, V.tensor_copy(TOT, cnt_ps[:, 1, :, :]))
                src, dst = TOT, PA
                for s in (1, 2, 4, 8):
                    V.tensor_copy(dst[:, 0:s, :], src[:, 0:s, :])
                    chained(dve, V.tensor_tensor(dst[:, s:NTILE, :], src[:, s:NTILE, :], src[:, 0:NTILE - s, :], ALU.add))
                    src, dst = dst, (PB if dst is PA else PA)
                run = src
                total = run[:, NTILE - 1, :]
                chained(dve, V.tensor_scalar(blk_e[:, 0:NTILE], iota[:, 0:NTILE], float(P), None, ALU.mult))
                chained(dve, V.tensor_tensor(blk[:, 0:NTILE, :],
                                             total.rearrange("p (o e) -> p o e", o=1).broadcast_to([P, NTILE, E]),
                                             blk_e[:, 0:NTILE].rearrange("p (t o) -> p t o", o=1).broadcast_to([P, NTILE, E]),
                                             ALU.is_gt))
                nb, na, spare = blk[:, 45, :], blk[:, 46, :], blk[:, 47, :]
                chained(dve, V.tensor_reduce(nb, blk[:, 0:NTILE, :].rearrange("p t e -> p e t"), AX_X, ALU.add))
                src, dst = nb, na
                for s in (1, 2, 4):
                    V.tensor_copy(dst[:, 0:s], src[:, 0:s])
                    chained(dve, V.tensor_tensor(dst[:, s:E], src[:, s:E], src[:, 0:E - s], ALU.add))
                    src, dst = dst, (spare if dst is na else na)
                ends, first = src, dst
                chained(dve, V.tensor_tensor(first, ends, nb, ALU.subtract))
                chained(dve, V.tensor_scalar(first, first, float(P), None, ALU.mult))
                chained(dve, V.tensor_tensor(POS, run, TOT, ALU.subtract))
                chained(dve, V.tensor_tensor(POS, POS, by_tile(first), ALU.add))
                chained(dve, V.tensor_tensor(POS, POS, cnt_ps[:, 0, :, :], ALU.add))
                for c, m in enumerate((M1, M2)):
                    chained(dve, V.tensor_tensor(LG, m, POS, ALU.mult))
                    chained(dve, V.tensor_reduce(small[:, 8 + c, :], LG, AX_X, ALU.add))
                V.tensor_copy(slot_i[:, :, :], small[:, 8:10, :]).then_inc(slots_ready, 1)
                shared_act(1)
                shared_act(2)
                dve.wait_ge(egap_ready, 1)
                chained(dve, V.tensor_scalar(small[:, 4, :], small[:, 3, :], 1.0, None, ALU.add))
                chained(dve, V.reciprocal(small[:, 6, :], small[:, 4, :]))
                chained(dve, V.tensor_tensor(small[:, 7, :], small[:, 3, :], small[:, 6, :], ALU.mult))
                chained(dve, V.tensor_tensor(blk[:, 0:BLOCKS, 0:E - 1],
                                             iota[:, 0:BLOCKS].rearrange("p (t o) -> p t o", o=1).broadcast_to([P, BLOCKS, E - 1]),
                                             ends[:, 0:E - 1].rearrange("p (o e) -> p o e", o=1).broadcast_to([P, BLOCKS, E - 1]),
                                             ALU.is_ge))
                chained(dve, V.tensor_reduce(blk_e[:, 0:BLOCKS], blk[:, 0:BLOCKS, 0:E - 1], AX_X, ALU.add))
                V.tensor_copy(blk_i[:, 0:BLOCKS], blk_e[:, 0:BLOCKS]).then_inc(blocks_ready, 1)
                shared_act(3)
                for t in range(2 * GT):
                    shared_add(t)
                shared_act(4)
                shared_act(5)

                def turn_copy(k0, it):
                    dve.wait_ge(act_turned, k0 + 1 + 2 * it)
                    if k0 >= 1:
                        dve.wait_ge(dn_ready, k0 + 2 * it)
                    V.tensor_copy(act_t[:, :, :], at_ps[:, :, :]).then_inc(actT_ready, 1)

                def step(k0, it):
                    if k0 >= 1:
                        turn_copy(k0 - 1, it)
                    dve.wait_ge(silu_done, k0 + 1 + 2 * it)
                    if k0 >= 1:
                        dve.wait_ge(act_turned, k0 + 2 * it)
                    V.tensor_tensor(act_gu[:, :], silu_g[:, 0, 0:F], gu_ps[:, F:2 * F], ALU.mult).then_inc(act_ready, 1)

                pairs(dve, step, BLOCKS)
                turn_copy(BLOCKS - 1, 0)

                def mix(t):
                    dve.wait_ge(shared_added, t + 1)
                    for c in range(TOPK):
                        dve.wait_ge(got[c][t % GOT], 16 * (t // GOT + 1))
                        done = V.scalar_tensor_tensor(out=x_sb[:, t, :], in0=h_all[:, GT + TOPK * (t % GOT) + c, :],
                                                      scalar=small[:, 6 + c, t:t + 1], in1=x_sb[:, t, :],
                                                      op0=ALU.mult, op1=ALU.add)
                        if c == 0:
                            chained(dve, done)
                        else:
                            done.then_inc(mixed, 1)

                for t in range(2 * GT, 3 * GT):
                    shared_add(t)
                for t in range(3):
                    mix(t)
                shared_act(6)
                for t in range(3, 6):
                    mix(t)
                shared_act(7)
                for i in range(GT):
                    mix(6 + i)
                    shared_add(3 * GT + i)
                for t in range(6 + GT, NTILE):
                    mix(t)

        token_ctx.close()


_INS = [n for n in (
    'x', 'ctx_2048', 'L0_xattn_Wq', 'L0_xattn_bq', 'L0_xattn_Wk', 'L0_xattn_bk', 'L0_xattn_Wv', 'L0_xattn_bv',
    'L0_xattn_Wo', 'L0_xattn_bo', 'L0_ffn_rms_weight', 'L0_ffn_router_w', 'L0_ffn_w_gate', 'L0_ffn_w_up',
    'L0_ffn_w_down', 'L0_ffn_sw_gate', 'L0_ffn_sw_up', 'L0_ffn_sw_down')]


def kernel(**inputs):
    import numpy as np
    import concourse.bacc as bacc
    from concourse.bass_utils import run_bass_kernel_spmd

    nc = bacc.Bacc("TRN2", target_bir_lowering=False, num_devices=1)
    arrays, args = {}, []
    for name in _INS:
        a = np.ascontiguousarray(inputs[name])
        arrays[f"in_{name}"] = a
        args.append(nc.dram_tensor(f"in_{name}", a.shape, mybir.dt.from_np(a.dtype), kind="ExternalInput").ap())
    args.append(nc.dram_tensor("out_0", (B, C, T), F32, kind="ExternalOutput").ap())
    xattn_ffn_kernel(nc, *args)
    r = run_bass_kernel_spmd(nc, [arrays], core_ids=[0])
    return r.results[0]["out_0"]
```
